# Optimizing a Trainium2 kernel written in Bass

```python
import numpy as np
import jax
import jax.numpy as jnp

def _softmax(x, axis=-1):
    return jax.nn.softmax(x, axis=axis)

def _gelu(x):
    return jax.nn.gelu(x, approximate=True)

def _silu(x):
    return jax.nn.silu(x)

def _sigmoid(x):
    return jax.nn.sigmoid(x)

def _layernorm(x, axis=-1, eps=1e-05):
    m = jnp.mean(x, axis=axis, keepdims=True)
    v = jnp.var(x, axis=axis, keepdims=True)
    return (x - m) / jnp.sqrt(v + eps)

def _scatter_add(tgt, idx, src, axis=0):
    return tgt.at[idx].add(src)

def _segment_sum(src, seg, n):
    return jax.ops.segment_sum(src, seg, n)
kernel_name = 'mk_lm_tower_d2_tok_ids768_r4_0ce7c9'

def setup_inputs(seed: int=0):
    np.random.seed(seed)
    _w = jnp.asarray

    def _rec_inputs():
        import jax
        import jax.numpy as jnp
        _rk = jax.random.key(seed)
        x = jax.random.randint(jax.random.fold_in(_rk, 1), (4, 1024), 0, 12564, jnp.int32)
        return x
    x = _rec_inputs()

    def _L0_tok_setup():
        import jax, jax.numpy as jnp
        import numpy as np
        VOCAB = 50257
        EMBED_DIM = 192
        key = jax.random.key(seed)
        k1, k2 = jax.random.split(key)
        x = jax.random.randint(k1, (8, 512), 0, VOCAB, dtype=jnp.int64 if jax.config.jax_enable_x64 else jnp.int32)
        weight = jax.random.normal(k2, (EMBED_DIM, VOCAB), dtype=jnp.float32)
        return {'x': x, 'weight': weight}
    _L0_tok_all = _L0_tok_setup()
    _L0_tok_in = {k: v for k, v in _L0_tok_all.items() if k in ('weight',)}
    del _L0_tok_all

    def _L0_attn_setup():
        import jax, jax.numpy as jnp
        import numpy as np
        FEATS = 192
        HEAD = 12
        HD = FEATS // HEAD
        B, N = (128, 197)
        key = jax.random.key(seed)
        k0, k1, k2 = jax.random.split(key, 3)
        x = jax.random.normal(k0, (B, N, FEATS), dtype=jnp.float32)
        W_qkv = jax.random.normal(k1, (HEAD, HD, 3 * HD), dtype=jnp.float32) * 0.05
        b_qkv = jnp.zeros((HEAD, 3 * HD), dtype=jnp.float32)
        W_out = jax.random.normal(k2, (FEATS, FEATS), dtype=jnp.float32) * 0.02
        b_out = jnp.zeros((FEATS,), dtype=jnp.float32)
        return {'x': x, 'W_qkv': W_qkv, 'b_qkv': b_qkv, 'W_out': W_out, 'b_out': b_out}
    _L0_attn_all = _L0_attn_setup()
    _L0_attn_in = {k: v for k, v in _L0_attn_all.items() if k in ('W_qkv', 'b_qkv', 'W_out', 'b_out')}
    del _L0_attn_all

    def _L0_ffn_setup():
        import jax, jax.numpy as jnp
        import numpy as np
        S, B, DIM = (256, 4, 192)
        N_EXPERTS = 8
        HID = 512
        key = jax.random.key(seed)
        ks = jax.random.split(key, 6)
        scale = 0.02
        return {'hidden_states': jax.random.normal(ks[0], (S, B, DIM), dtype=jnp.float32), 'router_w': jax.random.normal(ks[1], (DIM, N_EXPERTS), dtype=jnp.float32) * scale, 'router_b': jnp.zeros((N_EXPERTS,), dtype=jnp.float32), 'w1': jax.random.normal(ks[2], (N_EXPERTS, DIM, HID), dtype=jnp.float32) * scale, 'w2': jax.random.normal(ks[3], (N_EXPERTS, DIM, HID), dtype=jnp.float32) * scale, 'w3': jax.random.normal(ks[4], (N_EXPERTS, HID, DIM), dtype=jnp.float32) * scale}
    _L0_ffn_all = _L0_ffn_setup()
    _L0_ffn_in = {k: v for k, v in _L0_ffn_all.items() if k in ('router_w', 'router_b', 'w1', 'w2', 'w3')}
    del _L0_ffn_all

    def _L1_attn_setup():
        import jax, jax.numpy as jnp
        import numpy as np
        NUM_HEADS = 12
        KERNEL_EPS = 0.001

        def _performer_relu_attention(q, k, v, projection):
            d = q.shape[-1]
            data_normalizer = 1.0 / jnp.sqrt(jnp.sqrt(jnp.asarray(d, q.dtype)))
            qp = jax.nn.relu(jnp.einsum('bhnd,md->bhnm', q * data_normalizer, projection)) + KERNEL_EPS
            kp = jax.nn.relu(jnp.einsum('bhnd,md->bhnm', k * data_normalizer, projection)) + KERNEL_EPS
            k_sum = kp.sum(axis=2)
            d_inv = 1.0 / jnp.einsum('bhnm,bhm->bhn', qp, k_sum)
            context = jnp.einsum('bhnm,bhnd->bhmd', kp, v)
            out = jnp.einsum('bhnm,bhmd->bhnd', qp, context) * d_inv[..., None]
            return out
        key = jax.random.key(seed)
        ks = jax.random.split(key, 6)
        B, N, C = (4, 1024, 192)
        H = NUM_HEADS
        d = C // H
        m = 64
        x = jax.random.normal(ks[0], (B, N, C), dtype=jnp.float32)
        w_qkv = jax.random.normal(ks[1], (3 * C, C), dtype=jnp.float32) * 0.02
        b_qkv = jnp.zeros((3 * C,), dtype=jnp.float32)
        w_proj = jax.random.normal(ks[2], (C, C), dtype=jnp.float32) * 0.02
        b_proj = jnp.zeros((C,), dtype=jnp.float32)
        projection = jax.random.normal(ks[3], (m, d), dtype=jnp.float32)
        return {'x': x, 'w_qkv': w_qkv, 'b_qkv': b_qkv, 'w_proj': w_proj, 'b_proj': b_proj, 'projection': projection}
    _L1_attn_all = _L1_attn_setup()
    _L1_attn_in = {k: v for k, v in _L1_attn_all.items() if k in ('w_qkv', 'b_qkv', 'w_proj', 'b_proj', 'projection')}
    del _L1_attn_all

    def _L1_ffn_setup():
        import jax, jax.numpy as jnp
        import numpy as np
        B, S, D = (2, 512, 192)
        E, K, F = (8, 2, 384)

        def _swiglu(xf, wg, wu, wd):
            return jax.nn.silu(xf @ wg.T) * (xf @ wu.T) @ wd.T
        key = jax.random.key(seed)
        ks = jax.random.split(key, 9)
        scale = 0.02
        x = jax.random.normal(ks[0], (B, S, D), dtype=jnp.float32)
        w_router = jax.random.normal(ks[1], (E, D), dtype=jnp.float32) * scale
        expert_bias = jnp.zeros((E,), dtype=jnp.float32)
        Wg = jax.random.normal(ks[2], (E, F, D), dtype=jnp.float32) * scale
        Wu = jax.random.normal(ks[3], (E, F, D), dtype=jnp.float32) * scale
        Wd = jax.random.normal(ks[4], (E, D, F), dtype=jnp.float32) * scale
        sg = jax.random.normal(ks[5], (F, D), dtype=jnp.float32) * scale
        su = jax.random.normal(ks[6], (F, D), dtype=jnp.float32) * scale
        sd = jax.random.normal(ks[7], (D, F), dtype=jnp.float32) * scale
        return {'x': x, 'w_router': w_router, 'expert_bias': expert_bias, 'Wg': Wg, 'Wu': Wu, 'Wd': Wd, 'sg': sg, 'su': su, 'sd': sd}
    _L1_ffn_all = _L1_ffn_setup()
    _L1_ffn_in = {k: v for k, v in _L1_ffn_all.items() if k in ('w_router', 'expert_bias', 'Wg', 'Wu', 'Wd', 'sg', 'su', 'sd')}
    del _L1_ffn_all
    return {'x': x, 'L0_tok_weight': _L0_tok_in['weight'], 'L0_attn_W_qkv': _L0_attn_in['W_qkv'], 'L0_attn_b_qkv': _L0_attn_in['b_qkv'], 'L0_attn_W_out': _L0_attn_in['W_out'], 'L0_attn_b_out': _L0_attn_in['b_out'], 'L0_ffn_router_w': _L0_ffn_in['router_w'], 'L0_ffn_router_b': _L0_ffn_in['router_b'], 'L0_ffn_w1': _L0_ffn_in['w1'], 'L0_ffn_w2': _L0_ffn_in['w2'], 'L0_ffn_w3': _L0_ffn_in['w3'], 'L1_attn_w_qkv': _L1_attn_in['w_qkv'], 'L1_attn_b_qkv': _L1_attn_in['b_qkv'], 'L1_attn_w_proj': _L1_attn_in['w_proj'], 'L1_attn_b_proj': _L1_attn_in['b_proj'], 'L1_attn_projection': _L1_attn_in['projection'], 'L1_ffn_w_router': _L1_ffn_in['w_router'], 'L1_ffn_expert_bias': _L1_ffn_in['expert_bias'], 'L1_ffn_Wg': _L1_ffn_in['Wg'], 'L1_ffn_Wu': _L1_ffn_in['Wu'], 'L1_ffn_Wd': _L1_ffn_in['Wd'], 'L1_ffn_sg': _L1_ffn_in['sg'], 'L1_ffn_su': _L1_ffn_in['su'], 'L1_ffn_sd': _L1_ffn_in['sd']}

def reference(x, L0_tok_weight, L0_attn_W_qkv, L0_attn_b_qkv, L0_attn_W_out, L0_attn_b_out, L0_ffn_router_w, L0_ffn_router_b, L0_ffn_w1, L0_ffn_w2, L0_ffn_w3, L1_attn_w_qkv, L1_attn_b_qkv, L1_attn_w_proj, L1_attn_b_proj, L1_attn_projection, L1_ffn_w_router, L1_ffn_expert_bias, L1_ffn_Wg, L1_ffn_Wu, L1_ffn_Wd, L1_ffn_sg, L1_ffn_su, L1_ffn_sd):
    import jax
    import jax.numpy as jnp

    def _L0_tok_ref(x, weight):
        import jax, jax.numpy as jnp
        import numpy as np
        VOCAB = 50257
        EMBED_DIM = 192
        return jnp.take(weight.T, x, axis=0)

    def _L0_attn_ref(x, W_qkv, b_qkv, W_out, b_out):
        import jax, jax.numpy as jnp
        import numpy as np
        FEATS = 192
        HEAD = 12
        HD = FEATS // HEAD
        B, N = (128, 197)
        b, n, f = x.shape
        h, hd = (W_qkv.shape[0], W_qkv.shape[1])
        xh = x.reshape(b, n, h, hd)
        qkv = jnp.einsum('bnhd,hde->bnhe', xh, W_qkv) + b_qkv
        q, k, v = jnp.split(qkv, 3, axis=-1)
        scale = jnp.asarray(f, x.dtype) ** 0.5
        scores = jnp.einsum('bihd,bjhd->bhij', q, k) / scale
        p = jax.nn.softmax(scores, axis=-1)
        attn = jnp.einsum('bhij,bjhd->bihd', p, v)
        out = attn.reshape(b, n, f) @ W_out + b_out
        return out

    def _L0_ffn_ref(hidden_states, router_w, router_b, w1, w2, w3):
        import jax, jax.numpy as jnp
        import numpy as np
        S, B, DIM = (256, 4, 192)
        N_EXPERTS = 8
        HID = 512
        s, b, h = hidden_states.shape
        route = jax.nn.softmax(hidden_states @ router_w + router_b, axis=2)
        max_prob = jnp.max(route, axis=2).reshape(-1, 1)
        max_ind = jnp.argmax(route, axis=2).reshape(-1)
        x = hidden_states.reshape(-1, h)
        out = jnp.zeros_like(x)
        for e in range(N_EXPERTS):
            mask = (max_ind == e)[:, None]
            xe = jnp.where(mask, x, 0.0)
            oe = jax.nn.silu(xe @ w1[e]) * (xe @ w2[e]) @ w3[e]
            out = out + jnp.where(mask, oe, 0.0)
        out = out.astype(jnp.bfloat16) * max_prob
        return out.reshape(s, b, h)

    def _L1_attn_ref(x, w_qkv, b_qkv, w_proj, b_proj, projection):
        import jax, jax.numpy as jnp
        import numpy as np
        NUM_HEADS = 12
        KERNEL_EPS = 0.001

        def _performer_relu_attention(q, k, v, projection):
            d = q.shape[-1]
            data_normalizer = 1.0 / jnp.sqrt(jnp.sqrt(jnp.asarray(d, q.dtype)))
            qp = jax.nn.relu(jnp.einsum('bhnd,md->bhnm', q * data_normalizer, projection)) + KERNEL_EPS
            kp = jax.nn.relu(jnp.einsum('bhnd,md->bhnm', k * data_normalizer, projection)) + KERNEL_EPS
            k_sum = kp.sum(axis=2)
            d_inv = 1.0 / jnp.einsum('bhnm,bhm->bhn', qp, k_sum)
            context = jnp.einsum('bhnm,bhnd->bhmd', kp, v)
            out = jnp.einsum('bhnm,bhmd->bhnd', qp, context) * d_inv[..., None]
            return out
        B, N, C = x.shape
        H = NUM_HEADS
        d = C // H
        qkv = x @ w_qkv.T + b_qkv
        qkv = qkv.reshape(B, N, 3, H, d).transpose(0, 3, 2, 1, 4)
        q, k, v = (qkv[:, :, 0], qkv[:, :, 1], qkv[:, :, 2])
        out = _performer_relu_attention(q, k, v, projection)
        out = out.transpose(0, 2, 1, 3).reshape(B, N, C)
        return out @ w_proj.T + b_proj

    def _L1_ffn_ref(x, w_router, expert_bias, Wg, Wu, Wd, sg, su, sd):
        import jax, jax.numpy as jnp
        import numpy as np
        B, S, D = (2, 512, 192)
        E, K, F = (8, 2, 384)

        def _swiglu(xf, wg, wu, wd):
            return jax.nn.silu(xf @ wg.T) * (xf @ wu.T) @ wd.T
        b, s, d = x.shape
        xf = x.reshape(-1, d)
        T = xf.shape[0]
        e = w_router.shape[0]
        logits = xf @ w_router.T
        scores = jax.nn.softmax(logits, axis=-1)
        selection = scores + expert_bias[None, :]
        _, top_idx = jax.lax.top_k(selection, K)
        top_s = jnp.take_along_axis(scores, top_idx, axis=-1)
        top_s = top_s / (jnp.sum(top_s, axis=-1, keepdims=True) + 1e-09)
        comb = jnp.zeros((T, e), dtype=x.dtype).at[jnp.arange(T)[:, None], top_idx].add(top_s)

        def body(acc, p):
            wg, wu, wd, c = p
            return (acc + c[:, None] * _swiglu(xf, wg, wu, wd), None)
        routed, _ = jax.lax.scan(body, jnp.zeros_like(xf), (Wg, Wu, Wd, comb.T))
        out = routed + _swiglu(xf, sg, su, sd)
        return out.reshape(b, s, d)
    h = _L0_tok_ref(x, L0_tok_weight)
    h = h + _L0_attn_ref(_layernorm(h, axis=-1), L0_attn_W_qkv, L0_attn_b_qkv, L0_attn_W_out, L0_attn_b_out)
    h = h + _L0_ffn_ref(_layernorm(h, axis=-1), L0_ffn_router_w, L0_ffn_router_b, L0_ffn_w1, L0_ffn_w2, L0_ffn_w3)
    h = h + _L1_attn_ref(_layernorm(h, axis=-1), L1_attn_w_qkv, L1_attn_b_qkv, L1_attn_w_proj, L1_attn_b_proj, L1_attn_projection)
    h = h + _L1_ffn_ref(_layernorm(h, axis=-1), L1_ffn_w_router, L1_ffn_expert_bias, L1_ffn_Wg, L1_ffn_Wu, L1_ffn_Wd, L1_ffn_sg, L1_ffn_su, L1_ffn_sd)
    return h

_drawn_inputs = setup_inputs


def setup_inputs(seed=0):
    import zlib

    import numpy as np

    out = dict(_drawn_inputs(seed))
    spreads = {'L0_attn_b_qkv': (0.0, 0.299),
     'L0_attn_b_out': (0.0, 0.1),
     'L0_ffn_router_b': (0.0, 0.8),
     'L1_attn_b_qkv': (0.0, 0.898),
     'L1_attn_b_proj': (0.0, 0.1),
     'L1_ffn_expert_bias': (0.0, 0.762)}
    factors = {'L0_attn_W_qkv': 8.0,
     'L0_ffn_router_w': 8.0,
     'L0_ffn_w1': 8.0,
     'L0_ffn_w2': 8.0,
     'L0_ffn_w3': 8.0,
     'L1_attn_w_qkv': 26.642,
     'L1_attn_projection': 135.483,
     'L1_ffn_w_router': 7.652,
     'L1_ffn_Wg': 5.167,
     'L1_ffn_Wu': 5.104,
     'L1_ffn_Wd': 5.112,
     'L1_ffn_sg': 3.736,
     'L1_ffn_su': 3.688,
     'L1_ffn_sd': 3.702}
    for name, (base, spread) in spreads.items():
        noise = np.random.default_rng([zlib.crc32(name.encode()), seed]).standard_normal(out[name].shape)
        drawn = base * np.exp(spread * noise) if base else spread * noise
        out[name] = jnp.asarray(drawn.astype(out[name].dtype))
    for name, factor in factors.items():
        out[name] = (out[name] * factor).astype(out[name].dtype)
    return out
```

```python
from contextlib import ExitStack, contextmanager

import numpy as np
import concourse.bass as bass
from concourse import mybir

F32 = mybir.dt.float32
BF16 = mybir.dt.bfloat16
I32 = mybir.dt.int32
U32 = mybir.dt.uint32
ALU = mybir.AluOpType
ACT = mybir.ActivationFunctionType
AX = mybir.AxisListType

P = 128
D = 192
DB = D - P
B, S = 4, 1024
T = B * S
NT = T // P
CT = 4
CHUNK = CT * P
TB = S // P
H, HD = 12, 16
GH = 4
NG = H // GH
GD = GH * HD
E = 8
EPS = 1e-5
SCALE0 = float(D) ** -0.5
PARTS = 3
Q_STACK = (0, 0, 1, 1, 0, 2)
K_STACK = (0, 1, 0, 1, 2, 0)
SK = len(Q_STACK) * HD
M_FEAT = 64
KERNEL_EPS = 0.001
F0, F1 = 512, 384


@contextmanager
def semaphores(nc):
    taken = []

    def new_sem(name):
        taken.append(nc.alloc_semaphore(name))
        return taken[-1]
    yield new_sem
    nc.clear_and_free_semaphores(taken)
    nc.all_engine_barrier()


class Chain:

    def __init__(self, eng, sem, per_turn=0, turn=0):
        self.eng, self.sem, self.base, self.n, self.per_turn = eng, sem, turn * per_turn, 0, per_turn

    def __call__(self, ins):
        self.n += 1
        ins.then_inc(self.sem, 1)
        self.eng.wait_ge(self.sem, self.base + self.n)


def sems(new_sem, names):
    return {n: new_sem(n) for n in names.split()}


def layer_norm_stats(nc, dve, link, tiles, stats, mv, var_eps, var_ready):
    dve.nop(nofuse=True)
    for j, tile in enumerate(tiles):
        last = nc.vector.bn_stats(stats[:, j, :], tile)
    link(last)
    dve.nop(nofuse=True)
    for j in range(len(tiles)):
        last = nc.vector.bn_aggr(mv[:, j, :], stats[:, j, :])
    link(last)
    nc.vector.tensor_scalar(var_eps, mv[:, :, 1], EPS, None, ALU.add).then_inc(var_ready, 1)


def layer_norm_apply(nc, link, tiles, normed, mv, var_eps, std, tmp):
    link(nc.vector.reciprocal(tmp, std))
    link(nc.vector.tensor_tensor(tmp, tmp, var_eps, ALU.mult))
    link(nc.vector.tensor_tensor(tmp, tmp, std, ALU.add))
    link(nc.vector.tensor_scalar(tmp, tmp, 0.5, None, ALU.mult))
    link(nc.vector.reciprocal(tmp, tmp))
    for j, tile in enumerate(tiles):
        last = nc.vector.tensor_scalar(normed[:, j, :], tile, mv[:, j, 0:1], tmp[:, j:j + 1],
                                       ALU.subtract, ALU.mult)
    return last


def embed_and_project(nc, a, s):
    with ExitStack() as ctx:
        new_sem = ctx.enter_context(semaphores(nc))

        def sb(name, shape, dt=F32):
            return ctx.enter_context(nc.sbuf_tensor("ep_" + name, shape, dt))

        h, v_nat, ps = s.h, s.v_nat, s.psum
        ids = sb("ids", [P, NT], I32)
        w_a = sb("w_a", [P, 2, P])
        w_b = sb("w_b", [DB, P])
        wv_a = sb("wv_a", [P, D])
        wv_b = sb("wv_b", [DB + 1, D])
        bias = sb("bias", [P, 3])
        stats = sb("stats", [P, 2, CT, 6])
        mv = sb("mv", [P, 2, CT, 2])
        var_eps = sb("var_eps", [P, 2, CT])
        std = sb("std", [P, 2, CT])
        tmp = sb("tmp", [P, 2, CT])
        xn = sb("xn", [P, 2, CT, D])
        xt_a = sb("xt_a", [P, 2, CHUNK])
        xt_b = sb("xt_b", [DB + 1, 2, CHUNK])
        full = sb("full", [P, 2, 3, CHUNK])
        rest = sb("rest", [P, 2, 3, CHUNK])
        parts = sb("parts", [P, 2, 3, PARTS, CHUNK], BF16)
        m = sems(new_sem, "ep_ids ep_weights ep_ones ep_ident ep_xt_ps ep_xt_left ep_qk_ps "
                          "ep_qk_left ep_v_left ep_link ep_pool_link ep_rest")
        two = {n: [new_sem(f"ep_{n}{u}") for u in range(2)] for n in
               ("var", "std", "xn", "xt_act", "xt_dve", "v_ps", "high", "middle", "low", "sent")}
        gathered = [new_sem(f"ep_gathered{t}") for t in range(TB)]
        zeros = sb("zeros", [P, D])
        zeroed, zeros_stored = (new_sem("ep_" + n) for n in ("zeroed", "zeros_stored"))
        block = ctx.enter_context(nc.Block())
        PS_XA, PS_XB, PS_QK, PS_V = 0, 1, 2, 5

        @block.gpsimd
        def _(pool):
            nc.gpsimd.memset(s.ident[:], 0.0).then_inc(m["ep_pool_link"], 1)
            pool.wait_ge(m["ep_pool_link"], 1)
            nc.gpsimd.affine_select(out=s.ident[:], in_=s.ident[:], compare_op=ALU.not_equal, fill=1.0, base=0,
                                    pattern=[[-1, P]], channel_multiplier=1).then_inc(m["ep_ident"], 1)
            pool.wait_ge(m["ep_ids"], 16)
            for t in range(NT):
                if t >= TB:
                    pool.wait_ge(gathered[t % TB], 16 * (t // TB))
                pool.indirect_dma_start(out=h[:, t, :], out_offset=None, in_=a["table"],
                                        in_offset=bass.IndirectOffsetOnAxis(ap=ids[:, t:t + 1], axis=0)
                                        ).then_inc(gathered[t % TB], 16)
            with pool.Fori(0, B) as b:
                for u in range(2):
                    for r in range(3):
                        pool.wait_ge(two["middle"][u], 3 * b + r + 1)
                        nc.gpsimd.tensor_tensor(parts[:, u, r, 2, :], rest[:, u, r, :], parts[:, u, r, 1, :],
                                                ALU.subtract).then_inc(two["low"][u], 1)

        @block.sync
        def _(sp):
            sp.dma_start(ids[:], a["ids"]).then_inc(m["ep_ids"], 16)
            for dst, src in ((w_a[:], a["w0_qk_a"]), (w_b[:], a["w0_qk_b"]), (wv_a[:], a["w0_v"][0:P, :]),
                             (wv_b[:], a["w0_v"][P:D + 1, :]), (bias[:], a["b0_qk"])):
                sp.dma_start(dst, src).then_inc(m["ep_weights"], 16)
            sp.wait_ge(zeroed, 1)
            for x_rows, n in zip(s.x_rows, (blocks_of(1), blocks_of(2))):
                sp.dma_start(x_rows[0:n * P, :].rearrange("(n p) d -> p n d", p=P),
                             zeros[:].unsqueeze(1).to_broadcast([P, n, D])).then_inc(zeros_stored, 16)
            with sp.Fori(0, B) as b:
                for u in range(2):
                    sp.wait_ge(two["low"][u], 3 * (b + 1))
                    cols = slice(u * CHUNK, (u + 1) * CHUNK)
                    for r, (src, which, row) in enumerate(((slice(0, P), 0, 0), (slice(0, P), 1, 0),
                                                           (slice(0, DB), 0, P), (slice(DB, P), 1, P))):
                        n = src.stop - src.start
                        dst = s.qk_parts[which, :, bass.ds(b * D + row, n), cols]
                        sp.dma_start(dst.rearrange("c r t -> r c t"),
                                     parts[src, u, min(r, 2), :, :]).then_inc(two["sent"][u], 16)
            for u in range(2):
                sp.wait_ge(two["sent"][u], 4 * 16 * B)
            sp.wait_ge(zeros_stored, 32)

        @block.vector
        def _(dve):
            nc.vector.memset(zeros[:], 0.0).then_inc(zeroed, 1)
            nc.vector.memset(xt_b[DB:DB + 1, :, :], 1.0).then_inc(m["ep_ones"], 1)
            per_turn = 2 * 7
            with dve.Fori(0, B) as b:
                link = Chain(dve, m["ep_link"], per_turn, b)
                for u in range(2):
                    tiles = [h[:, b * TB + (u * CT + j), :] for j in range(CT)]
                    for j in range(CT):
                        dve.wait_ge(gathered[u * CT + j], 16 * (b + 1))
                    layer_norm_stats(nc, dve, link, tiles, stats[:, u], mv[:, u], var_eps[:, u], two["var"][u])
                    dve.wait_ge(two["std"][u], b + 1)
                    layer_norm_apply(nc, link, tiles, xn[:, u], mv[:, u], var_eps[:, u], std[:, u],
                                     tmp[:, u]).then_inc(two["xn"][u], 1)
                    dve.wait_ge(m["ep_xt_ps"], 2 * b + u + 1)
                    dve.wait_ge(two["v_ps"][u], 2 * b)
                    nc.vector.tensor_copy(xt_b[0:DB, u, :], ps[0:DB, PS_XB, :]).then_inc(two["xt_dve"][u], 1)
                    for half in range(2):
                        dve.wait_ge(two["v_ps"][u], 2 * b + half + 1)
                        nc.vector.tensor_copy(v_nat[:, bass.ds(b * TB + u * CT + 2 * half, 2), :],
                                              ps[:, PS_V + half, 0:2 * D].rearrange("p (t d) -> p t d", d=D)
                                              ).then_inc(m["ep_v_left"], 1)
                    for r in range(3):
                        dve.wait_ge(two["high"][u], 3 * b + r + 1)
                        dve.wait_ge(two["low"][u], 3 * b)
                        nc.vector.tensor_tensor(rest[:, u, r, :], full[:, u, r, :], parts[:, u, r, 0, :],
                                                ALU.subtract).then_inc(m["ep_rest"], 1)
                        dve.wait_ge(m["ep_rest"], 6 * b + 3 * u + r + 1)
                        nc.vector.tensor_copy(parts[:, u, r, 1, :], rest[:, u, r, :]).then_inc(two["middle"][u], 1)

        @block.scalar
        def _(act):
            act.wait_ge(m["ep_weights"], 80)
            with act.Fori(0, B) as b:
                for u in range(2):
                    act.wait_ge(two["var"][u], b + 1)
                    nc.scalar.activation(std[:, u], var_eps[:, u], ACT.Sqrt).then_inc(two["std"][u], 1)
                    act.wait_ge(m["ep_xt_ps"], 2 * b + u + 1)
                    act.wait_ge(two["v_ps"][u], 2 * b)
                    nc.scalar.copy(xt_a[:, u, :], ps[:, PS_XA, :]).then_inc(two["xt_act"][u], 1)
                    for r in range(3):
                        act.wait_ge(m["ep_qk_ps"], 6 * b + 3 * u + r + 1)
                        act.wait_ge(two["middle"][u], 3 * b)
                        act.wait_ge(two["sent"][u], 64 * b)
                        nc.scalar.activation(full[:, u, r, :], ps[:, PS_QK + r, :], ACT.Identity,
                                             bias=bias[:, r:r + 1])
                        nc.scalar.activation(parts[:, u, r, 0, :], ps[:, PS_QK + r, :], ACT.Identity,
                                             bias=bias[:, r:r + 1]).then_inc(two["high"][u], 1)

        @block.tensor
        def _(pe):
            pe.wait_ge(m["ep_ident"], 1)
            pe.wait_ge(m["ep_weights"], 80)
            pe.wait_ge(m["ep_ones"], 1)
            with pe.Fori(0, B) as b:
                for u in range(2):
                    pe.wait_ge(two["xn"][u], b + 1)
                    if u == 0:
                        pe.wait_ge(two["xt_act"][1], b)
                        pe.wait_ge(two["xt_dve"][1], b)
                    else:
                        pe.wait_ge(two["xt_act"][0], b + 1)
                        pe.wait_ge(two["xt_dve"][0], b + 1)
                    for j in range(CT):
                        nc.tensor.transpose(ps[:, PS_XA, j * P:(j + 1) * P], xn[:, u, j, 0:P], s.ident[:])
                        last = nc.tensor.transpose(ps[0:DB, PS_XB, j * P:(j + 1) * P], xn[:, u, j, P:D], s.ident[:])
                    last.then_inc(m["ep_xt_ps"], 1)
                    pe.wait_ge(two["xt_act"][u], b + 1)
                    pe.wait_ge(two["xt_dve"][u], b + 1)
                    for r in range(3):
                        if u == 0:
                            pe.wait_ge(two["high"][1], 3 * b)
                        else:
                            pe.wait_ge(two["high"][0], 3 * (b + 1))
                        if r < 2:
                            last = nc.tensor.matmul(ps[:, PS_QK + r, :], w_a[:, r, :], xt_a[:, u, :],
                                                    start=True, stop=True)
                        else:
                            last = nc.tensor.matmul(ps[:, PS_QK + r, :], w_b[:], xt_b[0:DB, u, :],
                                                    start=True, stop=True)
                        last.then_inc(m["ep_qk_ps"], 1)
                    for half in range(2):
                        pe.wait_ge(m["ep_v_left"], 4 * b + 2 * u)
                        for j in range(2):
                            toks = slice((2 * half + j) * P, (2 * half + j + 1) * P)
                            dst = ps[:, PS_V + half, j * D:(j + 1) * D]
                            nc.tensor.matmul(dst, xt_a[:, u, toks], wv_a[:], start=True, stop=False)
                            last = nc.tensor.matmul(dst, xt_b[:, u, toks], wv_b[:], start=False, stop=True)
                        last.then_inc(two["v_ps"][u], 1)


def softmax_attention(nc, s):
    with ExitStack() as ctx:
        new_sem = ctx.enter_context(semaphores(nc))

        def sb(name, shape, dt=F32):
            return ctx.enter_context(nc.sbuf_tensor("sa_" + name, shape, dt))

        ps, v_nat, attn = s.psum, s.v_nat, s.attn
        HALF = 512
        STEPS = 2 * TB
        W = 32
        IT = HALF // P
        qst = sb("qst", [SK + 1, NG, GH, S], BF16)
        kst = sb("kst", [SK + 1, NG, GH, S], BF16)
        v_ext = sb("v_ext", [P, NG, TB, GH, W])
        probs = sb("probs", [P, 2, GH, HALF])
        out_t = sb("out_t", [P, 2, HALF])
        half_max = sb("half_max", [P, NG, GH, TB, 2])
        row_max = sb("row_max", [P, NG, GH, TB])
        max_rows = sb("max_rows", [HD, NG, 2, P], BF16)
        inv = sb("inv", [P, 2, IT, GH])
        max_dram = nc.dram_tensor("max_rows_dram", [NG, GH * TB, P], BF16, kind="Internal").ap()

        def per_group(name):
            return [new_sem(f"sa_{name}{g}") for g in range(NG)]

        loaded, max_stored, max_loaded, v_ready = map(per_group, ("loaded", "max_stored", "max_loaded", "v_ready"))
        scores_done, exp_done, pv_done, max_done = map(per_group, ("scores_done", "exp_done", "pv_done", "max_done"))
        ring_full = [new_sem(f"sa_ring_full{r}") for r in range(2)]
        ring_free = [new_sem(f"sa_ring_free{r}") for r in range(2)]
        out_copied = [new_sem(f"sa_out_copied{r}") for r in range(2)]
        inv_done, v_init, ones_row = (new_sem("sa_" + n)
                                      for n in ("inv_done", "v_init", "ones_row"))
        LOADS = 2 * len(Q_STACK)
        block = ctx.enter_context(nc.Block())

        def max_units(g, first, last):
            return [("max", g, k // (2 * TB), k // 2 % TB, k % 2) for k in range(first, last)]

        UNITS = GH * TB * 2
        AHEAD = 4
        PER = UNITS // STEPS
        before = max_units(0, 0, UNITS) + [("rows", 0, 0), ("rows", 0, 1)] + max_units(1, 0, AHEAD * PER)

        def step_units(g, st, last):
            n1, n2 = g + 1, g + 2
            split, tail = [], []
            if st < STEPS - AHEAD:
                if not (last and n1 >= NG):
                    split = max_units(n1 % NG, (AHEAD + st) * PER, (AHEAD + st + 1) * PER)
            elif not (last and n2 >= NG):
                k = st - (STEPS - AHEAD)
                split = max_units(n2 % NG, k * PER, (k + 1) * PER)
            if st == 1 and g > 0:
                tail.append(("out", g - 1, 1))
            if st == TB + 1:
                tail.append(("out", g, 0))
            if st == STEPS - AHEAD + 1 and not (last and n1 >= NG):
                tail += [("rows", n1 % NG, 0), ("rows", n1 % NG, 1)]
            if st == STEPS - 1 and g == NG - 1:
                tail.append(("out", g, 1))
            return split, tail

        def order(last):
            return [u for g in range(NG) for st in range(STEPS) for part in step_units(g, st, last) for u in part]

        RING0 = len(before)
        RING = len(order(False))
        assert RING0 % 2 == 0 and RING % 2 == 0
        place = {last: {u: n for n, u in enumerate(order(last))} for last in (False, True)}

        def turns(eng, body):
            with eng.Fori(0, B - 1) as b:
                body(b, False)
            body(B - 1, True)

        def uses(b, n):
            return n % 2, RING // 2 * b + (RING0 + n) // 2

        def load_stacks(sp, b, g):
            for which, (stack, order_) in enumerate(((qst, Q_STACK), (kst, K_STACK))):
                for k, part in enumerate(order_):
                    src = s.qk_parts[which, part, bass.ds(b * D + g * GD, GD), :]
                    sp.dma_start(stack[k * HD:(k + 1) * HD, g, :, :],
                                 src.rearrange("(s r) t -> r s t", r=HD)).then_inc(loaded[g], 16)

        def load_max(sp, g, b):
            sp.dma_start(max_dram[g].rearrange("(u k) t -> k u t", u=2), max_rows[:, g, :, :]).then_inc(max_stored[g], 16)
            sp.wait_ge(max_stored[g], 16 * (b + 1))
            sp.dma_start(qst[SK:SK + 1, g, :, :].rearrange("o s t -> o (s t)"),
                         max_dram[g].rearrange("(o k) t -> o (k t)", o=1)).then_inc(max_loaded[g], 16)

        @block.sync
        def _(sp):
            for g in range(NG):
                load_stacks(sp, 0, g)
            for r in range(2):
                sp.wait_ge(ring_free[r], (UNITS + 2) // 2)
            load_max(sp, 0, 0)

            def sequence(b, last):
                for g in range(NG):
                    if not (last and g == NG - 1):
                        n1, b1 = ((g + 1) % NG, b + (g + 1) // NG)
                        for half in range(2):
                            r, k = uses(b, place[last][("rows", n1, half)])
                            sp.wait_ge(ring_free[r], k + 1)
                            sp.nop(nofuse=True)
                        load_max(sp, n1, b1)
                    if not last:
                        sp.wait_ge(scores_done[g], 2 * STEPS * (b + 1))
                        load_stacks(sp, b + 1, g)
            turns(sp, sequence)

        @block.gpsimd
        def _(pool):
            nc.gpsimd.memset(v_ext[:], 0.0).then_inc(v_init, 1)
            pool.wait_ge(v_init, 1)
            nc.gpsimd.memset(v_ext[:, :, :, :, HD:HD + 1], 1.0).then_inc(v_init, 1)
            pool.wait_ge(v_init, 2)
            nc.gpsimd.memset(kst[SK:SK + 1, :, :, :], 1.0).then_inc(ones_row, 1)
            pool.wait_ge(ones_row, 1)
            with pool.Fori(0, B) as b:
                for g in range(NG):
                    pool.wait_ge(pv_done[g], STEPS * b)
                    src = v_nat[:, bass.ds(b * TB, TB), g * GD:(g + 1) * GD]
                    nc.gpsimd.tensor_copy(v_ext[:, g, :, :, 0:HD], src.rearrange("p t (s d) -> p t s d", s=GH)
                                          ).then_inc(v_ready[g], 1)

        @block.vector
        def _(dve):
            def consume(b, n, unit, r, k):
                kind, g = unit[0], unit[1]
                slot = ps[:, 4 + r, :]
                dve.wait_ge(ring_full[r], k + 1)
                if kind == "max":
                    hd, qt, half = unit[2:]
                    nc.vector.tensor_reduce(half_max[:, g, hd, qt, half:half + 1], slot, AX.X,
                                            ALU.max).then_inc(ring_free[r], 1)
                elif kind == "rows":
                    nc.vector.tensor_scalar(max_rows[:, g, unit[2], :], slot[0:HD, 0:P], -1.0, None,
                                            ALU.mult).then_inc(ring_free[r], 1)
                else:
                    half = unit[2]
                    heads = slot.rearrange("p (i s w) -> p i s w", s=GH, w=W)
                    nc.vector.reciprocal(inv[:, half], heads[:, :, :, HD]).then_inc(inv_done, 1)
                    dve.wait_ge(inv_done, b * 2 * NG + 2 * g + half + 1)
                    dst = attn[:, bass.ds(b * TB + half * IT, IT), g * GD:(g + 1) * GD]
                    nc.vector.tensor_tensor(dst.rearrange("p i (s d) -> p i s d", s=GH), heads[:, :, :, 0:HD],
                                            inv[:, half].unsqueeze(3).to_broadcast([P, IT, GH, HD]),
                                            ALU.mult).then_inc(ring_free[r], 1)

            def combine(g, r, k):
                dve.wait_ge(ring_free[1 - r], k + (1 if r else 0))
                dve.wait_ge(ring_free[r], k + 1)
                nc.vector.tensor_tensor(row_max[:, g], half_max[:, g, :, :, 0], half_max[:, g, :, :, 1],
                                        ALU.max).then_inc(max_done[g], 1)

            for n, unit in enumerate(before):
                if unit[0] == "rows" and unit[2] == 0:
                    combine(unit[1], (n - 1) % 2, (n - 1) // 2)
                consume(0, n, unit, n % 2, n // 2)

            def sequence(b, last):
                for n, unit in enumerate(order(last)):
                    r, k = uses(b, n)
                    g = unit[1]
                    if unit[0] == "rows":
                        b1 = b + 1 if g == 0 else b
                        if unit[2] == 0:
                            r1, k1 = uses(b, n - 1)
                            combine(g, r1, k1)
                        dve.wait_ge(max_stored[g], 16 * b1)
                    consume(b, n, unit, r, k)
            turns(dve, sequence)

        @block.scalar
        def _(act):
            def exps(b, g, st):
                for pair in range(2):
                    act.wait_ge(scores_done[g], 2 * STEPS * b + 2 * st + pair + 1)
                    if pair == 0:
                        if st >= 2:
                            act.wait_ge(pv_done[g], STEPS * b + st - 1)
                        elif g > 0:
                            act.wait_ge(pv_done[g - 1], STEPS * b + STEPS - 1 + st)
                        else:
                            act.wait_ge(pv_done[NG - 1], STEPS * b)
                    nc.scalar.activation(probs[:, st % 2, 2 * pair:2 * pair + 2, :], ps[:, 2 * pair:2 * pair + 2, :],
                                         ACT.Exp, scale=SCALE0).then_inc(exp_done[g], 1)

            def copy_out(b, g, half, last):
                act.wait_ge(pv_done[g], STEPS * b + TB * (half + 1))
                k_half = 2 * g + half
                if k_half >= 2:
                    r, k = uses(b, place[last][("out", g - 1, half)])
                else:
                    r, k = uses(b - 1, place[False][("out", NG - 1, half)])
                act.wait_ge(ring_full[r], k + 1)
                nc.scalar.copy(out_t[:, half, :], ps[:, 6 + half, :]).then_inc(out_copied[half], 1)

            def sequence(b, last):
                for g in range(NG):
                    for st in range(STEPS):
                        exps(b, g, st)
                        if st == 0 and g > 0:
                            copy_out(b, g - 1, 1, last)
                        if st == TB:
                            copy_out(b, g, 0, last)
                copy_out(b, NG - 1, 1, last)
            turns(act, sequence)

        @block.tensor
        def _(pe):
            pe.wait_ge(ones_row, 1)

            def scores(b, g, st, pair, follows):
                half, kt = st // TB, st % TB
                if pair == 0 and st == 0:
                    pe.wait_ge(loaded[g], 16 * LOADS * (b + 1))
                    pe.wait_ge(max_loaded[g], 16 * (b + 1))
                if follows is not None:
                    pe.wait_ge(exp_done[follows[0]], follows[1] + pair + 1)
                for hd in (2 * pair, 2 * pair + 1):
                    last = nc.tensor.matmul(ps[:, hd, :], kst[:, g, hd, kt * P:(kt + 1) * P],
                                            qst[:, g, hd, half * HALF:(half + 1) * HALF], start=True, stop=True)
                last.then_inc(scores_done[g], 1)

            def produce(b, unit, r, k):
                kind, g = unit[0], unit[1]
                pe.wait_ge(ring_free[r], k)
                if kind == "max":
                    hd, qt, half = unit[2:]
                    last = nc.tensor.matmul(ps[:, 4 + r, :], qst[0:SK, g, hd, qt * P:(qt + 1) * P],
                                            kst[0:SK, g, hd, half * 512:(half + 1) * 512], start=True, stop=True)
                elif kind == "rows":
                    heads = row_max[:, g].rearrange("p s t -> p (s t)")
                    last = nc.tensor.transpose(ps[0:HD, 4 + r, 0:P], heads[:, unit[2] * HD:(unit[2] + 1) * HD],
                                               s.ident[:])
                else:
                    half = unit[2]
                    pe.wait_ge(out_copied[half], NG * b + g + 1)
                    for i in range(IT):
                        last = nc.tensor.transpose(ps[:, 4 + r, i * P:(i + 1) * P],
                                                   out_t[:, half, i * P:(i + 1) * P], s.ident[:])
                last.then_inc(ring_full[r], 1)

            def times_v(b, g, st):
                half, kt = st // TB, st % TB
                if st == 0:
                    pe.wait_ge(v_ready[g], b + 1)
                if kt == 0:
                    pe.wait_ge(out_copied[half], NG * b + g)
                pe.wait_ge(exp_done[g], 2 * STEPS * b + 2 * st + 2)
                for hd in range(GH):
                    last = nc.tensor.matmul(ps[hd * W:(hd + 1) * W, 6 + half, :], v_ext[:, g, kt, hd, :],
                                            probs[:, st % 2, hd, :], start=(kt == 0), stop=(kt == TB - 1))
                last.then_inc(pv_done[g], 1)

            for n, unit in enumerate(before):
                if unit[0] == "max" and unit[2:] == (0, 0, 0):
                    pe.wait_ge(loaded[unit[1]], 16 * LOADS)
                if unit[0] == "rows":
                    pe.wait_ge(max_done[unit[1]], 1)
                produce(0, unit, n % 2, n // 2)
            for pair in range(2):
                scores(0, 0, 0, pair, None)

            def sequence(b, last):
                n = 0
                for g in range(NG):
                    for st in range(STEPS):
                        split, tail = step_units(g, st, last)
                        final = last and g == NG - 1 and st == STEPS - 1
                        nb, ng, nst = (b, g, st + 1) if st + 1 < STEPS else (b + (g + 1) // NG, (g + 1) % NG, 0)
                        for pair in range(2):
                            if not final:
                                scores(nb, ng, nst, pair, (g, 2 * STEPS * b + 2 * st))
                            for unit in split[pair * PER // 2:(pair + 1) * PER // 2]:
                                ug = unit[1]
                                if unit[2:] == (0, 0, 0):
                                    pe.wait_ge(loaded[ug], 16 * LOADS * ((b if ug > g else b + 1) + 1))
                                produce(b, unit, *uses(b, n))
                                n += 1
                        times_v(b, g, st)
                        for unit in tail:
                            if unit[0] == "rows":
                                pe.wait_ge(max_done[unit[1]], (b + 1 if unit[1] == 0 else b) + 1)
                            produce(b, unit, *uses(b, n))
                            n += 1
            turns(pe, sequence)


def close_attention(nc, a, s, layer):
    with ExitStack() as ctx:
        new_sem = ctx.enter_context(semaphores(nc))

        def sb(name, shape, dt=F32):
            return ctx.enter_context(nc.sbuf_tensor(f"ca{layer}_" + name, shape, dt))

        h, attn, ps = s.h, s.attn, s.psum
        router = a[f"w{layer}_router"]
        RB = router.shape[0] - P
        wo_a = sb("wo_a", [P, D])
        wo_b = sb("wo_b", [DB + 1, D])
        wr_a = sb("wr_a", [P, E])
        wr_b = sb("wr_b", [RB, E])
        rows = sb("rows", [P, 2, CT, D])
        rows_ta = sb("rows_ta", [P, 2, CHUNK])
        rows_tb = sb("rows_tb", [DB + 1, 2, CHUNK])
        x2 = sb("x2", [P, 2, CT, D])
        x2_ta = sb("x2_ta", [P, 2, CHUNK])
        x2_tb = sb("x2_tb", [DB + 1, 2, CHUNK])
        stats = sb("stats", [P, 2, CT, 6])
        mv = sb("mv", [P, 2, CT, 2])
        var_eps = sb("var_eps", [P, 2, CT])
        std = sb("std", [P, 2, CT])
        tmp = sb("tmp", [P, 2, CT])
        weights, ones, chain = (new_sem(f"ca{layer}_{n}") for n in ("weights", "ones", "chain"))
        two = {n: [new_sem(f"ca{layer}_{n}{u}") for u in range(2)] for n in
               ("rows", "rows_ps", "rows_act", "rows_dve", "out_ps", "var", "std", "x2", "x2_ps", "x2_act", "x2_dve",
                "logits_ps", "logits", "kept", "added")}
        block = ctx.enter_context(nc.Block())
        PS_A, PS_B, PS_O, PS_XA, PS_XB, PS_L = 0, 1, 2, 4, 5, 6

        @block.sync
        def _(sp):
            for dst, src in ((wo_a[:], a[f"w{layer}_out"][0:P, :]), (wo_b[:], a[f"w{layer}_out"][P:D + 1, :]),
                             (wr_a[:], router[0:P, :]), (wr_b[:], router[P:, :])):
                sp.dma_start(dst, src).then_inc(weights, 16)

        def before(sem, b, u):
            return (sem[1], b) if u == 0 else (sem[0], b + 1)

        @block.gpsimd
        def _(pool):
            with pool.Fori(0, B) as b:
                for u in range(2):
                    pool.wait_ge(two["rows_ps"][u], b)
                    pool.nop(nofuse=True)
                    nc.gpsimd.tensor_copy(rows[:, u], attn[:, bass.ds(b * TB + u * CT, CT), :]
                                          ).then_inc(two["rows"][u], 1)
                    pool.wait_ge(two["rows"][u], b + 1)
                    pool.wait_ge(two["x2"][u], b + 1)
                    pool.nop(nofuse=True)
                    nc.gpsimd.tensor_copy(attn[:, bass.ds(b * TB + u * CT, CT), :], x2[:, u]
                                          ).then_inc(two["kept"][u], 1)

        @block.vector
        def _(dve):
            nc.vector.memset(rows_tb[DB:DB + 1, :, :], 1.0).then_inc(ones, 1)
            nc.vector.memset(x2_tb[DB:DB + 1, :, :], 1.0).then_inc(ones, 1)
            with dve.Fori(0, B) as b:
                link = Chain(dve, chain, 2 * 7, b)
                for u in range(2):
                    dve.wait_ge(two["rows_ps"][u], b + 1)
                    dve.wait_ge(two["out_ps"][u], 2 * b)
                    nc.vector.tensor_copy(rows_tb[0:DB, u, :], ps[0:DB, PS_B, :]).then_inc(two["rows_dve"][u], 1)
                    for half in range(2):
                        dve.wait_ge(two["out_ps"][u], 2 * b + half + 1)
                        tiles = h[:, bass.ds(b * TB + u * CT + 2 * half, 2), :]
                        nc.vector.tensor_tensor(tiles, tiles, ps[:, PS_O + half, 0:2 * D].rearrange(
                            "p (t d) -> p t d", d=D), ALU.add).then_inc(two["added"][u], 1)
                    dve.wait_ge(two["added"][u], 2 * b + 2)
                    tiles = [h[:, b * TB + (u * CT + j), :] for j in range(CT)]
                    layer_norm_stats(nc, dve, link, tiles, stats[:, u], mv[:, u], var_eps[:, u], two["var"][u])
                    dve.wait_ge(two["std"][u], b + 1)
                    dve.wait_ge(two["x2_ps"][u], b)
                    dve.wait_ge(two["kept"][u], b)
                    layer_norm_apply(nc, link, tiles, x2[:, u], mv[:, u], var_eps[:, u], std[:, u],
                                     tmp[:, u]).then_inc(two["x2"][u], 1)
                    dve.wait_ge(two["x2_ps"][u], b + 1)
                    dve.wait_ge(two["logits_ps"][u], b)
                    nc.vector.tensor_copy(x2_tb[0:DB, u, :], ps[0:DB, PS_XB, :]).then_inc(two["x2_dve"][u], 1)
                    dve.wait_ge(two["logits_ps"][u], b + 1)
                    nc.vector.tensor_copy(s.logits[:, bass.ds(b * TB + u * CT, CT), :],
                                          ps[:, PS_L, 0:CT * E].rearrange("p (t e) -> p t e", e=E)
                                          ).then_inc(two["logits"][u], 1)

        @block.scalar
        def _(act):
            with act.Fori(0, B) as b:
                for u in range(2):
                    act.wait_ge(two["rows_ps"][u], b + 1)
                    act.wait_ge(two["out_ps"][u], 2 * b)
                    nc.scalar.copy(rows_ta[:, u, :], ps[:, PS_A, :]).then_inc(two["rows_act"][u], 1)
                    act.wait_ge(two["var"][u], b + 1)
                    nc.scalar.activation(std[:, u], var_eps[:, u], ACT.Sqrt).then_inc(two["std"][u], 1)
                    act.wait_ge(two["x2_ps"][u], b + 1)
                    act.wait_ge(two["logits_ps"][u], b)
                    nc.scalar.copy(x2_ta[:, u, :], ps[:, PS_XA, :]).then_inc(two["x2_act"][u], 1)

        @block.tensor
        def _(pe):
            pe.wait_ge(weights, 64)
            pe.wait_ge(ones, 2)

            def transposes(src, bank_a, bank_b):
                for j in range(CT):
                    nc.tensor.transpose(ps[:, bank_a, j * P:(j + 1) * P], src[:, j, 0:P], s.ident[:])
                    last = nc.tensor.transpose(ps[0:DB, bank_b, j * P:(j + 1) * P], src[:, j, P:D], s.ident[:])
                return last

            with pe.Fori(0, B) as b:
                for u in range(2):
                    pe.wait_ge(two["rows"][u], b + 1)
                    pe.wait_ge(*before(two["rows_act"], b, u))
                    pe.wait_ge(*before(two["rows_dve"], b, u))
                    transposes(rows[:, u], PS_A, PS_B).then_inc(two["rows_ps"][u], 1)
                    pe.wait_ge(two["rows_act"][u], b + 1)
                    pe.wait_ge(two["rows_dve"][u], b + 1)
                    sem, n = before(two["added"], 2 * b, u) if u == 0 else (two["added"][0], 2 * b + 2)
                    pe.wait_ge(sem, n)
                    for half in range(2):
                        for j in range(2):
                            toks = slice((2 * half + j) * P, (2 * half + j + 1) * P)
                            dst = ps[:, PS_O + half, j * D:(j + 1) * D]
                            nc.tensor.matmul(dst, rows_ta[:, u, toks], wo_a[:], start=True, stop=False)
                            last = nc.tensor.matmul(dst, rows_tb[:, u, toks], wo_b[:], start=False, stop=True)
                        last.then_inc(two["out_ps"][u], 1)
                    pe.wait_ge(two["x2"][u], b + 1)
                    pe.wait_ge(*before(two["x2_act"], b, u))
                    pe.wait_ge(*before(two["x2_dve"], b, u))
                    transposes(x2[:, u], PS_XA, PS_XB).then_inc(two["x2_ps"][u], 1)
                    pe.wait_ge(two["x2_act"][u], b + 1)
                    pe.wait_ge(two["x2_dve"][u], b + 1)
                    pe.wait_ge(*before(two["logits"], b, u))
                    for j in range(CT):
                        toks = slice(j * P, (j + 1) * P)
                        dst = ps[:, PS_L, j * E:(j + 1) * E]
                        nc.tensor.matmul(dst, x2_ta[:, u, toks], wr_a[:], start=True, stop=False)
                        last = nc.tensor.matmul(dst, x2_tb[0:RB, u, toks], wr_b[:], start=False, stop=True)
                    last.then_inc(two["logits_ps"][u], 1)


def blocks_of(k):
    n = k * NT + E - 1
    return n + n % 2


def route(nc, a, s, layer, k_top, x_rows):
    with ExitStack() as ctx:
        new_sem = ctx.enter_context(semaphores(nc))

        def sb(name, shape, dt=F32):
            return ctx.enter_context(nc.sbuf_tensor(f"ro{layer}_" + name, shape, dt))

        NBLK, KT = blocks_of(k_top), k_top * NT
        SHARED = NT if layer == 1 else 0
        ps = s.psum
        before_me = sb("before_me", [P, P])
        all_ones = sb("all_ones", [P, P])
        expert_i = sb("expert_i", [P, E], I32)
        block_i = sb("block_i", [P, NBLK], I32)
        expert_f = sb("expert_f", [P, E])
        block_f = sb("block_f", [P, NBLK])
        bias = sb("bias", [P, E])
        top = sb("top", [P, NT])
        shifted = sb("shifted", [P, NT, E])
        exps = sb("exps", [P, NT, E])
        total = sb("total", [P, NT])
        scores = sb("scores", [P, NT, E])
        choice = sb("choice", [P, NT, E])
        best = sb("best", [P, NT, 8])
        best_i = sb("best_i", [P, NT, 8], U32)
        best_f = sb("best_f", [P, NT, 8])
        chosen = sb("chosen", [P, k_top, NT, E])
        tile_sum = sb("tile_sum", [P, KT, E])
        run_sum = sb("run_sum", [P, E, KT])
        count_i = sb("count_i", [P, E], I32)
        n_blocks = sb("n_blocks", [P, E])
        end_block = sb("end_block", [P, E])
        start_row = sb("start_row", [P, E])
        place = sb("place", [P, KT, E])
        place_f = sb("place_f", [P, KT])
        reached = sb("reached", [P, NBLK, E])
        owner = sb("owner", [P, NBLK + SHARED])
        picked = sb("picked", [P, NT, E])
        weight_sum = sb("weight_sum", [P, NT])
        m = {n: new_sem(f"ro{layer}_{n}") for n in
             ("chain", "ones", "iota", "shifted", "exps", "chosen", "ranks", "placed", "bias", "sent")}
        scattered = [new_sem(f"ro{layer}_scattered{i}") for i in range(8)]
        block = ctx.enter_context(nc.Block())

        @block.sync
        def _(sp):
            if layer == 1:
                sp.dma_start(bias[:], a["b1_expert"]).then_inc(m["bias"], 16)
                sp.dma_start(x_rows[NBLK * P:, :].rearrange("(t p) d -> p t d", p=P), s.attn[:]
                             ).then_inc(m["sent"], 16)
                sp.wait_ge(m["sent"], 16)

        @block.gpsimd
        def _(pool):
            nc.gpsimd.iota(expert_i[:], [[1, E]], base=0, channel_multiplier=0).then_inc(m["iota"], 1)
            nc.gpsimd.iota(block_i[:], [[1, NBLK]], base=0, channel_multiplier=0).then_inc(m["iota"], 1)
            nc.gpsimd.memset(all_ones[:], 1.0).then_inc(m["ones"], 1)
            pool.wait_ge(m["ones"], 1)
            nc.gpsimd.affine_select(out=before_me[:], in_=all_ones[:], compare_op=ALU.is_gt, fill=0.0, base=0,
                                    pattern=[[1, P]], channel_multiplier=-1).then_inc(m["ones"], 1)
            pool.wait_ge(m["placed"], 1)
            for i in range(KT):
                pool.indirect_dma_start(out=x_rows, out_offset=bass.IndirectOffsetOnAxis(ap=s.place[:, i:i + 1], axis=0),
                                        in_=s.attn[:, i % NT, :], in_offset=None).then_inc(scattered[i % 8], 16)
            for i in range(8):
                pool.wait_ge(scattered[i], 16 * (KT // 8))

        @block.tensor
        def _(pe):
            pe.wait_ge(m["ones"], 2)
            pe.wait_ge(m["chosen"], k_top)
            flat = chosen[:].rearrange("p k t e -> p (k t e)")
            nc.tensor.matmul(ps[:, 0, 0:KT * E], before_me[:], flat, start=True, stop=True)
            nc.tensor.matmul(ps[:, 1, 0:KT * E], all_ones[:], flat, start=True, stop=True).then_inc(m["ranks"], 1)

        @block.scalar
        def _(act):
            act.wait_ge(m["shifted"], 1)
            nc.scalar.activation(exps[:], shifted[:], ACT.Exp).then_inc(m["exps"], 1)

        @block.vector
        def _(dve):
            link = Chain(dve, m["chain"])

            def over(x, shape):
                return x.to_broadcast(shape)

            te = [P, NT, E]
            link(nc.vector.tensor_reduce(top[:], s.logits[:], AX.X, ALU.max))
            nc.vector.tensor_tensor(shifted[:], s.logits[:], over(top[:].unsqueeze(2), te),
                                    ALU.subtract).then_inc(m["shifted"], 1)
            dve.wait_ge(m["exps"], 1)
            link(nc.vector.tensor_reduce(total[:], exps[:], AX.X, ALU.add))
            link(nc.vector.reciprocal(total[:], total[:]))
            link(nc.vector.tensor_tensor(scores[:], exps[:], over(total[:].unsqueeze(2), te), ALU.mult))
            ranked = scores
            if layer == 1:
                dve.wait_ge(m["bias"], 16)
                link(nc.vector.tensor_tensor(choice[:], scores[:], over(bias[:].unsqueeze(1), te), ALU.add))
                ranked = choice
            for t in range(NT):
                last = nc.vector.max(best[:, t, :], ranked[:, t, :])
            link(last)
            for t in range(NT):
                last = nc.vector.max_index(best_i[:, t, :], best[:, t, :], ranked[:, t, :])
            link(last)
            link(nc.vector.tensor_copy(best_f[:], best_i[:]))
            dve.wait_ge(m["iota"], 2)
            link(nc.vector.tensor_copy(expert_f[:], expert_i[:]))
            link(nc.vector.tensor_copy(block_f[:], block_i[:]))
            for k in range(k_top):
                nc.vector.tensor_tensor(chosen[:, k], over(expert_f[:].unsqueeze(1), te),
                                        over(best_f[:, :, k:k + 1], te), ALU.is_equal).then_inc(m["chosen"], 1)
            if layer == 0:
                link(nc.vector.tensor_copy(s.gate[:, 0, :], total[:]))
            else:
                for k in range(k_top):
                    dve.wait_ge(m["chosen"], k + 1)
                    link(nc.vector.tensor_tensor(picked[:], scores[:], chosen[:, k], ALU.mult))
                    link(nc.vector.tensor_reduce(s.gate[:, k, :], picked[:], AX.X, ALU.add))
                link(nc.vector.tensor_tensor(weight_sum[:], s.gate[:, 0, :], s.gate[:, 1, :], ALU.add))
                link(nc.vector.tensor_scalar(weight_sum[:], weight_sum[:], 1e-9, None, ALU.add))
                link(nc.vector.reciprocal(weight_sum[:], weight_sum[:]))
                for k in range(k_top):
                    link(nc.vector.tensor_tensor(s.gate[:, k, :], s.gate[:, k, :], weight_sum[:], ALU.mult))
            dve.wait_ge(m["ranks"], 1)
            link(nc.vector.tensor_copy(tile_sum[:].rearrange("p t e -> p (t e)"), ps[:, 1, 0:KT * E]))
            dve.wait_ge(m["ones"], 2)
            for e in range(E):
                last = nc.vector.tensor_tensor_scan(run_sum[:, e, :], all_ones[:, 0:KT], tile_sum[:, :, e], 0.0,
                                                    ALU.mult, ALU.add)
            link(last)
            link(nc.vector.tensor_scalar(n_blocks[:], run_sum[:, :, KT - 1], float(P - 1), None, ALU.add))
            link(nc.vector.tensor_copy(count_i[:], n_blocks[:]))
            link(nc.vector.tensor_scalar(count_i[:], count_i[:], P.bit_length() - 1, None, ALU.arith_shift_right))
            link(nc.vector.tensor_copy(n_blocks[:], count_i[:]))
            link(nc.vector.tensor_tensor_scan(end_block[:], all_ones[:, 0:E], n_blocks[:], 0.0, ALU.mult, ALU.add))
            link(nc.vector.tensor_tensor(start_row[:], end_block[:], n_blocks[:], ALU.subtract))
            link(nc.vector.tensor_scalar(start_row[:], start_row[:], float(P), None, ALU.mult))
            kte = [P, KT, E]
            link(nc.vector.tensor_tensor(place[:], run_sum[:].rearrange("p e t -> p t e"), tile_sum[:], ALU.subtract))
            link(nc.vector.tensor_tensor(place[:], place[:], ps[:, 0, 0:KT * E].rearrange("p (t e) -> p t e", e=E),
                                         ALU.add))
            link(nc.vector.tensor_tensor(place[:], place[:], over(start_row[:].unsqueeze(1), kte), ALU.add))
            link(nc.vector.tensor_tensor(place[:], place[:], chosen[:].rearrange("p k t e -> p (k t) e"), ALU.mult))
            link(nc.vector.tensor_reduce(place_f[:], place[:], AX.X, ALU.add))
            nc.vector.tensor_copy(s.place[:, 0:KT], place_f[:]).then_inc(m["placed"], 1)
            nbe = [P, NBLK, E]
            if SHARED:
                nc.vector.memset(owner[:, NBLK:], float(E))
            link(nc.vector.tensor_tensor(reached[:], over(block_f[:].unsqueeze(2), nbe),
                                         over(end_block[:].unsqueeze(1), nbe), ALU.is_ge))
            link(nc.vector.tensor_reduce(owner[:, 0:NBLK], reached[:], AX.X, ALU.add))
            link(nc.vector.tensor_scalar(owner[:, 0:NBLK], owner[:, 0:NBLK], float(E - 1), None, ALU.min))
            link(nc.vector.tensor_copy(s.owner[:, 0:NBLK + SHARED], owner[:]))


def experts(nc, a, s, layer, k_top, x_rows, y_rows):
    with ExitStack() as ctx:
        new_sem = ctx.enter_context(semaphores(nc))

        def sb(name, shape, dt=F32):
            return ctx.enter_context(nc.sbuf_tensor(f"ex{layer}_" + name, shape, dt))

        F = (F0, F1)[layer]
        FC = F // P
        NE = E + layer
        N = blocks_of(k_top) + NT * layer
        TURNS = N // 2
        ps = s.psum
        up_a = sb("up_a", [P, 2, NE, F])
        up_b = sb("up_b", [DB, 2, NE, F])
        down = sb("down", [P, NE, FC, D])
        x = sb("x", [P, 2, D])
        xt_a = sb("xt_a", [P, 2, P])
        xt_b = sb("xt_b", [DB, 2, P])
        silu = sb("silu", [P, 2, F])
        g = sb("g", [P, 2, F])
        g_t = sb("g_t", [P, 2, F])
        y = sb("y", [P, 2, D])
        weights = new_sem(f"ex{layer}_weights")
        two = {n: [new_sem(f"ex{layer}_{n}{u}") for u in range(2)] for n in
               ("loaded", "stored", "x_ps", "xt_a", "xt_b", "gate_ps", "up_ps", "silu", "g", "g_ps", "g_t", "y_ps", "y")}
        block = ctx.enter_context(nc.Block())
        PS_X, PS_GATE, PS_UP, PS_G, PS_Y = 0, 1, 3, 5, 6

        def blocks(eng, first, step, final):
            first()
            with eng.Fori(0, TURNS - 1) as i:
                step(1, i, 0, i, 0, i + 1)
                step(0, i + 1, 1, i, 1, i + 1)
            final(1, TURNS - 1, 0, TURNS - 1)

        @block.sync
        def _(sp):
            for dst, src in ((up_a[:], a[f"e{layer}_up_a"]), (up_b[:], a[f"e{layer}_up_b"]), (down[:], a[f"e{layer}_down"])):
                sp.dma_start(dst, src).then_inc(weights, 16)

            def load(u, k):
                sp.wait_ge(two["x_ps"][u], k)
                sp.dma_start(x[:, u, :], x_rows[bass.ds((2 * k + u) * P, P), :]).then_inc(two["loaded"][u], 16)

            def store(u, k):
                sp.wait_ge(two["y"][u], k + 1)
                sp.dma_start(y_rows[bass.ds((2 * k + u) * P, P), :], y[:, u, :]).then_inc(two["stored"][u], 16)

            def first():
                load(0, 0)
                load(1, 0)

            def step(u, k, pu, pk, nu, nk):
                load(nu, nk)
                store(pu, pk)

            def final(u, k, pu, pk):
                store(pu, pk)
                store(u, k)
            first()
            with sp.Fori(0, TURNS - 1) as i:
                load(0, i + 1)
                store(0, i)
                load(1, i + 1)
                store(1, i)
            final(1, TURNS - 1, 0, TURNS - 1)
            for u in range(2):
                sp.wait_ge(two["stored"][u], 16 * TURNS)

        @block.scalar
        def _(act):
            def copy_x(u, k):
                act.wait_ge(two["x_ps"][u], k + 1)
                act.wait_ge(two["up_ps"][u], k)
                nc.scalar.copy(xt_a[:, u, :], ps[:, PS_X, 0:P]).then_inc(two["xt_a"][u], 1)
                nc.scalar.copy(xt_b[:, u, :], ps[0:DB, PS_X, P:2 * P]).then_inc(two["xt_b"][u], 1)

            def activate(u, k):
                act.wait_ge(two["gate_ps"][u], k + 1)
                act.wait_ge(two["g"][u], k)
                nc.scalar.activation(silu[:, u, :], ps[:, PS_GATE + u, 0:F], ACT.Silu).then_inc(two["silu"][u], 1)

            def first():
                copy_x(0, 0)
                activate(0, 0)
                copy_x(1, 0)

            def step(u, k, pu, pk, nu, nk):
                activate(u, k)
                copy_x(nu, nk)

            blocks(act, first, step, lambda u, k, pu, pk: activate(u, k))

        @block.vector
        def _(dve):
            def product(u, k):
                dve.wait_ge(two["silu"][u], k + 1)
                dve.wait_ge(two["up_ps"][u], k + 1)
                dve.wait_ge(two["g_ps"][u], k)
                nc.vector.tensor_tensor(g[:, u, :], silu[:, u, :], ps[:, PS_UP + u, 0:F], ALU.mult
                                        ).then_inc(two["g"][u], 1)

            def copy_g(u, k):
                dve.wait_ge(two["g_ps"][u], k + 1)
                dve.wait_ge(two["y_ps"][u], k)
                nc.vector.tensor_copy(g_t[:, u, :], ps[:, PS_G, 0:F]).then_inc(two["g_t"][u], 1)

            def copy_y(u, k):
                dve.wait_ge(two["y_ps"][u], k + 1)
                dve.wait_ge(two["stored"][u], 16 * k)
                nc.vector.tensor_copy(y[:, u, :], ps[:, PS_Y, 0:D]).then_inc(two["y"][u], 1)

            def step(u, k, pu, pk, nu, nk):
                copy_g(pu, pk)
                product(u, k)
                copy_y(pu, pk)

            def final(u, k, pu, pk):
                step(u, k, pu, pk, None, None)
                copy_g(u, k)
                copy_y(u, k)
            blocks(dve, lambda: product(0, 0), step, final)

        @block.tensor
        def _(pe):
            pe.wait_ge(weights, 48)

            def owner(u, k):
                return pe.value_load(s.owner[0:1, bass.ds(2 * k + u, 1)], min_val=0, max_val=NE - 1)

            def transpose_x(u, k, pu, pk):
                pe.wait_ge(two["loaded"][u], 16 * (k + 1))
                if pk is not None:
                    pe.wait_ge(two["xt_b"][pu], pk + 1)
                nc.tensor.transpose(ps[:, PS_X, 0:P], x[:, u, 0:P], s.ident[:])
                nc.tensor.transpose(ps[0:DB, PS_X, P:2 * P], x[:, u, P:D], s.ident[:]).then_inc(two["x_ps"][u], 1)

            def project(u, k, e, which, bank, done):
                dst = ps[:, bank + u, 0:F]
                nc.tensor.matmul(dst, xt_a[:, u, :], up_a[:, which, bass.ds(e, 1), :].rearrange("p o f -> p (o f)"),
                                 start=True, stop=False)
                nc.tensor.matmul(dst, xt_b[:, u, :], up_b[:, which, bass.ds(e, 1), :].rearrange("p o f -> p (o f)"),
                                 start=False, stop=True).then_inc(done[u], 1)

            def gate(u, k, e):
                pe.wait_ge(two["xt_b"][u], k + 1)
                pe.wait_ge(two["silu"][u], k)
                project(u, k, e, 0, PS_GATE, two["gate_ps"])

            def up(u, k, e):
                pe.wait_ge(two["g"][u], k)
                project(u, k, e, 1, PS_UP, two["up_ps"])

            def transpose_g(u, k, pu, pk):
                pe.wait_ge(two["g"][u], k + 1)
                if pk is not None:
                    pe.wait_ge(two["g_t"][pu], pk)
                for c in range(FC):
                    last = nc.tensor.transpose(ps[:, PS_G, c * P:(c + 1) * P], g[:, u, c * P:(c + 1) * P], s.ident[:])
                last.then_inc(two["g_ps"][u], 1)

            def down_project(u, k, e, pu, pk):
                pe.wait_ge(two["g_t"][u], k + 1)
                if pk is not None:
                    pe.wait_ge(two["y"][pu], pk)
                for c in range(FC):
                    last = nc.tensor.matmul(ps[:, PS_Y, 0:D], g_t[:, u, c * P:(c + 1) * P],
                                            down[:, bass.ds(e, 1), c, :].rearrange("p o d -> p (o d)"),
                                            start=(c == 0), stop=(c == FC - 1))
                last.then_inc(two["y_ps"][u], 1)

            def first():
                transpose_x(0, 0, None, None)
                e = owner(0, 0)
                gate(0, 0, e)
                up(0, 0, e)
                transpose_x(1, 0, 0, 0)

            def middle(u, k, pu, pk):
                e = owner(u, k)
                gate(u, k, e)
                transpose_g(pu, pk, u, k)
                up(u, k, e)
                down_project(pu, pk, owner(pu, pk), u, k)

            def step(u, k, pu, pk, nu, nk):
                middle(u, k, pu, pk)
                transpose_x(nu, nk, u, k)

            def final(u, k, pu, pk):
                middle(u, k, pu, pk)
                transpose_g(u, k, pu, pk + 1)
                down_project(u, k, owner(u, k), pu, pk + 1)
            blocks(pe, first, step, final)




def mix_experts(nc, a, s, layer, k_top, y_rows):
    with ExitStack() as ctx:
        new_sem = ctx.enter_context(semaphores(nc))

        def sb(name, shape, dt=F32):
            return ctx.enter_context(nc.sbuf_tensor(f"mx{layer}_" + name, shape, dt))

        RING = 8
        h = s.h
        rows = sb("rows", [P, RING, D])
        rounded = sb("rounded", [P, 2, D], BF16)
        landed = [new_sem(f"mx{layer}_landed{i}") for i in range(RING)]
        chain, added, shared, mixed = (new_sem(f"mx{layer}_{n}")
                                       for n in ("chain", "added", "shared", "mixed"))
        block = ctx.enter_context(nc.Block())
        jobs = [(t, k) for t in range(NT) for k in range(k_top)]

        if layer == 1:
            @block.sync
            def _(sp):
                sp.dma_start(s.attn[:], y_rows[blocks_of(k_top) * P:, :].rearrange("(t p) d -> p t d", p=P)
                             ).then_inc(shared, 16)

        @block.gpsimd
        def _(pool):
            for n, (t, k) in enumerate(jobs):
                if n >= RING:
                    pool.wait_ge(added, n - RING + 1)
                i = k * NT + t
                pool.indirect_dma_start(out=rows[:, n % RING, :], out_offset=None, in_=y_rows,
                                        in_offset=bass.IndirectOffsetOnAxis(ap=s.place[:, i:i + 1], axis=0)
                                        ).then_inc(landed[n % RING], 16)

        @block.vector
        def _(dve):
            link = Chain(dve, chain)
            if layer == 1:
                dve.wait_ge(shared, 16)
                for t in range(NT):
                    last = nc.vector.tensor_tensor(h[:, t, :], h[:, t, :], s.attn[:, t, :], ALU.add)
                link(last)
            for n, (t, k) in enumerate(jobs):
                dve.wait_ge(landed[n % RING], 16 * (n // RING + 1))
                if k:
                    dve.wait_ge(added, n)
                src = rows[:, n % RING, :]
                if layer == 0:
                    link(nc.vector.tensor_copy(rounded[:, n % 2, :], src))
                    src = rounded[:, n % 2, :]
                nc.vector.scalar_tensor_tensor(out=h[:, t, :], in0=src, scalar=s.gate[:, k, t:t + 1],
                                               in1=h[:, t, :], op0=ALU.mult, op1=ALU.add).then_inc(added, 1)


def relu_attention(nc, a, s):
    with ExitStack() as ctx:
        new_sem = ctx.enter_context(semaphores(nc))

        def sb(name, shape, dt=F32):
            return ctx.enter_context(nc.sbuf_tensor("ra_" + name, shape, dt))

        h, attn, ps = s.h, s.attn, s.psum
        V1 = HD + 1
        HH = H // 2
        PAIRS = H // 2
        PA = P // (2 * HD)
        FA = 2 * PA * M_FEAT
        FB = H * M_FEAT - FA
        NORM = float(HD) ** -0.25
        CTX, OUT, SLOTS = 4, 6, 3
        w_a = sb("w_a", [P, 3, P])
        w_b = sb("w_b", [DB, 3, P])
        wv_a = sb("wv_a", [P, D])
        wv_b = sb("wv_b", [DB + 1, D])
        bias = sb("bias", [P, 3])
        half_bias = sb("half_bias", [P, 3])
        feat_a = sb("feat_a", [P, FA])
        feat_b = sb("feat_b", [P, 2, FB])
        stats = sb("stats", [P, 2, CT, 6])
        mv = sb("mv", [P, 2, CT, 2])
        var_eps = sb("var_eps", [P, 2, CT])
        std = sb("std", [P, 2, CT])
        tmp = sb("tmp", [P, 2, CT])
        xn = sb("xn", [P, 2, CT, D])
        xt_a = sb("xt_a", [P, 2, CHUNK])
        xt_b = sb("xt_b", [DB + 1, 2, CHUNK])
        qk = sb("qk", [P, 2, 3, CHUNK])
        q_feat = sb("q_feat", [P, PAIRS, S])
        k_feat = sb("k_feat", [P, 2, H * M_FEAT])
        v_ext = sb("v_ext", [P, 2, CT, H, V1])
        context = sb("context", [P, PAIRS, HH * V1])
        inv = sb("inv", [P, 2, H])
        weights, ones, halved, chain, inv_done = (new_sem("ra_" + n) for n in
                                                  ("weights", "ones", "halved", "chain", "inv_done"))
        ring_full, ring_act, ring_dve = ([new_sem(f"ra_{n}{i}") for i in range(SLOTS)]
                                         for n in ("ring_full", "ring_act", "ring_dve"))
        var, ln_std, normed = ([new_sem(f"ra_{n}{u}") for u in range(2)] for n in ("var", "std", "normed"))
        context_full, context_ready, accumulated = (new_sem("ra_" + n) for n in
                                                    ("context_full", "context_ready", "accumulated"))
        out_full = [new_sem(f"ra_out_full{i}") for i in range(2)]
        out_free = [new_sem(f"ra_out_free{i}") for i in range(2)]
        block = ctx.enter_context(nc.Block())

        UNITS = ([("xa", 0, "act"), ("xb", 0, "act")] + [("qk", r, "act") for r in range(3)]
                 + [("v", i, "act") for i in range(2)] + [("qf", p, "dve") for p in range(PAIRS)]
                 + [("kf", i, "dve") for i in range(2 * CT)])
        assert 2 * len(UNITS) % SLOTS == 0
        PER_BODY = 2 * len(UNITS) // SLOTS

        def readers(eng, n_last):
            return [sum(1 for n in range(n_last) if n % SLOTS == i and UNITS[n % len(UNITS)][2] == eng)
                    for i in range(SLOTS)]

        TOTAL = {eng: readers(eng, 2 * len(UNITS)) for eng in ("act", "dve")}
        ring_free = {"act": ring_act, "dve": ring_dve}

        def at(kind, i, u):
            return u * len(UNITS) + [x[:2] for x in UNITS].index((kind, i))

        def full(b, n):
            return ring_full[n % SLOTS], PER_BODY * b + n // SLOTS + 1

        def left(b, n):
            eng = UNITS[n % len(UNITS)][2]
            return ring_free[eng][n % SLOTS], TOTAL[eng][n % SLOTS] * b + readers(eng, n + 1)[n % SLOTS]

        def wait_left(eng, b, numbers):
            newest = {(UNITS[n % len(UNITS)][2], n % SLOTS): n for n in sorted(numbers)}
            for n in newest.values():
                eng.wait_ge(*left(b, n))

        @block.sync
        def _(sp):
            for dst, src in ((w_a[:], a["w1_qk"][0:P]), (w_b[:], a["w1_qk"][P:D]), (wv_a[:], a["w1_v"][0:P]),
                             (wv_b[:], a["w1_v"][P:D + 1]), (bias[:], a["b1_qk"]), (feat_a[:], a["feat_a"]),
                             (feat_b[:], a["feat_b"])):
                sp.dma_start(dst, src).then_inc(weights, 16)

        @block.gpsimd
        def _(pool):
            nc.gpsimd.memset(context[:], 0.0).then_inc(ones, 1)
            pool.wait_ge(ones, 1)
            nc.gpsimd.memset(v_ext[:, :, :, :, HD:V1], 1.0).then_inc(ones, 1)

        @block.vector
        def _(dve):
            nc.vector.memset(xt_b[DB:DB + 1, :, :], 1.0).then_inc(halved, 1)
            dve.wait_ge(weights, 112)
            nc.vector.tensor_scalar(half_bias[:], bias[:], NORM, None, ALU.mult).then_inc(halved, 1)
            dve.wait_ge(ones, 2)

            def features(b, n, dst):
                dve.wait_ge(*full(b, n))
                nc.vector.tensor_scalar(dst, ps[:, n % SLOTS, 0:dst.shape[-1]], 0.0, KERNEL_EPS, ALU.max, ALU.add
                                        ).then_inc(ring_dve[n % SLOTS], 1)

            with dve.Fori(0, B) as b:
                link = Chain(dve, chain, 2 * 7, b)
                for u in range(2):
                    tiles = [h[:, b * TB + (u * CT + j), :] for j in range(CT)]
                    layer_norm_stats(nc, dve, link, tiles, stats[:, u], mv[:, u], var_eps[:, u], var[u])
                    dve.wait_ge(ln_std[u], b + 1)
                    layer_norm_apply(nc, link, tiles, xn[:, u], mv[:, u], var_eps[:, u], std[:, u],
                                     tmp[:, u]).then_inc(normed[u], 1)
                    for i in range(2):
                        dve.wait_ge(out_full[i], TB // 2 * b)
                    for p in range(PAIRS):
                        features(b, at("qf", p, u), q_feat[:, p, u * CHUNK:(u + 1) * CHUNK])
                    for j in range(CT):
                        n_before = 2 * u * CT // 2 + j - 1
                        dve.wait_ge(accumulated, TB * b + max(n_before, 0))
                        features(b, at("kf", 2 * j, u), k_feat[:, j % 2, 0:FA])
                        features(b, at("kf", 2 * j + 1, u), k_feat[:, j % 2, FA:])
                dve.wait_ge(accumulated, TB * (b + 1))
                for bank in range(2):
                    for lo in range(2):
                        part = slice(lo * M_FEAT, (lo + 1) * M_FEAT)
                        for p in range(PAIRS // 2):
                            col = (2 * p + lo) * V1
                            last = nc.vector.tensor_copy(
                                context[part, bank * PAIRS // 2 + p, col:col + V1],
                                ps[part, CTX + bank, p * HH * V1 + col:p * HH * V1 + col + V1])
                last.then_inc(context_ready, 1)
                for t in range(TB):
                    i = t % 2
                    dve.wait_ge(out_full[i], TB // 2 * b + t // 2 + 1)
                    heads = ps[:, OUT + i, 0:H * V1].rearrange("p (h v) -> p h v", v=V1)
                    nc.vector.reciprocal(inv[:, i, :], heads[:, :, HD]).then_inc(inv_done, 1)
                    dve.wait_ge(inv_done, TB * b + t + 1)
                    nc.vector.tensor_tensor(attn[:, b * TB + t, :].rearrange("p (h d) -> p h d", d=HD),
                                            heads[:, :, 0:HD], inv[:, i, :].unsqueeze(2).to_broadcast([P, H, HD]),
                                            ALU.mult).then_inc(out_free[i], 1)

        @block.scalar
        def _(act):
            act.wait_ge(halved, 2)
            act.wait_ge(ones, 2)
            with act.Fori(0, B) as b:
                for u in range(2):
                    act.wait_ge(var[u], b + 1)
                    nc.scalar.activation(std[:, u], var_eps[:, u], ACT.Sqrt).then_inc(ln_std[u], 1)
                    for n, (kind, i, eng) in enumerate(UNITS):
                        if eng != "act":
                            continue
                        n += u * len(UNITS)
                        slot = n % SLOTS
                        act.wait_ge(*full(b, n))
                        if kind == "xa":
                            ins = nc.scalar.copy(xt_a[:, u, :], ps[:, slot, :])
                        elif kind == "xb":
                            ins = nc.scalar.copy(xt_b[0:DB, u, :], ps[0:DB, slot, :])
                        elif kind == "qk":
                            ins = nc.scalar.activation(qk[:, u, i, :], ps[:, slot, :], ACT.Identity,
                                                       bias=half_bias[:, i:i + 1], scale=NORM)
                        else:
                            ins = nc.scalar.copy(v_ext[:, u, 2 * i:2 * i + 2, :, 0:HD],
                                                 ps[:, slot, 0:2 * D].rearrange("p (t h d) -> p t h d", t=2, d=HD))
                        ins.then_inc(ring_act[slot], 1)

        @block.tensor
        def _(pe):
            pe.wait_ge(weights, 112)
            pe.wait_ge(halved, 2)

            def slot_left(b, n):
                slot = n % SLOTS
                for eng in ("act", "dve"):
                    count = readers(eng, n)[slot]
                    if n >= SLOTS:
                        if UNITS[(n - SLOTS) % len(UNITS)][2] == eng:
                            pe.wait_ge(ring_free[eng][slot], TOTAL[eng][slot] * b + count)
                    else:
                        pe.wait_ge(ring_free[eng][slot], TOTAL[eng][slot] * b)

            def unit(b, u, kind, i):
                n = at(kind, i, u)
                slot = n % SLOTS
                if kind == "xa":
                    slot_left(b, n)
                    slot_left(b, n + 1)
                elif kind != "xb":
                    slot_left(b, n)
                if kind == "xa":
                    for j in range(CT):
                        last = nc.tensor.transpose(ps[:, slot, j * P:(j + 1) * P], xn[:, u, j, 0:P], s.ident[:])
                elif kind == "xb":
                    for j in range(CT):
                        last = nc.tensor.transpose(ps[0:DB, slot, j * P:(j + 1) * P], xn[:, u, j, P:D], s.ident[:])
                elif kind == "qk":
                    nc.tensor.matmul(ps[:, slot, :], w_a[:, i, :], xt_a[:, u, :], start=True, stop=False)
                    last = nc.tensor.matmul(ps[:, slot, :], w_b[:, i, :], xt_b[0:DB, u, :], start=False, stop=True)
                elif kind == "v":
                    for j in range(2):
                        toks = slice((2 * i + j) * P, (2 * i + j + 1) * P)
                        dst = ps[:, slot, j * D:(j + 1) * D]
                        nc.tensor.matmul(dst, xt_a[:, u, toks], wv_a[:], start=True, stop=False)
                        last = nc.tensor.matmul(dst, xt_b[:, u, toks], wv_b[:], start=False, stop=True)
                elif kind == "qf":
                    if i < PA:
                        last = nc.tensor.matmul(ps[:, slot, :], feat_a[:, i * P:(i + 1) * P], qk[:, u, 0, :],
                                                start=True, stop=True)
                    else:
                        last = nc.tensor.matmul(ps[:, slot, :], feat_b[:, 0, (i - PA) * P:(i - PA + 1) * P],
                                                qk[:, u, 2, :], start=True, stop=True)
                else:
                    toks = slice(i // 2 * P, (i // 2 + 1) * P)
                    if i % 2 == 0:
                        last = nc.tensor.matmul(ps[:, slot, 0:FA], qk[:, u, 1, toks], feat_a[:], start=True, stop=True)
                    else:
                        last = nc.tensor.matmul(ps[:, slot, 0:FB], qk[:, u, 2, toks], feat_b[:, 1, :],
                                                start=True, stop=True)
                last.then_inc(ring_full[slot], 1)

            def accumulate(b, u, j):
                t = u * CT + j
                needed = [at("kf", 2 * j, u), at("kf", 2 * j + 1, u)]
                if j == 0:
                    needed += [at("v", 0, u), at("v", 1, u)]
                wait_left(pe, b, needed)
                if t == 0:
                    pe.wait_ge(context_ready, b)
                for p in range(PAIRS):
                    bank, col = p // (PAIRS // 2), p % (PAIRS // 2) * HH * V1
                    heads = slice(bank * HH, (bank + 1) * HH)
                    last = nc.tensor.matmul(ps[:, CTX + bank, col:col + HH * V1], k_feat[:, j % 2, p * P:(p + 1) * P],
                                            v_ext[:, u, j, heads, :].rearrange("p h v -> p (h v)"),
                                            start=(t == 0 and col == 0), stop=(t == TB - 1), skip_group_check=True)
                last.then_inc(accumulated, 1)

            with pe.Fori(0, B) as b:
                for u in range(2):
                    pe.wait_ge(normed[u], b + 1)
                    unit(b, u, "xa", 0)
                    unit(b, u, "xb", 0)
                    wait_left(pe, b, [at("xa", 0, u), at("xb", 0, u)])
                    for i in range(3):
                        unit(b, u, "qk", i)
                    for i in range(2):
                        unit(b, u, "v", i)
                    wait_left(pe, b, [at("qk", i, u) for i in range(3)])
                    for i in range(PAIRS):
                        unit(b, u, "qf", i)
                    unit(b, u, "kf", 0)
                    unit(b, u, "kf", 1)
                    for j in range(CT):
                        if j + 1 < CT:
                            unit(b, u, "kf", 2 * j + 2)
                            unit(b, u, "kf", 2 * j + 3)
                        accumulate(b, u, j)
                pe.wait_ge(context_ready, b + 1)
                wait_left(pe, b, [at("qf", p, u) for p in range(PAIRS) for u in range(2)])
                for t in range(TB):
                    i = t % 2
                    pe.wait_ge(out_free[i], TB // 2 * b + t // 2)
                    for p in range(PAIRS):
                        bank = p // (PAIRS // 2)
                        last = nc.tensor.matmul(ps[:, OUT + i, bank * HH * V1:(bank + 1) * HH * V1],
                                                q_feat[:, p, t * P:(t + 1) * P], context[:, p, :],
                                                start=(p % (PAIRS // 2) == 0), stop=(p % (PAIRS // 2) == PAIRS // 2 - 1))
                    last.then_inc(out_full[i], 1)


class Stores:
    pass


def tower(nc, a, out):
    with ExitStack() as ctx:
        def sb(name, shape, dt=F32):
            return ctx.enter_context(nc.sbuf_tensor(name, shape, dt))

        def scratch(name, shape, dt=F32):
            return nc.dram_tensor(name, shape, dt, kind="Internal").ap()

        s = Stores()
        s.psum = ctx.enter_context(nc.psum_tensor("psum", [P, 8, 512], F32))
        s.h = sb("h", [P, NT, D])
        s.attn = sb("attn", [P, NT, D])
        s.ident = sb("ident", [P, P])
        s.logits = sb("logits", [P, NT, E])
        s.gate = sb("gate", [P, 2, NT])
        s.place = sb("place", [P, 2 * NT], U32)
        s.owner = sb("owner", [P, blocks_of(2) + NT], I32)
        s.qk_parts = scratch("qk_parts", [2, PARTS, B * D, S], BF16)
        rows = (blocks_of(1) * P, (blocks_of(2) + NT) * P)
        s.x_rows = [scratch(f"x_rows{i}", [n, D]) for i, n in enumerate(rows)]
        y_rows = [scratch(f"y_rows{i}", [n, D]) for i, n in enumerate(rows)]
        with nc.sbuf_tensor("v_nat", [P, NT, D], F32) as s.v_nat:
            embed_and_project(nc, a, s)
            softmax_attention(nc, s)
        for layer, k_top in enumerate((1, 2)):
            if layer == 1:
                relu_attention(nc, a, s)
            close_attention(nc, a, s, layer)
            route(nc, a, s, layer, k_top, s.x_rows[layer])
            experts(nc, a, s, layer, k_top, s.x_rows[layer], y_rows[layer])
            mix_experts(nc, a, s, layer, k_top, y_rows[layer])
        store_out(nc, s, out)


def store_out(nc, s, out):
    with nc.semaphore("out_stored") as stored, nc.Block() as block:
        @block.sync
        def _(sp):
            sp.dma_start(out.rearrange("(t p) d -> p t d", p=P), s.h[:]).then_inc(stored, 16)
            sp.wait_ge(stored, 16)


def _layouts(x, L0_tok_weight, L0_attn_W_qkv, L0_attn_b_qkv, L0_attn_W_out, L0_attn_b_out, L0_ffn_router_w,
             L0_ffn_router_b, L0_ffn_w1, L0_ffn_w2, L0_ffn_w3, L1_attn_w_qkv, L1_attn_b_qkv, L1_attn_w_proj,
             L1_attn_b_proj, L1_attn_projection, L1_ffn_w_router, L1_ffn_expert_bias, L1_ffn_Wg, L1_ffn_Wu,
             L1_ffn_Wd, L1_ffn_sg, L1_ffn_su, L1_ffn_sd):
    f = np.float32

    def rows_of(w, n):
        full = np.zeros((n * P, w.shape[-1]), f)
        full[:w.shape[0]] = w
        return np.ascontiguousarray(full.reshape(n, P, -1).transpose(1, 0, 2))

    blocks = np.zeros((3, D, D), f)
    for hd in range(H):
        at = slice(hd * HD, (hd + 1) * HD)
        for k in range(3):
            blocks[k, at, at] = L0_attn_W_qkv[hd, :, k * HD:(k + 1) * HD]
    bq, bk, bv = (np.asarray(L0_attn_b_qkv)[:, k * HD:(k + 1) * HD].reshape(D) for k in range(3))
    q1, k1, v1 = (np.asarray(L1_attn_w_qkv)[k * D:(k + 1) * D].T for k in range(3))
    bq1, bk1, bv1 = (np.asarray(L1_attn_b_qkv)[k * D:(k + 1) * D] for k in range(3))
    feat = np.zeros((H, HD, H, M_FEAT), f)
    for hd in range(H):
        feat[hd, :, hd, :] = np.asarray(L1_attn_projection).T
    feat = feat.reshape(D, H * M_FEAT)
    feat_b = np.zeros((2, P, (H - P // HD) * M_FEAT), f)
    feat_b[0, :DB] = feat[P:, P // HD * M_FEAT:]
    feat_b[1, DB:] = feat[P:, P // HD * M_FEAT:]
    wg = np.concatenate([L1_ffn_Wg, np.asarray(L1_ffn_sg)[None]]).transpose(2, 0, 1)
    wu = np.concatenate([L1_ffn_Wu, np.asarray(L1_ffn_su)[None]]).transpose(2, 0, 1)
    wd = np.concatenate([L1_ffn_Wd, np.asarray(L1_ffn_sd)[None]]).transpose(0, 2, 1)

    def cat(*rows):
        return np.ascontiguousarray(np.concatenate([np.asarray(r).reshape(-1, np.shape(rows[0])[-1]) for r in rows]))

    return {
        "ids": np.ascontiguousarray(np.asarray(x).reshape(NT, P).T),
        "table": np.ascontiguousarray(np.asarray(L0_tok_weight).T),
        "w0_qk_a": np.ascontiguousarray(blocks[:2, :P, :P].transpose(1, 0, 2)),
        "w0_qk_b": np.ascontiguousarray(np.concatenate([blocks[0, P:, P:], blocks[1, P:, P:]], 1)),
        "w0_v": cat(blocks[2], bv),
        "b0_qk": np.ascontiguousarray(np.stack([bq[:P], bk[:P], np.concatenate([bq[P:], bk[P:]])], 1)),
        "w0_out": cat(L0_attn_W_out, L0_attn_b_out),
        "w0_router": cat(L0_ffn_router_w, L0_ffn_router_b),
        "e0_up_a": np.ascontiguousarray(np.stack([np.asarray(L0_ffn_w1)[:, :P], np.asarray(L0_ffn_w2)[:, :P]]).transpose(2, 0, 1, 3)),
        "e0_up_b": np.ascontiguousarray(np.stack([np.asarray(L0_ffn_w1)[:, P:], np.asarray(L0_ffn_w2)[:, P:]]).transpose(2, 0, 1, 3)),
        "e0_down": np.ascontiguousarray(np.asarray(L0_ffn_w3).reshape(E, F0 // P, P, D).transpose(2, 0, 1, 3)),
        "w1_qk": np.ascontiguousarray(np.stack([q1[:, :P], k1[:, :P], np.concatenate([q1[:, P:], k1[:, P:]], 1)], 1)),
        "w1_v": cat(v1, bv1),
        "b1_qk": np.ascontiguousarray(np.stack([bq1[:P], bk1[:P], np.concatenate([bq1[P:], bk1[P:]])], 1)),
        "feat_a": np.ascontiguousarray(feat[:P, :P // HD * M_FEAT]),
        "feat_b": np.ascontiguousarray(feat_b.transpose(1, 0, 2)),
        "w1_out": cat(np.asarray(L1_attn_w_proj).T, L1_attn_b_proj),
        "w1_router": np.ascontiguousarray(np.asarray(L1_ffn_w_router).T),
        "b1_expert": np.ascontiguousarray(np.broadcast_to(np.asarray(L1_ffn_expert_bias), (P, E))),
        "e1_up_a": np.ascontiguousarray(np.stack([wg[:P], wu[:P]], 1)),
        "e1_up_b": np.ascontiguousarray(np.stack([wg[P:], wu[P:]], 1)),
        "e1_down": np.ascontiguousarray(wd.reshape(E + 1, F1 // P, P, D).transpose(2, 0, 1, 3)),
    }


def kernel(**inputs):
    import concourse.bacc as _bacc
    from concourse.bass_utils import run_bass_kernel_spmd as _run

    nc = _bacc.Bacc("TRN2", target_bir_lowering=False, num_devices=1)
    arrays = _layouts(**{k: np.asarray(v) for k, v in inputs.items()})
    a = {n: nc.dram_tensor(n, v.shape, mybir.dt.from_np(v.dtype), kind="ExternalInput").ap()
         for n, v in arrays.items()}
    out = nc.dram_tensor("out", [T, D], F32, kind="ExternalOutput").ap()
    tower(nc, a, out)
    r = _run(nc, [arrays], core_ids=[0])
    return r.results[0]["out"].reshape(B, S, D)
```

```python
from contextlib import ExitStack, contextmanager

import numpy as np
import concourse.bass as bass
from concourse import mybir

F32 = mybir.dt.float32
BF16 = mybir.dt.bfloat16
I32 = mybir.dt.int32
U32 = mybir.dt.uint32
ALU = mybir.AluOpType
ACT = mybir.ActivationFunctionType
AX = mybir.AxisListType

P = 128
D = 192
DB = D - P
B, S = 4, 1024
T = B * S
NT = T // P
CT = 4
CHUNK = CT * P
TB = S // P
H, HD = 12, 16
GH = 4
NG = H // GH
GD = GH * HD
E = 8
EPS = 1e-5
SCALE0 = float(D) ** -0.5
PARTS = 3
Q_STACK = (0, 0, 1, 1, 0, 2)
K_STACK = (0, 1, 0, 1, 2, 0)
SK = len(Q_STACK) * HD
M_FEAT = 64
KERNEL_EPS = 0.001
F0, F1 = 512, 384
LEAD = NT // 2
START = 1


@contextmanager
def semaphores(nc):
    taken = []

    def new_sem(name, start=START):
        taken.append(nc.alloc_semaphore(name))
        if start:
            nc.sync.sem_inc(taken[-1], start)
        return taken[-1]
    yield new_sem
    nc.clear_and_free_semaphores(taken)
    nc.all_engine_barrier()


class Chain:

    def __init__(self, eng, sem, per_turn=0, turn=0):
        self.eng, self.sem, self.base, self.n, self.per_turn = eng, sem, turn * per_turn, 0, per_turn

    def __call__(self, ins):
        self.n += 1
        ins.then_inc(self.sem, 1)
        self.eng.wait_ge(self.sem, START + self.base + self.n)


def sems(new_sem, names):
    return {n: new_sem(n) for n in names.split()}


def layer_norm_stats(nc, dve, link, tiles, stats, mv, var_eps, var_ready):
    dve.nop(nofuse=True)
    for j, tile in enumerate(tiles):
        last = nc.vector.bn_stats(stats[:, j, :], tile)
    link(last)
    dve.nop(nofuse=True)
    for j in range(len(tiles)):
        last = nc.vector.bn_aggr(mv[:, j, :], stats[:, j, :])
    link(last)
    nc.vector.tensor_scalar(var_eps, mv[:, :, 1], EPS, None, ALU.add).then_inc(var_ready, 1)


def layer_norm_apply(nc, link, tiles, normed, mv, var_eps, std, tmp):
    link(nc.vector.reciprocal(tmp, std))
    link(nc.vector.tensor_tensor(tmp, tmp, var_eps, ALU.mult))
    link(nc.vector.tensor_tensor(tmp, tmp, std, ALU.add))
    link(nc.vector.tensor_scalar(tmp, tmp, 0.5, None, ALU.mult))
    link(nc.vector.reciprocal(tmp, tmp))
    for j, tile in enumerate(tiles):
        last = nc.vector.tensor_scalar(normed[:, j, :], tile, mv[:, j, 0:1], tmp[:, j:j + 1],
                                       ALU.subtract, ALU.mult)
    return last


def pipeline(eng, turns, start, step, finish):
    start()
    step((0, 0), None, (1, 0))
    with eng.Fori(0, turns - 1) as i:
        step((1, i), (0, i), (0, i + 1))
        step((0, i + 1), (1, i), (1, i + 1))
    step((1, turns - 1), (0, turns - 1), None)
    finish()


def embed_and_project(nc, a, s):
    with ExitStack() as ctx:
        new_sem = ctx.enter_context(semaphores(nc))

        def sb(name, shape, dt=F32):
            return ctx.enter_context(nc.sbuf_tensor("ep_" + name, shape, dt))

        h, v_nat, ps = s.h, s.v_nat, s.psum
        ids = sb("ids", [P, NT], I32)
        w_a = sb("w_a", [P, 2, P])
        w_b = sb("w_b", [DB, P])
        wv_a = sb("wv_a", [P, D])
        wv_b = sb("wv_b", [DB + 1, D])
        bias = sb("bias", [P, 3])
        stats = sb("stats", [P, 2, CT, 6])
        mv = sb("mv", [P, 2, CT, 2])
        var_eps = sb("var_eps", [P, 2, CT])
        std = sb("std", [P, 2, CT])
        tmp = sb("tmp", [P, 2, CT])
        xn = sb("xn", [P, 2, CT, D])
        xt_a = sb("xt_a", [P, 2, CHUNK])
        xt_b = sb("xt_b", [DB + 1, 2, CHUNK])
        full = sb("full", [P, 2, 3, CHUNK])
        rest = sb("rest", [P, 2, 3, CHUNK])
        parts = sb("parts", [P, 2, 3, PARTS, CHUNK], BF16)
        m = sems(new_sem, "ep_ids ep_weights ep_ones ep_ident ep_qk_ps ep_v_left ep_link ep_pool_link ep_rest")
        two = {n: [new_sem(f"ep_{n}{u}") for u in range(2)] for n in
               ("var", "std", "xn", "xt_ps", "xt", "v_ps", "high", "middle", "low", "sent")}
        gathered = [new_sem(f"ep_gathered{t}", start=0) for t in range(TB)]
        nc.all_engine_barrier()
        block = ctx.enter_context(nc.Block())
        PS_XA, PS_XB, PS_QK, PS_V = 0, 1, 2, 5

        @block.gpsimd
        def _(pool):
            nc.gpsimd.memset(s.ident[:], 0.0).then_inc(m["ep_pool_link"], 1)
            pool.wait_ge(m["ep_pool_link"], START + 1)
            nc.gpsimd.affine_select(out=s.ident[:], in_=s.ident[:], compare_op=ALU.not_equal, fill=1.0, base=0,
                                    pattern=[[-1, P]], channel_multiplier=1).then_inc(m["ep_ident"], 1)
            pool.wait_ge(m["ep_ids"], START + 16)
            for t in range(NT):
                if t >= TB:
                    pool.wait_ge(gathered[t % TB], 16 * (t // TB))
                pool.indirect_dma_start(out=h[:, t, :], out_offset=None, in_=a["table"],
                                        in_offset=bass.IndirectOffsetOnAxis(ap=ids[:, t:t + 1], axis=0)
                                        ).then_inc(gathered[t % TB], 16)
            with pool.Fori(0, B) as b:
                for u in range(2):
                    for r in range(3):
                        pool.wait_ge(two["middle"][u], START + 3 * b + r + 1)
                        nc.gpsimd.tensor_tensor(parts[:, u, r, 2, :], rest[:, u, r, :], parts[:, u, r, 1, :],
                                                ALU.subtract).then_inc(two["low"][u], 1)

        @block.sync
        def _(sp):
            sp.dma_start(ids[:], a["ids"]).then_inc(m["ep_ids"], 16)
            for dst, src in ((w_a[:], a["w0_qk_a"]), (w_b[:], a["w0_qk_b"]), (wv_a[:], a["w0_v"][0:P, :]),
                             (wv_b[:], a["w0_v"][P:D + 1, :]), (bias[:], a["b0_qk"])):
                sp.dma_start(dst, src).then_inc(m["ep_weights"], 16)
            with sp.Fori(0, B) as b:
                for u in range(2):
                    sp.wait_ge(two["low"][u], START + 3 * (b + 1))
                    cols = slice(u * CHUNK, (u + 1) * CHUNK)
                    for r, (src, which, row) in enumerate(((slice(0, P), 0, 0), (slice(0, P), 1, 0),
                                                           (slice(0, DB), 0, P), (slice(DB, P), 1, P))):
                        n = src.stop - src.start
                        dst = s.qk_parts[which, :, bass.ds(b * D + row, n), cols]
                        sp.dma_start(dst.rearrange("c r t -> r c t"),
                                     parts[src, u, min(r, 2), :, :]).then_inc(two["sent"][u], 16)
            for u in range(2):
                sp.wait_ge(two["sent"][u], START + 4 * 16 * B)

        @block.vector
        def _(dve):
            nc.vector.memset(xt_b[DB:DB + 1, :, :], 1.0).then_inc(m["ep_ones"], 1)

            def tiles_of(u, k):
                return [h[:, k * TB + (u * CT + j), :] for j in range(CT)]

            def chain(u, k):
                return Chain(dve, m["ep_link"], 7, 2 * k + u)

            def statistics(u, k, link):
                for j in range(CT):
                    dve.wait_ge(gathered[u * CT + j], 16 * (k + 1))
                layer_norm_stats(nc, dve, link, tiles_of(u, k), stats[:, u], mv[:, u], var_eps[:, u], two["var"][u])

            def normalise(u, k, link):
                dve.wait_ge(two["std"][u], START + k + 1)
                dve.wait_ge(two["xt_ps"][u], START + k)
                layer_norm_apply(nc, link, tiles_of(u, k), xn[:, u], mv[:, u], var_eps[:, u], std[:, u],
                                 tmp[:, u]).then_inc(two["xn"][u], 1)

            def split(u, k, r):
                dve.wait_ge(two["high"][u], START + 3 * k + r + 1)
                dve.wait_ge(two["low"][u], START + 3 * k)
                nc.vector.tensor_tensor(rest[:, u, r, :], full[:, u, r, :], parts[:, u, r, 0, :],
                                        ALU.subtract).then_inc(m["ep_rest"], 1)
                dve.wait_ge(m["ep_rest"], START + 3 * (2 * k + u) + r + 1)
                nc.vector.tensor_copy(parts[:, u, r, 1, :], rest[:, u, r, :]).then_inc(two["middle"][u], 1)

            def start():
                link = chain(0, 0)
                statistics(0, 0, link)
                normalise(0, 0, link)

            def step(this, prev, nxt):
                u, k = this
                if nxt:
                    link = chain(*nxt)
                    statistics(*nxt, link)
                split(u, k, 0)
                if nxt:
                    normalise(*nxt, link)
                for half in range(2):
                    dve.wait_ge(two["v_ps"][u], START + 2 * k + half + 1)
                    nc.vector.tensor_copy(v_nat[:, bass.ds(k * TB + u * CT + 2 * half, 2), :],
                                          ps[:, PS_V + half, 0:2 * D].rearrange("p (t d) -> p t d", d=D)
                                          ).then_inc(m["ep_v_left"], 1)
                split(u, k, 1)
                split(u, k, 2)
            pipeline(dve, B, start, step, lambda: None)

        @block.scalar
        def _(act):
            act.wait_ge(m["ep_weights"], START + 80)
            act.wait_ge(m["ep_ones"], START + 1)

            def root(u, k):
                act.wait_ge(two["var"][u], START + k + 1)
                nc.scalar.activation(std[:, u], var_eps[:, u], ACT.Sqrt).then_inc(two["std"][u], 1)

            def copy_xt(u, k):
                act.wait_ge(two["xt_ps"][u], START + k + 1)
                act.wait_ge(two["v_ps"][u], START + 2 * k)
                nc.scalar.copy(xt_a[:, u, :], ps[:, PS_XA, :]).then_inc(two["xt"][u], 1)
                nc.scalar.copy(xt_b[0:DB, u, :], ps[0:DB, PS_XB, :]).then_inc(two["xt"][u], 1)

            def start():
                root(0, 0)
                copy_xt(0, 0)

            def step(this, prev, nxt):
                u, k = this
                for r in range(3):
                    act.wait_ge(m["ep_qk_ps"], START + 3 * (2 * k + u) + r + 1)
                    act.wait_ge(two["middle"][u], START + 3 * k)
                    act.wait_ge(two["sent"][u], START + 64 * k)
                    nc.scalar.activation(full[:, u, r, :], ps[:, PS_QK + r, :], ACT.Identity, bias=bias[:, r:r + 1])
                    nc.scalar.activation(parts[:, u, r, 0, :], ps[:, PS_QK + r, :], ACT.Identity,
                                         bias=bias[:, r:r + 1]).then_inc(two["high"][u], 1)
                    if nxt and r == 0:
                        root(*nxt)
                if nxt:
                    copy_xt(*nxt)
            pipeline(act, B, start, step, lambda: None)

        @block.tensor
        def _(pe):
            pe.wait_ge(m["ep_ident"], START + 1)
            pe.wait_ge(m["ep_weights"], START + 80)
            pe.wait_ge(m["ep_ones"], START + 1)

            def transpose(u, k, prev):
                pe.wait_ge(two["xn"][u], START + k + 1)
                if prev:
                    pe.wait_ge(two["xt"][prev[0]], START + 2 * (prev[1] + 1))
                for j in range(CT):
                    nc.tensor.transpose(ps[:, PS_XA, j * P:(j + 1) * P], xn[:, u, j, 0:P], s.ident[:])
                    last = nc.tensor.transpose(ps[0:DB, PS_XB, j * P:(j + 1) * P], xn[:, u, j, P:D], s.ident[:])
                last.then_inc(two["xt_ps"][u], 1)

            def step(this, prev, nxt):
                u, k = this
                pe.wait_ge(two["xt"][u], START + 2 * (k + 1))
                for r in range(3):
                    if prev:
                        pe.wait_ge(two["high"][prev[0]], START + 3 * prev[1] + r + 1)
                    if r < 2:
                        last = nc.tensor.matmul(ps[:, PS_QK + r, :], w_a[:, r, :], xt_a[:, u, :], start=True, stop=True)
                    else:
                        last = nc.tensor.matmul(ps[:, PS_QK + r, :], w_b[:], xt_b[0:DB, u, :], start=True, stop=True)
                    last.then_inc(m["ep_qk_ps"], 1)
                for half in range(2):
                    pe.wait_ge(m["ep_v_left"], START + 2 * (2 * k + u))
                    for j in range(2):
                        toks = slice((2 * half + j) * P, (2 * half + j + 1) * P)
                        dst = ps[:, PS_V + half, j * D:(j + 1) * D]
                        nc.tensor.matmul(dst, xt_a[:, u, toks], wv_a[:], start=True, stop=False)
                        last = nc.tensor.matmul(dst, xt_b[:, u, toks], wv_b[:], start=False, stop=True)
                    last.then_inc(two["v_ps"][u], 1)
                if nxt:
                    transpose(*nxt, this)
            pipeline(pe, B, lambda: transpose(0, 0, None), step, lambda: None)


def softmax_attention(nc, s):
    with ExitStack() as ctx:
        new_sem = ctx.enter_context(semaphores(nc))

        def sb(name, shape, dt=F32):
            return ctx.enter_context(nc.sbuf_tensor("sa_" + name, shape, dt))

        ps, v_nat, attn = s.psum, s.v_nat, s.attn
        HALF = 512
        SLOTS = 3
        OUT = 4 + SLOTS
        STEPS = 2 * TB
        W = 32
        IT = HALF // P
        qst = sb("qst", [SK + 1, NG, GH, S], BF16)
        kst = sb("kst", [SK + 1, NG, GH, S], BF16)
        v_ext = sb("v_ext", [P, NG, TB, GH, W])
        probs = sb("probs", [P, 2, GH, HALF])
        out_t = sb("out_t", [P, 2, HALF])
        half_max = sb("half_max", [P, NG, GH, TB, 2])
        row_max = sb("row_max", [P, NG, GH, TB])
        max_rows = sb("max_rows", [HD, NG, 2, P], BF16)
        inv = sb("inv", [P, 2, IT, GH])
        max_dram = nc.dram_tensor("max_rows_dram", [NG, GH * TB, P], BF16, kind="Internal").ap()

        def per_group(name):
            return [new_sem(f"sa_{name}{g}") for g in range(NG)]

        loaded, max_stored, max_loaded, v_ready = map(per_group, ("loaded", "max_stored", "max_loaded", "v_ready"))
        scores_done, exp_done, pv_done, max_done = map(per_group, ("scores_done", "exp_done", "pv_done", "max_done"))
        ring_full = [new_sem(f"sa_ring_full{r}") for r in range(SLOTS)]
        ring_free = [new_sem(f"sa_ring_free{r}") for r in range(SLOTS)]
        out_copied = [new_sem(f"sa_out_copied{r}") for r in range(2)]
        zeros = sb("zeros", [P, D])
        zeroed, zeros_stored = (new_sem("sa_" + n) for n in ("zeroed", "zeros_stored"))
        inv_done, v_init, ones_row = (new_sem("sa_" + n)
                                      for n in ("inv_done", "v_init", "ones_row"))
        LOADS = 2 * len(Q_STACK)
        nc.all_engine_barrier()
        block = ctx.enter_context(nc.Block())

        def max_units(g, first, last):
            return [("max", g, k // (2 * TB), k // 2 % TB, k % 2) for k in range(first, last)]

        UNITS = GH * TB * 2
        AHEAD = 5
        PER = UNITS // STEPS
        before = max_units(0, 0, UNITS) + [("rows", 0, 0), ("rows", 0, 1)] + max_units(1, 0, AHEAD * PER)

        def step_units(g, st, last):
            n1, n2 = g + 1, g + 2
            split, tail = [], []
            if st < STEPS - AHEAD:
                if not (last and n1 >= NG):
                    split = max_units(n1 % NG, (AHEAD + st) * PER, (AHEAD + st + 1) * PER)
            elif not (last and n2 >= NG):
                k = st - (STEPS - AHEAD)
                split = max_units(n2 % NG, k * PER, (k + 1) * PER)
            if st == 1 and g > 0:
                tail.append(("out", g - 1, 1))
            if st == TB + 1:
                tail.append(("out", g, 0))
            if st == STEPS - AHEAD + 1 and not (last and n1 >= NG):
                tail += [("rows", n1 % NG, 0), ("rows", n1 % NG, 1)]
            if st == STEPS - 1 and g == NG - 1:
                tail.append(("out", g, 1))
            return split, tail

        def order(last):
            return [u for g in range(NG) for st in range(STEPS) for part in step_units(g, st, last) for u in part]

        RING0 = len(before)
        RING = len(order(False))
        assert RING % SLOTS == 0
        place = {last: {u: n for n, u in enumerate(order(last))} for last in (False, True)}

        def turns(eng, body):
            with eng.Fori(0, B - 1) as b:
                body(b, False)
            body(B - 1, True)

        def uses(b, n):
            return (RING0 + n) % SLOTS, RING // SLOTS * b + (RING0 + n) // SLOTS

        def load_stacks(sp, b, g):
            for which, (stack, order_) in enumerate(((qst, Q_STACK), (kst, K_STACK))):
                for k, part in enumerate(order_):
                    src = s.qk_parts[which, part, bass.ds(b * D + g * GD, GD), :]
                    sp.dma_start(stack[k * HD:(k + 1) * HD, g, :, :],
                                 src.rearrange("(s r) t -> r s t", r=HD)).then_inc(loaded[g], 16)

        def load_max(sp, g, b):
            sp.dma_start(max_dram[g].rearrange("(u k) t -> k u t", u=2), max_rows[:, g, :, :]).then_inc(max_stored[g], 16)
            sp.wait_ge(max_stored[g], START + 16 * (b + 1))
            sp.dma_start(qst[SK:SK + 1, g, :, :].rearrange("o s t -> o (s t)"),
                         max_dram[g].rearrange("(o k) t -> o (k t)", o=1)).then_inc(max_loaded[g], 16)

        @block.sync
        def _(sp):
            for g in range(NG):
                load_stacks(sp, 0, g)
            for n in (UNITS, UNITS + 1):
                sp.wait_ge(ring_free[n % SLOTS], START + n // SLOTS + 1)
            load_max(sp, 0, 0)
            sp.wait_ge(zeroed, START + 1)
            for x_rows, n in zip(s.x_rows, (blocks_of(1), blocks_of(2))):
                sp.dma_start(x_rows[0:n * P, :].rearrange("(n p) d -> p n d", p=P),
                             zeros[:].unsqueeze(1).to_broadcast([P, n, D])).then_inc(zeros_stored, 16)

            def sequence(b, last):
                for g in range(NG):
                    if not (last and g == NG - 1):
                        n1, b1 = ((g + 1) % NG, b + (g + 1) // NG)
                        for half in range(2):
                            r, k = uses(b, place[last][("rows", n1, half)])
                            sp.wait_ge(ring_free[r], START + k + 1)
                            sp.nop(nofuse=True)
                        load_max(sp, n1, b1)
                    if not last:
                        sp.wait_ge(scores_done[g], START + 2 * STEPS * (b + 1))
                        load_stacks(sp, b + 1, g)
            turns(sp, sequence)
            sp.wait_ge(zeros_stored, START + 32)

        @block.gpsimd
        def _(pool):
            nc.gpsimd.memset(v_ext[:], 0.0).then_inc(v_init, 1)
            pool.wait_ge(v_init, START + 1)
            nc.gpsimd.memset(v_ext[:, :, :, :, HD:HD + 1], 1.0).then_inc(v_init, 1)
            pool.wait_ge(v_init, START + 2)
            nc.gpsimd.memset(kst[SK:SK + 1, :, :, :], 1.0).then_inc(ones_row, 1)
            pool.wait_ge(ones_row, START + 1)
            with pool.Fori(0, B) as b:
                for g in range(NG):
                    pool.wait_ge(pv_done[g], START + STEPS * b)
                    src = v_nat[:, bass.ds(b * TB, TB), g * GD:(g + 1) * GD]
                    nc.gpsimd.tensor_copy(v_ext[:, g, :, :, 0:HD], src.rearrange("p t (s d) -> p t s d", s=GH)
                                          ).then_inc(v_ready[g], 1)

        @block.vector
        def _(dve):
            def consume(b, n, unit, r, k):
                kind, g = unit[0], unit[1]
                slot = ps[:, 4 + r, :]
                dve.wait_ge(ring_full[r], START + k + 1)
                if kind == "max":
                    hd, qt, half = unit[2:]
                    nc.vector.tensor_reduce(half_max[:, g, hd, qt, half:half + 1], slot, AX.X,
                                            ALU.max).then_inc(ring_free[r], 1)
                elif kind == "rows":
                    nc.vector.tensor_scalar(max_rows[:, g, unit[2], :], slot[0:HD, 0:P], -1.0, None,
                                            ALU.mult).then_inc(ring_free[r], 1)
                else:
                    half = unit[2]
                    heads = slot.rearrange("p (i s w) -> p i s w", s=GH, w=W)
                    nc.vector.reciprocal(inv[:, half], heads[:, :, :, HD]).then_inc(inv_done, 1)
                    dve.wait_ge(inv_done, START + b * 2 * NG + 2 * g + half + 1)
                    dst = attn[:, bass.ds(b * TB + half * IT, IT), g * GD:(g + 1) * GD]
                    nc.vector.tensor_tensor(dst.rearrange("p i (s d) -> p i s d", s=GH), heads[:, :, :, 0:HD],
                                            inv[:, half].unsqueeze(3).to_broadcast([P, IT, GH, HD]),
                                            ALU.mult).then_inc(ring_free[r], 1)

            def combine(g, turn, n):
                for i in range(n - SLOTS + 1, n + 1):
                    r, k = turn(i)
                    dve.wait_ge(ring_free[r], START + k + 1)
                nc.vector.tensor_tensor(row_max[:, g], half_max[:, g, :, :, 0], half_max[:, g, :, :, 1],
                                        ALU.max).then_inc(max_done[g], 1)

            nc.vector.memset(zeros[:], 0.0).then_inc(zeroed, 1)
            for n, unit in enumerate(before):
                if unit[0] == "rows" and unit[2] == 0:
                    combine(unit[1], lambda i: (i % SLOTS, i // SLOTS), n - 1)
                consume(0, n, unit, n % SLOTS, n // SLOTS)

            def sequence(b, last):
                units = order(last)
                newest = {unit[1]: max(i for i, u in enumerate(units[:n]) if u[:2] == ("max", unit[1]))
                          for n, unit in enumerate(units) if unit[0] == "rows"}
                combine_at = {g: min(last_max + SLOTS, place[last][("rows", g, 0)]) for g, last_max in newest.items()}
                for n, unit in enumerate(units):
                    r, k = uses(b, n)
                    for g, last_max in newest.items():
                        if n == combine_at[g]:
                            combine(g, lambda i: uses(b, i), last_max)
                    if unit[0] == "rows":
                        dve.wait_ge(max_stored[unit[1]], START + 16 * (b + 1 if unit[1] == 0 else b))
                    consume(b, n, unit, r, k)
            turns(dve, sequence)

        @block.scalar
        def _(act):
            def exps(b, g, st):
                for pair in range(2):
                    act.wait_ge(scores_done[g], START + 2 * STEPS * b + 2 * st + pair + 1)
                    if pair == 0:
                        if st >= 2:
                            act.wait_ge(pv_done[g], START + STEPS * b + st - 1)
                        elif g > 0:
                            act.wait_ge(pv_done[g - 1], START + STEPS * b + STEPS - 1 + st)
                        else:
                            act.wait_ge(pv_done[NG - 1], START + STEPS * b)
                    nc.scalar.activation(probs[:, st % 2, 2 * pair:2 * pair + 2, :], ps[:, 2 * pair:2 * pair + 2, :],
                                         ACT.Exp, scale=SCALE0).then_inc(exp_done[g], 1)

            def copy_out(b, g, half, last):
                act.wait_ge(pv_done[g], START + STEPS * b + TB * (half + 1))
                k_half = 2 * g + half
                if k_half >= 2:
                    r, k = uses(b, place[last][("out", g - 1, half)])
                else:
                    r, k = uses(b - 1, place[False][("out", NG - 1, half)])
                act.wait_ge(ring_full[r], START + k + 1)
                nc.scalar.copy(out_t[:, half, :], ps[:, OUT, :]).then_inc(out_copied[half], 1)

            def sequence(b, last):
                for g in range(NG):
                    for st in range(STEPS):
                        exps(b, g, st)
                        if st == 0 and g > 0:
                            copy_out(b, g - 1, 1, last)
                        if st == TB:
                            copy_out(b, g, 0, last)
                copy_out(b, NG - 1, 1, last)
            turns(act, sequence)

        @block.tensor
        def _(pe):
            pe.wait_ge(ones_row, START + 1)

            def scores(b, g, st, pair, follows):
                half, kt = st // TB, st % TB
                if pair == 0 and st == 0:
                    pe.wait_ge(loaded[g], START + 16 * LOADS * (b + 1))
                    pe.wait_ge(max_loaded[g], START + 16 * (b + 1))
                if follows is not None:
                    pe.wait_ge(exp_done[follows[0]], START + follows[1] + pair + 1)
                for hd in (2 * pair, 2 * pair + 1):
                    last = nc.tensor.matmul(ps[:, hd, :], kst[:, g, hd, kt * P:(kt + 1) * P],
                                            qst[:, g, hd, half * HALF:(half + 1) * HALF], start=True, stop=True)
                last.then_inc(scores_done[g], 1)

            def produce(b, unit, r, k):
                kind, g = unit[0], unit[1]
                pe.wait_ge(ring_free[r], START + k)
                if kind == "max":
                    hd, qt, half = unit[2:]
                    last = nc.tensor.matmul(ps[:, 4 + r, :], qst[0:SK, g, hd, qt * P:(qt + 1) * P],
                                            kst[0:SK, g, hd, half * 512:(half + 1) * 512], start=True, stop=True)
                elif kind == "rows":
                    heads = row_max[:, g].rearrange("p s t -> p (s t)")
                    last = nc.tensor.transpose(ps[0:HD, 4 + r, 0:P], heads[:, unit[2] * HD:(unit[2] + 1) * HD],
                                               s.ident[:])
                else:
                    half = unit[2]
                    pe.wait_ge(out_copied[half], START + NG * b + g + 1)
                    for i in range(IT):
                        last = nc.tensor.transpose(ps[:, 4 + r, i * P:(i + 1) * P],
                                                   out_t[:, half, i * P:(i + 1) * P], s.ident[:])
                last.then_inc(ring_full[r], 1)

            def times_v(b, g, st):
                half, kt = st // TB, st % TB
                if st == 0:
                    pe.wait_ge(v_ready[g], START + b + 1)
                if kt == 0:
                    pe.wait_ge(out_copied[1 - half], START + NG * b + g + half)
                pe.wait_ge(exp_done[g], START + 2 * STEPS * b + 2 * st + 2)
                for hd in range(GH):
                    last = nc.tensor.matmul(ps[hd * W:(hd + 1) * W, OUT, :], v_ext[:, g, kt, hd, :],
                                            probs[:, st % 2, hd, :], start=(kt == 0), stop=(kt == TB - 1))
                last.then_inc(pv_done[g], 1)

            for n, unit in enumerate(before):
                if unit[0] == "max" and unit[2:] == (0, 0, 0):
                    pe.wait_ge(loaded[unit[1]], START + 16 * LOADS)
                if unit[0] == "rows":
                    pe.wait_ge(max_done[unit[1]], START + 1)
                produce(0, unit, n % SLOTS, n // SLOTS)
            for pair in range(2):
                scores(0, 0, 0, pair, None)

            ORDER = ("scores", "maxima", "scores", "maxima", "maxima", "outputs", "maxima")

            def sequence(b, last):
                n = 0
                for g in range(NG):
                    for st in range(STEPS):
                        split, tail = step_units(g, st, last)
                        final = last and g == NG - 1 and st == STEPS - 1
                        nb, ng, nst = (b, g, st + 1) if st + 1 < STEPS else (b + (g + 1) // NG, (g + 1) % NG, 0)
                        pair, left = 0, list(split)
                        for what in ORDER:
                            if what == "scores":
                                if not final:
                                    scores(nb, ng, nst, pair, (g, 2 * STEPS * b + 2 * st))
                                pair += 1
                            elif what == "outputs":
                                times_v(b, g, st)
                            elif left:
                                unit = left.pop(0)
                                ug = unit[1]
                                if unit[2:] == (0, 0, 0):
                                    pe.wait_ge(loaded[ug], START + 16 * LOADS * ((b if ug > g else b + 1) + 1))
                                produce(b, unit, *uses(b, n))
                                n += 1
                        for unit in tail:
                            if unit[0] == "rows":
                                pe.wait_ge(max_done[unit[1]], START + (b + 1 if unit[1] == 0 else b) + 1)
                            produce(b, unit, *uses(b, n))
                            n += 1
            turns(pe, sequence)


def close_attention(nc, a, s, layer):
    with ExitStack() as ctx:
        new_sem = ctx.enter_context(semaphores(nc))

        def sb(name, shape, dt=F32):
            return ctx.enter_context(nc.sbuf_tensor(f"ca{layer}_" + name, shape, dt))

        h, attn, ps = s.h, s.attn, s.psum
        router = a[f"w{layer}_router"]
        RB = router.shape[0] - P
        wo_a = sb("wo_a", [P, D])
        wo_b = sb("wo_b", [DB + 1, D])
        wr_a = sb("wr_a", [P, E])
        wr_b = sb("wr_b", [RB, E])
        rows = sb("rows", [P, 2, CT, D])
        rows_ta = sb("rows_ta", [P, 2, CHUNK])
        rows_tb = sb("rows_tb", [DB + 1, 2, CHUNK])
        x2 = sb("x2", [P, 2, CT, D])
        x2_ta = sb("x2_ta", [P, 2, CHUNK])
        x2_tb = sb("x2_tb", [DB + 1, 2, CHUNK])
        stats = sb("stats", [P, 2, CT, 6])
        mv = sb("mv", [P, 2, CT, 2])
        var_eps = sb("var_eps", [P, 2, CT])
        std = sb("std", [P, 2, CT])
        tmp = sb("tmp", [P, 2, CT])
        weights, ones, chain = (new_sem(f"ca{layer}_{n}") for n in ("weights", "ones", "chain"))
        two = {n: [new_sem(f"ca{layer}_{n}{u}") for u in range(2)] for n in
               ("rows", "rows_ps", "rows_act", "out_ps", "var", "std", "x2", "x2_ps", "x2_act", "x2_dve",
                "logits_ps", "logits", "kept", "added")}
        nc.all_engine_barrier()
        block = ctx.enter_context(nc.Block())
        PS_A, PS_B, PS_O, PS_XA, PS_XB, PS_L = 0, 1, 2, 4, 5, 6

        @block.sync
        def _(sp):
            for dst, src in ((wo_a[:], a[f"w{layer}_out"][0:P, :]), (wo_b[:], a[f"w{layer}_out"][P:D + 1, :]),
                             (wr_a[:], router[0:P, :]), (wr_b[:], router[P:, :])):
                sp.dma_start(dst, src).then_inc(weights, 16)
            for dst, src in s.expert_weights:
                sp.dma_start(dst, src).then_inc(s.experts_loaded, 16)

        def before(sem, u, k):
            return (sem[1], START + k) if u == 0 else (sem[0], START + k + 1)

        def tiles_of(chunk, first=0, n=CT):
            u, k = chunk
            return bass.ds(k * TB + (u * CT + first), n)

        @block.gpsimd
        def _(pool):
            def take(u, k):
                pool.wait_ge(two["rows_ps"][u], START + k)
                pool.nop(nofuse=True)
                nc.gpsimd.tensor_copy(rows[:, u], attn[:, tiles_of((u, k)), :]).then_inc(two["rows"][u], 1)
                pool.wait_ge(two["rows"][u], START + k + 1)

            def keep(u, k):
                pool.wait_ge(two["x2"][u], START + k + 1)
                pool.nop(nofuse=True)
                nc.gpsimd.tensor_copy(attn[:, tiles_of((u, k)), :], x2[:, u]).then_inc(two["kept"][u], 1)

            def step(this, prev, nxt):
                if nxt:
                    take(*nxt)
                if prev:
                    keep(*prev)

            pipeline(pool, B, lambda: take(0, 0), step, lambda: keep(1, B - 1))

        @block.vector
        def _(dve):
            nc.vector.memset(rows_tb[DB:DB + 1, :, :], 1.0).then_inc(ones, 1)
            nc.vector.memset(x2_tb[DB:DB + 1, :, :], 1.0).then_inc(ones, 1)

            def copy_x2(u, k):
                dve.wait_ge(two["x2_ps"][u], START + k + 1)
                dve.wait_ge(two["logits_ps"][u], START + k)
                nc.vector.tensor_copy(x2_tb[0:DB, u, :], ps[0:DB, PS_XB, :]).then_inc(two["x2_dve"][u], 1)

            def copy_logits(u, k):
                dve.wait_ge(two["logits_ps"][u], START + k + 1)
                nc.vector.tensor_copy(s.logits[:, tiles_of((u, k)), :],
                                      ps[:, PS_L, 0:CT * E].rearrange("p (t e) -> p t e", e=E)
                                      ).then_inc(two["logits"][u], 1)

            def step(this, prev, nxt):
                u, k = this
                link = Chain(dve, chain, 7, 2 * k + u)
                for half in range(2):
                    dve.wait_ge(two["out_ps"][u], START + 2 * k + half + 1)
                    tiles = h[:, tiles_of(this, 2 * half, 2), :]
                    nc.vector.tensor_tensor(tiles, tiles, ps[:, PS_O + half, 0:2 * D].rearrange(
                        "p (t d) -> p t d", d=D), ALU.add).then_inc(two["added"][u], 1)
                dve.wait_ge(two["added"][u], START + 2 * k + 2)
                tiles = [h[:, k * TB + (u * CT + j), :] for j in range(CT)]
                layer_norm_stats(nc, dve, link, tiles, stats[:, u], mv[:, u], var_eps[:, u], two["var"][u])
                if prev:
                    copy_x2(*prev)
                dve.wait_ge(two["std"][u], START + k + 1)
                dve.wait_ge(two["x2_ps"][u], START + k)
                dve.wait_ge(two["kept"][u], START + k)
                layer_norm_apply(nc, link, tiles, x2[:, u], mv[:, u], var_eps[:, u], std[:, u],
                                 tmp[:, u]).then_inc(two["x2"][u], 1)
                if prev:
                    copy_logits(*prev)

            def finish():
                copy_x2(1, B - 1)
                copy_logits(1, B - 1)
            pipeline(dve, B, lambda: None, step, finish)

        @block.scalar
        def _(act):
            def copy_rows(u, k):
                act.wait_ge(two["rows_ps"][u], START + k + 1)
                act.wait_ge(two["out_ps"][u], START + 2 * k)
                nc.scalar.copy(rows_ta[:, u, :], ps[:, PS_A, :]).then_inc(two["rows_act"][u], 1)
                nc.scalar.copy(rows_tb[0:DB, u, :], ps[0:DB, PS_B, :]).then_inc(two["rows_act"][u], 1)

            def copy_x2(u, k):
                act.wait_ge(two["x2_ps"][u], START + k + 1)
                act.wait_ge(two["logits_ps"][u], START + k)
                nc.scalar.copy(x2_ta[:, u, :], ps[:, PS_XA, :]).then_inc(two["x2_act"][u], 1)

            def step(this, prev, nxt):
                u, k = this
                if prev:
                    copy_x2(*prev)
                act.wait_ge(two["var"][u], START + k + 1)
                nc.scalar.activation(std[:, u], var_eps[:, u], ACT.Sqrt).then_inc(two["std"][u], 1)
                if nxt:
                    copy_rows(*nxt)

            def start():
                act.wait_ge(ones, START + 2)
                copy_rows(0, 0)
            pipeline(act, B, start, step, lambda: copy_x2(1, B - 1))

        @block.tensor
        def _(pe):
            pe.wait_ge(weights, START + 64)
            pe.wait_ge(ones, START + 2)

            def transposes(src, bank_a, bank_b):
                for j in range(CT):
                    nc.tensor.transpose(ps[:, bank_a, j * P:(j + 1) * P], src[:, j, 0:P], s.ident[:])
                    last = nc.tensor.transpose(ps[0:DB, bank_b, j * P:(j + 1) * P], src[:, j, P:D], s.ident[:])
                return last

            def transpose_rows(u, k):
                pe.wait_ge(two["rows"][u], START + k + 1)
                sem, done = two["rows_act"], 2 * k if u == 0 else 2 * (k + 1)
                pe.wait_ge(sem[1 - u], START + done)
                transposes(rows[:, u], PS_A, PS_B).then_inc(two["rows_ps"][u], 1)

            def transpose_x2(u, k):
                pe.wait_ge(two["x2"][u], START + k + 1)
                pe.wait_ge(*before(two["x2_act"], u, k))
                pe.wait_ge(*before(two["x2_dve"], u, k))
                transposes(x2[:, u], PS_XA, PS_XB).then_inc(two["x2_ps"][u], 1)

            def project_out(u, k):
                pe.wait_ge(two["rows_act"][u], START + 2 * (k + 1))
                pe.wait_ge(two["added"][1 - u], START + 2 * (k + u))
                for half in range(2):
                    for j in range(2):
                        toks = slice((2 * half + j) * P, (2 * half + j + 1) * P)
                        dst = ps[:, PS_O + half, j * D:(j + 1) * D]
                        nc.tensor.matmul(dst, rows_ta[:, u, toks], wo_a[:], start=True, stop=False)
                        last = nc.tensor.matmul(dst, rows_tb[:, u, toks], wo_b[:], start=False, stop=True)
                    last.then_inc(two["out_ps"][u], 1)

            def compute_logits(u, k):
                pe.wait_ge(two["x2_act"][u], START + k + 1)
                pe.wait_ge(two["x2_dve"][u], START + k + 1)
                pe.wait_ge(*before(two["logits"], u, k))
                for j in range(CT):
                    toks = slice(j * P, (j + 1) * P)
                    dst = ps[:, PS_L, j * E:(j + 1) * E]
                    nc.tensor.matmul(dst, x2_ta[:, u, toks], wr_a[:], start=True, stop=False)
                    last = nc.tensor.matmul(dst, x2_tb[0:RB, u, toks], wr_b[:], start=False, stop=True)
                last.then_inc(two["logits_ps"][u], 1)

            def step(this, prev, nxt):
                project_out(*this)
                if prev:
                    transpose_x2(*prev)
                if nxt:
                    transpose_rows(*nxt)
                if prev:
                    compute_logits(*prev)

            def finish():
                transpose_x2(1, B - 1)
                compute_logits(1, B - 1)
            pipeline(pe, B, lambda: transpose_rows(0, 0), step, finish)


def blocks_of(k):
    n = k * NT + E - 1
    return n + n % 2


def route(nc, a, s, layer, k_top, x_rows):
    with ExitStack() as ctx:
        new_sem = ctx.enter_context(semaphores(nc))

        def sb(name, shape, dt=F32):
            return ctx.enter_context(nc.sbuf_tensor(f"ro{layer}_" + name, shape, dt))

        NBLK, KT = blocks_of(k_top), k_top * NT
        BEFORE = LEAD * layer
        ps = s.psum
        before_me = sb("before_me", [P, P])
        all_ones = sb("all_ones", [P, P])
        expert_i = sb("expert_i", [P, E], I32)
        block_i = sb("block_i", [P, NBLK], I32)
        expert_f = sb("expert_f", [P, E])
        block_f = sb("block_f", [P, NBLK])
        bias = sb("bias", [P, E])
        top = sb("top", [P, NT])
        shifted = sb("shifted", [P, NT, E])
        exps = sb("exps", [P, NT, E])
        total = sb("total", [P, NT])
        scores = sb("scores", [P, NT, E])
        choice = sb("choice", [P, NT, E])
        best = sb("best", [P, NT, 8])
        best_i = sb("best_i", [P, NT, 8], U32)
        best_f = sb("best_f", [P, NT, 8])
        chosen = sb("chosen", [P, k_top, NT, E])
        tile_sum = sb("tile_sum", [P, KT, E])
        run_sum = sb("run_sum", [P, E, KT])
        count_i = sb("count_i", [P, E], I32)
        n_blocks = sb("n_blocks", [P, E])
        end_block = sb("end_block", [P, E])
        start_row = sb("start_row", [P, E])
        place = sb("place", [P, KT, E])
        place_f = sb("place_f", [P, KT])
        reached = sb("reached", [P, NBLK, E])
        owner = sb("owner", [P, NBLK + 2 * BEFORE])
        picked = sb("picked", [P, NT, E])
        weight_sum = sb("weight_sum", [P, NT])
        m = {n: new_sem(f"ro{layer}_{n}") for n in
             ("chain", "ones", "iota", "shifted", "exps", "chosen", "ranks", "bias", "sent")}
        nc.all_engine_barrier()
        block = ctx.enter_context(nc.Block())

        @block.sync
        def _(sp):
            if layer == 1:
                sp.dma_start(bias[:], a["b1_expert"]).then_inc(m["bias"], 16)
                sp.dma_start(x_rows[NBLK * P:, :].rearrange("(t p) d -> p t d", p=P), s.attn[:]
                             ).then_inc(m["sent"], 16)
                sp.wait_ge(m["sent"], START + 16)

        @block.gpsimd
        def _(pool):
            nc.gpsimd.iota(expert_i[:], [[1, E]], base=0, channel_multiplier=0).then_inc(m["iota"], 1)
            nc.gpsimd.iota(block_i[:], [[1, NBLK]], base=0, channel_multiplier=0).then_inc(m["iota"], 1)
            nc.gpsimd.memset(all_ones[:], 1.0).then_inc(m["ones"], 1)
            pool.wait_ge(m["ones"], START + 1)
            nc.gpsimd.affine_select(out=before_me[:], in_=all_ones[:], compare_op=ALU.is_gt, fill=0.0, base=0,
                                    pattern=[[1, P]], channel_multiplier=-1).then_inc(m["ones"], 1)

        @block.tensor
        def _(pe):
            pe.wait_ge(m["ones"], START + 2)
            pe.wait_ge(m["chosen"], START + k_top)
            flat = chosen[:].rearrange("p k t e -> p (k t e)")
            nc.tensor.matmul(ps[:, 0, 0:KT * E], before_me[:], flat, start=True, stop=True)
            nc.tensor.matmul(ps[:, 1, 0:KT * E], all_ones[:], flat, start=True, stop=True).then_inc(m["ranks"], 1)

        @block.scalar
        def _(act):
            act.wait_ge(m["shifted"], START + 1)
            nc.scalar.activation(exps[:], shifted[:], ACT.Exp).then_inc(m["exps"], 1)

        @block.vector
        def _(dve):
            link = Chain(dve, m["chain"])

            def over(x, shape):
                return x.to_broadcast(shape)

            te = [P, NT, E]
            link(nc.vector.tensor_reduce(top[:], s.logits[:], AX.X, ALU.max))
            nc.vector.tensor_tensor(shifted[:], s.logits[:], over(top[:].unsqueeze(2), te),
                                    ALU.subtract).then_inc(m["shifted"], 1)
            dve.wait_ge(m["exps"], START + 1)
            link(nc.vector.tensor_reduce(total[:], exps[:], AX.X, ALU.add))
            link(nc.vector.reciprocal(total[:], total[:]))
            link(nc.vector.tensor_tensor(scores[:], exps[:], over(total[:].unsqueeze(2), te), ALU.mult))
            ranked = scores
            if layer == 1:
                dve.wait_ge(m["bias"], START + 16)
                link(nc.vector.tensor_tensor(choice[:], scores[:], over(bias[:].unsqueeze(1), te), ALU.add))
                ranked = choice
            for t in range(NT):
                last = nc.vector.max(best[:, t, :], ranked[:, t, :])
            link(last)
            for t in range(NT):
                last = nc.vector.max_index(best_i[:, t, :], best[:, t, :], ranked[:, t, :])
            link(last)
            link(nc.vector.tensor_copy(best_f[:], best_i[:]))
            dve.wait_ge(m["iota"], START + 2)
            link(nc.vector.tensor_copy(expert_f[:], expert_i[:]))
            link(nc.vector.tensor_copy(block_f[:], block_i[:]))
            for k in range(k_top):
                nc.vector.tensor_tensor(chosen[:, k], over(expert_f[:].unsqueeze(1), te),
                                        over(best_f[:, :, k:k + 1], te), ALU.is_equal).then_inc(m["chosen"], 1)
            if layer == 0:
                link(nc.vector.tensor_copy(s.gate[:, 0, :], total[:]))
            else:
                for k in range(k_top):
                    dve.wait_ge(m["chosen"], START + k + 1)
                    link(nc.vector.tensor_tensor(picked[:], scores[:], chosen[:, k], ALU.mult))
                    link(nc.vector.tensor_reduce(s.gate[:, k, :], picked[:], AX.X, ALU.add))
                link(nc.vector.tensor_tensor(weight_sum[:], s.gate[:, 0, :], s.gate[:, 1, :], ALU.add))
                link(nc.vector.tensor_scalar(weight_sum[:], weight_sum[:], 1e-9, None, ALU.add))
                link(nc.vector.reciprocal(weight_sum[:], weight_sum[:]))
                for k in range(k_top):
                    link(nc.vector.tensor_tensor(s.gate[:, k, :], s.gate[:, k, :], weight_sum[:], ALU.mult))
            dve.wait_ge(m["ranks"], START + 1)
            link(nc.vector.tensor_copy(tile_sum[:].rearrange("p t e -> p (t e)"), ps[:, 1, 0:KT * E]))
            dve.wait_ge(m["ones"], START + 2)
            for e in range(E):
                last = nc.vector.tensor_tensor_scan(run_sum[:, e, :], all_ones[:, 0:KT], tile_sum[:, :, e], 0.0,
                                                    ALU.mult, ALU.add)
            link(last)
            link(nc.vector.tensor_scalar(n_blocks[:], run_sum[:, :, KT - 1], float(P - 1), None, ALU.add))
            link(nc.vector.tensor_copy(count_i[:], n_blocks[:]))
            link(nc.vector.tensor_scalar(count_i[:], count_i[:], P.bit_length() - 1, None, ALU.arith_shift_right))
            link(nc.vector.tensor_copy(n_blocks[:], count_i[:]))
            link(nc.vector.tensor_tensor_scan(end_block[:], all_ones[:, 0:E], n_blocks[:], 0.0, ALU.mult, ALU.add))
            link(nc.vector.tensor_tensor(start_row[:], end_block[:], n_blocks[:], ALU.subtract))
            link(nc.vector.tensor_scalar(start_row[:], start_row[:], float(P), None, ALU.mult))
            kte = [P, KT, E]
            link(nc.vector.tensor_tensor(place[:], run_sum[:].rearrange("p e t -> p t e"), tile_sum[:], ALU.subtract))
            link(nc.vector.tensor_tensor(place[:], place[:], ps[:, 0, 0:KT * E].rearrange("p (t e) -> p t e", e=E),
                                         ALU.add))
            link(nc.vector.tensor_tensor(place[:], place[:], over(start_row[:].unsqueeze(1), kte), ALU.add))
            link(nc.vector.tensor_tensor(place[:], place[:], chosen[:].rearrange("p k t e -> p (k t) e"), ALU.mult))
            link(nc.vector.tensor_reduce(place_f[:], place[:], AX.X, ALU.add))
            link(nc.vector.tensor_copy(s.place[:, 0:KT], place_f[:]))
            nbe = [P, NBLK, E]
            routed = owner[:, BEFORE:BEFORE + NBLK]
            if BEFORE:
                link(nc.vector.memset(owner[:], float(E)))
            link(nc.vector.tensor_tensor(reached[:], over(block_f[:].unsqueeze(2), nbe),
                                         over(end_block[:].unsqueeze(1), nbe), ALU.is_ge))
            link(nc.vector.tensor_reduce(routed, reached[:], AX.X, ALU.add))
            link(nc.vector.tensor_scalar(routed, routed, float(E - 1), None, ALU.min))
            link(nc.vector.tensor_copy(s.owner[:, 0:NBLK + 2 * BEFORE], owner[:]))


def experts(nc, a, s, layer, k_top, x_rows, y_rows, out):
    with ExitStack() as ctx:
        new_sem = ctx.enter_context(semaphores(nc))

        def sb(name, shape, dt=F32):
            return ctx.enter_context(nc.sbuf_tensor(f"ex{layer}_" + name, shape, dt))

        F = (F0, F1)[layer]
        FC = F // P
        NE = E + layer
        BEFORE = LEAD * layer
        KT = k_top * NT
        N = blocks_of(k_top) + 2 * BEFORE
        TURNS = N // 2
        FIRST = BEFORE // 2
        LAST = TURNS - FIRST
        ps = s.psum
        up_a, up_b, down = (dst for dst, _ in s.expert_weights)
        x = sb("x", [P, 2, D])
        xt_a = sb("xt_a", [P, 2, P])
        xt_b = sb("xt_b", [DB, 2, P])
        silu = sb("silu", [P, 2, F])
        g = sb("g", [P, 2, F])
        g_t = sb("g_t", [P, 2, F])
        y = sb("y", [P, 2, D])
        two = {n: [new_sem(f"ex{layer}_{n}{u}") for u in range(2)] for n in
               ("loaded", "stored", "x_ps", "xt_a", "xt_b", "gate_ps", "up_ps", "silu", "g", "g_ps", "g_t", "y_ps", "y")}
        scattered = [new_sem(f"ex{layer}_scattered{i}", start=0) for i in range(8)]
        rows_placed = new_sem(f"ex{layer}_rows_placed")
        if layer == 1:
            PAIR = 2
            ROUNDS = NT // (2 * PAIR)
            rows = sb("rows", [P, 2, k_top, PAIR, D])
            landed = [[new_sem(f"ex_landed{p}_{i}", start=0) for i in range(k_top * PAIR)] for p in range(2)]
            weighted, out_stored = (new_sem("ex_" + n) for n in ("weighted", "out_stored"))
            summed = [new_sem(f"ex_summed{p}") for p in range(2)]
        nc.all_engine_barrier()
        block = ctx.enter_context(nc.Block())
        PS_X, PS_GATE, PS_UP, PS_G, PS_Y = 0, 1, 3, 5, 6

        def turns(eng, lo, hi, step, behind=None):
            if hi > lo:
                with eng.Fori(lo, hi) as i:
                    step(1, i, 0, i, 0, i + 1)
                    if behind:
                        behind(i, 0)
                    step(0, i + 1, 1, i, 1, i + 1)
                    if behind:
                        behind(i, 1)

        def blocks(eng, first, step, final):
            first()
            turns(eng, 0, TURNS - 1, step)
            final(1, TURNS - 1, 0, TURNS - 1)

        @block.gpsimd
        def _(pool):
            for i in range(KT):
                pool.indirect_dma_start(out=x_rows, out_offset=bass.IndirectOffsetOnAxis(ap=s.place[:, i:i + 1], axis=0),
                                        in_=s.attn[:, i % NT, :], in_offset=None).then_inc(scattered[i % 8], 16)
            for i in range(8):
                pool.wait_ge(scattered[i], 16 * (KT // 8))
            pool.nop(nofuse=True).then_inc(rows_placed, 1)
            if layer == 1:
                for u in range(2):
                    pool.wait_ge(two["stored"][u], START + 16 * (LAST - FIRST))
                for c in range(ROUNDS):
                    for p in range(2):
                        if c:
                            pool.wait_ge(summed[p], START + k_top * c)
                        for k in range(k_top):
                            for j in range(PAIR):
                                i = k * NT + (2 * c + p) * PAIR + j
                                pool.indirect_dma_start(out=rows[:, p, k, j, :], out_offset=None, in_=y_rows,
                                                        in_offset=bass.IndirectOffsetOnAxis(ap=s.place[:, i:i + 1],
                                                                                            axis=0)
                                                        ).then_inc(landed[p][k * PAIR + j], 16)

        @block.sync
        def _(sp):
            def store(u, k):
                sp.wait_ge(two["y"][u], START + k + 1)
                sp.dma_start(y_rows[bass.ds((2 * k + u) * P - BEFORE * P, P), :], y[:, u, :]).then_inc(two["stored"][u], 16)

            with sp.Fori(FIRST, LAST) as i:
                store(0, i)
                store(1, i)
            for u in range(2):
                sp.wait_ge(two["stored"][u], START + 16 * (LAST - FIRST))
            if layer == 1:
                for c in range(ROUNDS):
                    for p in range(2):
                        sp.wait_ge(summed[p], START + k_top * (c + 1))
                    n = 2 * PAIR
                    sp.dma_start(out[c * n * P:(c + 1) * n * P, :].rearrange("(t p) d -> p t d", p=P),
                                 s.h[:, c * n:(c + 1) * n, :]).then_inc(out_stored, 16)
                sp.wait_ge(out_stored, START + 16 * ROUNDS)

        @block.scalar
        def _(act):
            LEAD_AT, ROUTED_AT, TAIL_AT = blocks_of(k_top), -BEFORE, 0

            def load(u, k, at):
                act.dma_start(x[:, u, :], x_rows[bass.ds(2 * k * P + (u + at) * P, P), :]
                              ).then_inc(two["loaded"][u], 16)

            def copy_x(u, k):
                act.wait_ge(two["x_ps"][u], START + k + 1)
                act.wait_ge(two["up_ps"][u], START + k)
                nc.scalar.copy(xt_a[:, u, :], ps[:, PS_X, 0:P]).then_inc(two["xt_a"][u], 1)
                nc.scalar.copy(xt_b[:, u, :], ps[0:DB, PS_X, P:2 * P]).then_inc(two["xt_b"][u], 1)

            def activate(u, k):
                act.wait_ge(two["gate_ps"][u], START + k + 1)
                act.wait_ge(two["g"][u], START + k)
                nc.scalar.activation(silu[:, u, :], ps[:, PS_GATE + u, 0:F], ACT.Silu).then_inc(two["silu"][u], 1)

            def first():
                if layer == 0:
                    act.wait_ge(rows_placed, START + 1)
                load(0, 0, LEAD_AT if BEFORE else ROUTED_AT)
                load(1, 0, LEAD_AT if BEFORE else ROUTED_AT)
                copy_x(0, 0)
                activate(0, 0)
                copy_x(1, 0)

            def step_at(at):
                def step(u, k, pu, pk, nu, nk):
                    load(nu, nk, at)
                    activate(u, k)
                    copy_x(nu, nk)
                return step

            first()
            if layer == 1:
                turns(act, 0, FIRST - 1, step_at(LEAD_AT))
                act.wait_ge(rows_placed, START + 1)
            turns(act, max(FIRST - 1, 0), LAST - 1, step_at(ROUTED_AT))
            turns(act, LAST - 1, TURNS - 1, step_at(TAIL_AT))
            activate(1, TURNS - 1)

        @block.vector
        def _(dve):
            def product(u, k):
                dve.wait_ge(two["silu"][u], START + k + 1)
                dve.wait_ge(two["up_ps"][u], START + k + 1)
                dve.wait_ge(two["g_ps"][u], START + k)
                nc.vector.tensor_tensor(g[:, u, :], silu[:, u, :], ps[:, PS_UP + u, 0:F], ALU.mult
                                        ).then_inc(two["g"][u], 1)

            def copy_g(u, k):
                dve.wait_ge(two["g_ps"][u], START + k + 1)
                dve.wait_ge(two["y_ps"][u], START + k)
                nc.vector.tensor_copy(g_t[:, u, :], ps[:, PS_G, 0:F]).then_inc(two["g_t"][u], 1)

            def copy_y(u, k):
                dve.wait_ge(two["y_ps"][u], START + k + 1)
                dve.wait_ge(two["stored"][u], START + 16 * (k - FIRST))
                nc.vector.tensor_copy(y[:, u, :], ps[:, PS_Y, 0:D]).then_inc(two["y"][u], 1)

            def add_shared(first_tile):
                def finish(u, k):
                    dve.wait_ge(two["y_ps"][u], START + k + 1)
                    tile = s.h[:, bass.ds(2 * k + (u + first_tile), 1), :].rearrange("p o d -> p (o d)")
                    nc.vector.tensor_tensor(tile, tile, ps[:, PS_Y, 0:D], ALU.add).then_inc(two["y"][u], 1)
                return finish

            def step_with(finish):
                def step(u, k, pu, pk, nu, nk):
                    copy_g(pu, pk)
                    product(u, k)
                    finish(pu, pk)
                return step

            def mix(c, p):
                for sem in landed[p]:
                    dve.wait_ge(sem, 16 * (c + 1))
                pair = bass.ds((2 * c + p) * PAIR, PAIR)
                for k in range(k_top):
                    weight = s.gate[:, k, pair].unsqueeze(2).to_broadcast([P, PAIR, D])
                    nc.vector.tensor_tensor(rows[:, p, k], rows[:, p, k], weight, ALU.mult).then_inc(weighted, 1)
                for k in range(k_top):
                    dve.wait_ge(weighted, START + k_top * (2 * c + p) + k + 1)
                    dve.wait_ge(summed[p], START + k_top * c + k)
                    nc.vector.tensor_tensor(s.h[:, pair, :], s.h[:, pair, :], rows[:, p, k], ALU.add
                                            ).then_inc(summed[p], 1)

            product(0, 0)
            if layer == 0:
                turns(dve, 0, TURNS - 1, step_with(copy_y))
                finish = copy_y
            else:
                turns(dve, 0, FIRST, step_with(add_shared(0)))
                turns(dve, FIRST, LAST, step_with(copy_y))
                finish = add_shared(LEAD - (BEFORE + blocks_of(k_top)))
                step = step_with(finish)
                step(1, LAST, 0, LAST, 0, LAST + 1)
                step(0, LAST + 1, 1, LAST, 1, LAST + 1)
                turns(dve, LAST + 1, TURNS - 1, step, lambda i, p: mix(i - (LAST + 1), p))
            step_with(finish)(1, TURNS - 1, 0, TURNS - 1, None, None)
            copy_g(1, TURNS - 1)
            finish(1, TURNS - 1)
            if layer == 1:
                for c in range(TURNS - 1 - (LAST + 1), ROUNDS):
                    for p in range(2):
                        mix(c, p)

        @block.tensor
        def _(pe):
            pe.wait_ge(s.experts_loaded, START + 16 * len(s.expert_weights))

            def owner(u, k):
                return pe.value_load(s.owner[0:1, bass.ds(2 * k + u, 1)], min_val=0, max_val=NE - 1)

            def transpose_x(u, k, pu, pk):
                pe.wait_ge(two["loaded"][u], START + 16 * (k + 1))
                if pk is not None:
                    pe.wait_ge(two["xt_b"][pu], START + pk + 1)
                nc.tensor.transpose(ps[:, PS_X, 0:P], x[:, u, 0:P], s.ident[:])
                nc.tensor.transpose(ps[0:DB, PS_X, P:2 * P], x[:, u, P:D], s.ident[:]).then_inc(two["x_ps"][u], 1)

            def project(u, k, e, which, bank, done):
                dst = ps[:, bank + u, 0:F]
                nc.tensor.matmul(dst, xt_a[:, u, :], up_a[:, which, bass.ds(e, 1), :].rearrange("p o f -> p (o f)"),
                                 start=True, stop=False)
                nc.tensor.matmul(dst, xt_b[:, u, :], up_b[:, which, bass.ds(e, 1), :].rearrange("p o f -> p (o f)"),
                                 start=False, stop=True).then_inc(done[u], 1)

            def gate(u, k, e):
                pe.wait_ge(two["xt_b"][u], START + k + 1)
                pe.wait_ge(two["silu"][u], START + k)
                project(u, k, e, 0, PS_GATE, two["gate_ps"])

            def up(u, k, e):
                pe.wait_ge(two["g"][u], START + k)
                project(u, k, e, 1, PS_UP, two["up_ps"])

            def transpose_g(u, k, pu, pk):
                pe.wait_ge(two["g"][u], START + k + 1)
                if pk is not None:
                    pe.wait_ge(two["g_t"][pu], START + pk)
                for c in range(FC):
                    last = nc.tensor.transpose(ps[:, PS_G, c * P:(c + 1) * P], g[:, u, c * P:(c + 1) * P], s.ident[:])
                last.then_inc(two["g_ps"][u], 1)

            def down_project(u, k, e, pu, pk):
                pe.wait_ge(two["g_t"][u], START + k + 1)
                if pk is not None:
                    pe.wait_ge(two["y"][pu], START + pk)
                for c in range(FC):
                    last = nc.tensor.matmul(ps[:, PS_Y, 0:D], g_t[:, u, c * P:(c + 1) * P],
                                            down[:, bass.ds(e, 1), c, :].rearrange("p o d -> p (o d)"),
                                            start=(c == 0), stop=(c == FC - 1))
                last.then_inc(two["y_ps"][u], 1)

            def first():
                transpose_x(0, 0, None, None)
                e = owner(0, 0)
                gate(0, 0, e)
                up(0, 0, e)
                transpose_x(1, 0, 0, 0)

            def step(u, k, pu, pk, nu, nk):
                e = owner(u, k)
                gate(u, k, e)
                transpose_g(pu, pk, u, k)
                if nu is not None:
                    transpose_x(nu, nk, u, k)
                up(u, k, e)
                down_project(pu, pk, owner(pu, pk), u, k)

            def final(u, k, pu, pk):
                step(u, k, pu, pk, None, None)
                transpose_g(u, k, pu, pk + 1)
                down_project(u, k, owner(u, k), pu, pk + 1)
            blocks(pe, first, step, final)




def mix_experts(nc, a, s, layer, k_top, y_rows):
    with ExitStack() as ctx:
        new_sem = ctx.enter_context(semaphores(nc))

        def sb(name, shape, dt=F32):
            return ctx.enter_context(nc.sbuf_tensor(f"mx{layer}_" + name, shape, dt))

        RING = 8
        h = s.h
        rows = sb("rows", [P, RING, D])
        rounded = sb("rounded", [P, 2, D], BF16)
        landed = [new_sem(f"mx{layer}_landed{i}", start=0) for i in range(RING)]
        chain, added, shared, mixed = (new_sem(f"mx{layer}_{n}")
                                       for n in ("chain", "added", "shared", "mixed"))
        nc.all_engine_barrier()
        block = ctx.enter_context(nc.Block())
        jobs = [(t, k) for t in range(NT) for k in range(k_top)]

        if layer == 1:
            @block.sync
            def _(sp):
                sp.dma_start(s.attn[:], y_rows[blocks_of(k_top) * P:, :].rearrange("(t p) d -> p t d", p=P)
                             ).then_inc(shared, 16)

        @block.gpsimd
        def _(pool):
            for n, (t, k) in enumerate(jobs):
                if n >= RING:
                    pool.wait_ge(added, START + n - RING + 1)
                i = k * NT + t
                pool.indirect_dma_start(out=rows[:, n % RING, :], out_offset=None, in_=y_rows,
                                        in_offset=bass.IndirectOffsetOnAxis(ap=s.place[:, i:i + 1], axis=0)
                                        ).then_inc(landed[n % RING], 16)

        @block.vector
        def _(dve):
            link = Chain(dve, chain)
            if layer == 1:
                dve.wait_ge(shared, START + 16)
                for t in range(NT):
                    last = nc.vector.tensor_tensor(h[:, t, :], h[:, t, :], s.attn[:, t, :], ALU.add)
                link(last)
            for n, (t, k) in enumerate(jobs):
                dve.wait_ge(landed[n % RING], 16 * (n // RING + 1))
                if k:
                    dve.wait_ge(added, START + n)
                src = rows[:, n % RING, :]
                if layer == 0:
                    link(nc.vector.tensor_copy(rounded[:, n % 2, :], src))
                    src = rounded[:, n % 2, :]
                nc.vector.scalar_tensor_tensor(out=h[:, t, :], in0=src, scalar=s.gate[:, k, t:t + 1],
                                               in1=h[:, t, :], op0=ALU.mult, op1=ALU.add).then_inc(added, 1)


def relu_attention(nc, a, s):
    with ExitStack() as ctx:
        new_sem = ctx.enter_context(semaphores(nc))

        def sb(name, shape, dt=F32):
            return ctx.enter_context(nc.sbuf_tensor("ra_" + name, shape, dt))

        h, attn, ps = s.h, s.attn, s.psum
        V1 = HD + 1
        HH = H // 2
        PAIRS = H // 2
        PA = P // (2 * HD)
        FA = 2 * PA * M_FEAT
        FB = H * M_FEAT - FA
        NORM = float(HD) ** -0.25
        CTX, OUT, SLOTS = 4, 6, 3
        w_a = sb("w_a", [P, 3, P])
        w_b = sb("w_b", [DB, 3, P])
        wv_a = sb("wv_a", [P, D])
        wv_b = sb("wv_b", [DB + 1, D])
        bias = sb("bias", [P, 3])
        half_bias = sb("half_bias", [P, 3])
        feat_a = sb("feat_a", [P, FA])
        feat_b = sb("feat_b", [P, 2, FB])
        stats = sb("stats", [P, 2, CT, 6])
        mv = sb("mv", [P, 2, CT, 2])
        var_eps = sb("var_eps", [P, 2, CT])
        std = sb("std", [P, 2, CT])
        tmp = sb("tmp", [P, 2, CT])
        xn = sb("xn", [P, 2, CT, D])
        xt_a = sb("xt_a", [P, 2, CHUNK])
        xt_b = sb("xt_b", [DB + 1, 2, CHUNK])
        qk = sb("qk", [P, 2, 3, CHUNK])
        q_feat = sb("q_feat", [P, PAIRS, S])
        k_feat = sb("k_feat", [P, 2, H * M_FEAT])
        v_ext = sb("v_ext", [P, 2, CT, H, V1])
        context = sb("context", [P, PAIRS, HH * V1])
        inv = sb("inv", [P, 2, H])
        weights, ones, halved, chain, inv_done = (new_sem("ra_" + n) for n in
                                                  ("weights", "ones", "halved", "chain", "inv_done"))
        ring_full, ring_act, ring_dve = ([new_sem(f"ra_{n}{i}") for i in range(SLOTS)]
                                         for n in ("ring_full", "ring_act", "ring_dve"))
        var, ln_std, normed = ([new_sem(f"ra_{n}{u}") for u in range(2)] for n in ("var", "std", "normed"))
        context_full, context_ready, accumulated = (new_sem("ra_" + n) for n in
                                                    ("context_full", "context_ready", "accumulated"))
        out_full = [new_sem(f"ra_out_full{i}") for i in range(2)]
        out_free = [new_sem(f"ra_out_free{i}") for i in range(2)]
        nc.all_engine_barrier()
        block = ctx.enter_context(nc.Block())

        UNITS = ([("xa", 0, "act"), ("xb", 0, "act")] + [("qk", r, "act") for r in range(3)]
                 + [("v", i, "act") for i in range(2)] + [("qf", p, "dve") for p in range(PAIRS)]
                 + [("kf", i, "dve") for i in range(2 * CT)])
        assert 2 * len(UNITS) % SLOTS == 0
        PER_BODY = 2 * len(UNITS) // SLOTS

        def readers(eng, n_last):
            return [sum(1 for n in range(n_last) if n % SLOTS == i and UNITS[n % len(UNITS)][2] == eng)
                    for i in range(SLOTS)]

        TOTAL = {eng: readers(eng, 2 * len(UNITS)) for eng in ("act", "dve")}
        ring_free = {"act": ring_act, "dve": ring_dve}

        def at(kind, i, u):
            return u * len(UNITS) + [x[:2] for x in UNITS].index((kind, i))

        def full(b, n):
            return ring_full[n % SLOTS], START + PER_BODY * b + n // SLOTS + 1

        def left(b, n):
            eng = UNITS[n % len(UNITS)][2]
            return ring_free[eng][n % SLOTS], START + TOTAL[eng][n % SLOTS] * b + readers(eng, n + 1)[n % SLOTS]

        def wait_left(eng, b, numbers):
            newest = {(UNITS[n % len(UNITS)][2], n % SLOTS): n for n in sorted(numbers)}
            for n in newest.values():
                eng.wait_ge(*left(b, n))

        @block.sync
        def _(sp):
            for dst, src in ((w_a[:], a["w1_qk"][0:P]), (w_b[:], a["w1_qk"][P:D]), (wv_a[:], a["w1_v"][0:P]),
                             (wv_b[:], a["w1_v"][P:D + 1]), (bias[:], a["b1_qk"]), (feat_a[:], a["feat_a"]),
                             (feat_b[:], a["feat_b"])):
                sp.dma_start(dst, src).then_inc(weights, 16)

        @block.gpsimd
        def _(pool):
            nc.gpsimd.memset(context[:], 0.0).then_inc(ones, 1)
            pool.wait_ge(ones, START + 1)
            nc.gpsimd.memset(v_ext[:, :, :, :, HD:V1], 1.0).then_inc(ones, 1)

        @block.vector
        def _(dve):
            nc.vector.memset(xt_b[DB:DB + 1, :, :], 1.0).then_inc(halved, 1)
            dve.wait_ge(weights, START + 112)
            nc.vector.tensor_scalar(half_bias[:], bias[:], NORM, None, ALU.mult).then_inc(halved, 1)
            dve.wait_ge(ones, START + 2)

            def features(b, n, dst):
                dve.wait_ge(*full(b, n))
                nc.vector.tensor_scalar(dst, ps[:, n % SLOTS, 0:dst.shape[-1]], 0.0, KERNEL_EPS, ALU.max, ALU.add
                                        ).then_inc(ring_dve[n % SLOTS], 1)

            with dve.Fori(0, B) as b:
                link = Chain(dve, chain, 2 * 7, b)
                for u in range(2):
                    tiles = [h[:, b * TB + (u * CT + j), :] for j in range(CT)]
                    layer_norm_stats(nc, dve, link, tiles, stats[:, u], mv[:, u], var_eps[:, u], var[u])
                    dve.wait_ge(ln_std[u], START + b + 1)
                    layer_norm_apply(nc, link, tiles, xn[:, u], mv[:, u], var_eps[:, u], std[:, u],
                                     tmp[:, u]).then_inc(normed[u], 1)
                    for i in range(2):
                        dve.wait_ge(out_full[i], START + TB // 2 * b)
                    for p in range(PAIRS):
                        features(b, at("qf", p, u), q_feat[:, p, u * CHUNK:(u + 1) * CHUNK])
                    for j in range(CT):
                        n_before = 2 * u * CT // 2 + j - 1
                        dve.wait_ge(accumulated, START + TB * b + max(n_before, 0))
                        features(b, at("kf", 2 * j, u), k_feat[:, j % 2, 0:FA])
                        features(b, at("kf", 2 * j + 1, u), k_feat[:, j % 2, FA:])
                dve.wait_ge(accumulated, START + TB * (b + 1))
                for bank in range(2):
                    for lo in range(2):
                        part = slice(lo * M_FEAT, (lo + 1) * M_FEAT)
                        for p in range(PAIRS // 2):
                            col = (2 * p + lo) * V1
                            last = nc.vector.tensor_copy(
                                context[part, bank * PAIRS // 2 + p, col:col + V1],
                                ps[part, CTX + bank, p * HH * V1 + col:p * HH * V1 + col + V1])
                last.then_inc(context_ready, 1)
                for t in range(TB):
                    i = t % 2
                    dve.wait_ge(out_full[i], START + TB // 2 * b + t // 2 + 1)
                    heads = ps[:, OUT + i, 0:H * V1].rearrange("p (h v) -> p h v", v=V1)
                    nc.vector.reciprocal(inv[:, i, :], heads[:, :, HD]).then_inc(inv_done, 1)
                    dve.wait_ge(inv_done, START + TB * b + t + 1)
                    nc.vector.tensor_tensor(attn[:, b * TB + t, :].rearrange("p (h d) -> p h d", d=HD),
                                            heads[:, :, 0:HD], inv[:, i, :].unsqueeze(2).to_broadcast([P, H, HD]),
                                            ALU.mult).then_inc(out_free[i], 1)

        @block.scalar
        def _(act):
            act.wait_ge(halved, START + 2)
            act.wait_ge(ones, START + 2)
            with act.Fori(0, B) as b:
                for u in range(2):
                    act.wait_ge(var[u], START + b + 1)
                    nc.scalar.activation(std[:, u], var_eps[:, u], ACT.Sqrt).then_inc(ln_std[u], 1)
                    for n, (kind, i, eng) in enumerate(UNITS):
                        if eng != "act":
                            continue
                        n += u * len(UNITS)
                        slot = n % SLOTS
                        act.wait_ge(*full(b, n))
                        if kind == "xa":
                            ins = nc.scalar.copy(xt_a[:, u, :], ps[:, slot, :])
                        elif kind == "xb":
                            ins = nc.scalar.copy(xt_b[0:DB, u, :], ps[0:DB, slot, :])
                        elif kind == "qk":
                            ins = nc.scalar.activation(qk[:, u, i, :], ps[:, slot, :], ACT.Identity,
                                                       bias=half_bias[:, i:i + 1], scale=NORM)
                        else:
                            ins = nc.scalar.copy(v_ext[:, u, 2 * i:2 * i + 2, :, 0:HD],
                                                 ps[:, slot, 0:2 * D].rearrange("p (t h d) -> p t h d", t=2, d=HD))
                        ins.then_inc(ring_act[slot], 1)

        @block.tensor
        def _(pe):
            pe.wait_ge(weights, START + 112)
            pe.wait_ge(halved, START + 2)

            def slot_left(b, n):
                slot = n % SLOTS
                for eng in ("act", "dve"):
                    count = readers(eng, n)[slot]
                    if n >= SLOTS:
                        if UNITS[(n - SLOTS) % len(UNITS)][2] == eng:
                            pe.wait_ge(ring_free[eng][slot], START + TOTAL[eng][slot] * b + count)
                    else:
                        pe.wait_ge(ring_free[eng][slot], START + TOTAL[eng][slot] * b)

            def unit(b, u, kind, i):
                n = at(kind, i, u)
                slot = n % SLOTS
                if kind == "xa":
                    slot_left(b, n)
                    slot_left(b, n + 1)
                elif kind != "xb":
                    slot_left(b, n)
                if kind == "xa":
                    for j in range(CT):
                        last = nc.tensor.transpose(ps[:, slot, j * P:(j + 1) * P], xn[:, u, j, 0:P], s.ident[:])
                elif kind == "xb":
                    for j in range(CT):
                        last = nc.tensor.transpose(ps[0:DB, slot, j * P:(j + 1) * P], xn[:, u, j, P:D], s.ident[:])
                elif kind == "qk":
                    nc.tensor.matmul(ps[:, slot, :], w_a[:, i, :], xt_a[:, u, :], start=True, stop=False)
                    last = nc.tensor.matmul(ps[:, slot, :], w_b[:, i, :], xt_b[0:DB, u, :], start=False, stop=True)
                elif kind == "v":
                    for j in range(2):
                        toks = slice((2 * i + j) * P, (2 * i + j + 1) * P)
                        dst = ps[:, slot, j * D:(j + 1) * D]
                        nc.tensor.matmul(dst, xt_a[:, u, toks], wv_a[:], start=True, stop=False)
                        last = nc.tensor.matmul(dst, xt_b[:, u, toks], wv_b[:], start=False, stop=True)
                elif kind == "qf":
                    if i < PA:
                        last = nc.tensor.matmul(ps[:, slot, :], feat_a[:, i * P:(i + 1) * P], qk[:, u, 0, :],
                                                start=True, stop=True)
                    else:
                        last = nc.tensor.matmul(ps[:, slot, :], feat_b[:, 0, (i - PA) * P:(i - PA + 1) * P],
                                                qk[:, u, 2, :], start=True, stop=True)
                else:
                    toks = slice(i // 2 * P, (i // 2 + 1) * P)
                    if i % 2 == 0:
                        last = nc.tensor.matmul(ps[:, slot, 0:FA], qk[:, u, 1, toks], feat_a[:], start=True, stop=True)
                    else:
                        last = nc.tensor.matmul(ps[:, slot, 0:FB], qk[:, u, 2, toks], feat_b[:, 1, :],
                                                start=True, stop=True)
                last.then_inc(ring_full[slot], 1)

            def accumulate(b, u, j):
                t = u * CT + j
                needed = [at("kf", 2 * j, u), at("kf", 2 * j + 1, u)]
                if j == 0:
                    needed += [at("v", 0, u), at("v", 1, u)]
                wait_left(pe, b, needed)
                if t == 0:
                    pe.wait_ge(context_ready, START + b)
                for p in range(PAIRS):
                    bank, col = p // (PAIRS // 2), p % (PAIRS // 2) * HH * V1
                    heads = slice(bank * HH, (bank + 1) * HH)
                    last = nc.tensor.matmul(ps[:, CTX + bank, col:col + HH * V1], k_feat[:, j % 2, p * P:(p + 1) * P],
                                            v_ext[:, u, j, heads, :].rearrange("p h v -> p (h v)"),
                                            start=(t == 0 and col == 0), stop=(t == TB - 1), skip_group_check=True)
                last.then_inc(accumulated, 1)

            with pe.Fori(0, B) as b:
                for u in range(2):
                    pe.wait_ge(normed[u], START + b + 1)
                    unit(b, u, "xa", 0)
                    unit(b, u, "xb", 0)
                    wait_left(pe, b, [at("xa", 0, u), at("xb", 0, u)])
                    for i in range(3):
                        unit(b, u, "qk", i)
                    for i in range(2):
                        unit(b, u, "v", i)
                    wait_left(pe, b, [at("qk", i, u) for i in range(3)])
                    for i in range(PAIRS):
                        unit(b, u, "qf", i)
                    unit(b, u, "kf", 0)
                    unit(b, u, "kf", 1)
                    for j in range(CT):
                        if j + 1 < CT:
                            unit(b, u, "kf", 2 * j + 2)
                            unit(b, u, "kf", 2 * j + 3)
                        accumulate(b, u, j)
                pe.wait_ge(context_ready, START + b + 1)
                wait_left(pe, b, [at("qf", p, u) for p in range(PAIRS) for u in range(2)])
                for t in range(TB):
                    i = t % 2
                    pe.wait_ge(out_free[i], START + TB // 2 * b + t // 2)
                    for p in range(PAIRS):
                        bank = p // (PAIRS // 2)
                        last = nc.tensor.matmul(ps[:, OUT + i, bank * HH * V1:(bank + 1) * HH * V1],
                                                q_feat[:, p, t * P:(t + 1) * P], context[:, p, :],
                                                start=(p % (PAIRS // 2) == 0), stop=(p % (PAIRS // 2) == PAIRS // 2 - 1))
                    last.then_inc(out_full[i], 1)


class Stores:
    pass


@contextmanager
def expert_weights(nc, a, layer):
    names = [f"e{layer}_{n}" for n in ("up_a", "up_b", "down")]
    with ExitStack() as ctx:
        new_sem = ctx.enter_context(semaphores(nc))
        pairs = [(ctx.enter_context(nc.sbuf_tensor("w_" + n, a[n].shape, F32))[:], a[n]) for n in names]
        yield pairs, new_sem(f"experts{layer}_loaded")


def tower(nc, a, out):
    with ExitStack() as ctx:
        def sb(name, shape, dt=F32):
            return ctx.enter_context(nc.sbuf_tensor(name, shape, dt))

        def scratch(name, shape, dt=F32):
            return nc.dram_tensor(name, shape, dt, kind="Internal").ap()

        s = Stores()
        s.psum = ctx.enter_context(nc.psum_tensor("psum", [P, 8, 512], F32))
        s.h = sb("h", [P, NT, D])
        s.attn = sb("attn", [P, NT, D])
        s.ident = sb("ident", [P, P])
        s.logits = sb("logits", [P, NT, E])
        s.gate = sb("gate", [P, 2, NT])
        s.place = sb("place", [P, 2 * NT], U32)
        s.owner = sb("owner", [P, blocks_of(2) + NT], I32)
        s.qk_parts = scratch("qk_parts", [2, PARTS, B * D, S], BF16)
        s.x_rows = [scratch(f"x_rows{i}", [(blocks_of(i + 1) + i * NT) * P, D]) for i in range(2)]
        y_rows = [scratch(f"y_rows{i}", [blocks_of(i + 1) * P, D]) for i in range(2)]
        with nc.sbuf_tensor("v_nat", [P, NT, D], F32) as s.v_nat:
            embed_and_project(nc, a, s)
            softmax_attention(nc, s)
        for layer, k_top in enumerate((1, 2)):
            if layer == 1:
                relu_attention(nc, a, s)
            with expert_weights(nc, a, layer) as (s.expert_weights, s.experts_loaded):
                close_attention(nc, a, s, layer)
                route(nc, a, s, layer, k_top, s.x_rows[layer])
                experts(nc, a, s, layer, k_top, s.x_rows[layer], y_rows[layer], out)
            if layer == 0:
                mix_experts(nc, a, s, layer, k_top, y_rows[layer])


def _layouts(x, L0_tok_weight, L0_attn_W_qkv, L0_attn_b_qkv, L0_attn_W_out, L0_attn_b_out, L0_ffn_router_w,
             L0_ffn_router_b, L0_ffn_w1, L0_ffn_w2, L0_ffn_w3, L1_attn_w_qkv, L1_attn_b_qkv, L1_attn_w_proj,
             L1_attn_b_proj, L1_attn_projection, L1_ffn_w_router, L1_ffn_expert_bias, L1_ffn_Wg, L1_ffn_Wu,
             L1_ffn_Wd, L1_ffn_sg, L1_ffn_su, L1_ffn_sd):
    f = np.float32

    def rows_of(w, n):
        full = np.zeros((n * P, w.shape[-1]), f)
        full[:w.shape[0]] = w
        return np.ascontiguousarray(full.reshape(n, P, -1).transpose(1, 0, 2))

    blocks = np.zeros((3, D, D), f)
    for hd in range(H):
        at = slice(hd * HD, (hd + 1) * HD)
        for k in range(3):
            blocks[k, at, at] = L0_attn_W_qkv[hd, :, k * HD:(k + 1) * HD]
    bq, bk, bv = (np.asarray(L0_attn_b_qkv)[:, k * HD:(k + 1) * HD].reshape(D) for k in range(3))
    q1, k1, v1 = (np.asarray(L1_attn_w_qkv)[k * D:(k + 1) * D].T for k in range(3))
    bq1, bk1, bv1 = (np.asarray(L1_attn_b_qkv)[k * D:(k + 1) * D] for k in range(3))
    feat = np.zeros((H, HD, H, M_FEAT), f)
    for hd in range(H):
        feat[hd, :, hd, :] = np.asarray(L1_attn_projection).T
    feat = feat.reshape(D, H * M_FEAT)
    feat_b = np.zeros((2, P, (H - P // HD) * M_FEAT), f)
    feat_b[0, :DB] = feat[P:, P // HD * M_FEAT:]
    feat_b[1, DB:] = feat[P:, P // HD * M_FEAT:]
    wg = np.concatenate([L1_ffn_Wg, np.asarray(L1_ffn_sg)[None]]).transpose(2, 0, 1)
    wu = np.concatenate([L1_ffn_Wu, np.asarray(L1_ffn_su)[None]]).transpose(2, 0, 1)
    wd = np.concatenate([L1_ffn_Wd, np.asarray(L1_ffn_sd)[None]]).transpose(0, 2, 1)

    def cat(*rows):
        return np.ascontiguousarray(np.concatenate([np.asarray(r).reshape(-1, np.shape(rows[0])[-1]) for r in rows]))

    return {
        "ids": np.ascontiguousarray(np.asarray(x).reshape(NT, P).T),
        "table": np.ascontiguousarray(np.asarray(L0_tok_weight).T),
        "w0_qk_a": np.ascontiguousarray(blocks[:2, :P, :P].transpose(1, 0, 2)),
        "w0_qk_b": np.ascontiguousarray(np.concatenate([blocks[0, P:, P:], blocks[1, P:, P:]], 1)),
        "w0_v": cat(blocks[2], bv),
        "b0_qk": np.ascontiguousarray(np.stack([bq[:P], bk[:P], np.concatenate([bq[P:], bk[P:]])], 1)),
        "w0_out": cat(L0_attn_W_out, L0_attn_b_out),
        "w0_router": cat(L0_ffn_router_w, L0_ffn_router_b),
        "e0_up_a": np.ascontiguousarray(np.stack([np.asarray(L0_ffn_w1)[:, :P], np.asarray(L0_ffn_w2)[:, :P]]).transpose(2, 0, 1, 3)),
        "e0_up_b": np.ascontiguousarray(np.stack([np.asarray(L0_ffn_w1)[:, P:], np.asarray(L0_ffn_w2)[:, P:]]).transpose(2, 0, 1, 3)),
        "e0_down": np.ascontiguousarray(np.asarray(L0_ffn_w3).reshape(E, F0 // P, P, D).transpose(2, 0, 1, 3)),
        "w1_qk": np.ascontiguousarray(np.stack([q1[:, :P], k1[:, :P], np.concatenate([q1[:, P:], k1[:, P:]], 1)], 1)),
        "w1_v": cat(v1, bv1),
        "b1_qk": np.ascontiguousarray(np.stack([bq1[:P], bk1[:P], np.concatenate([bq1[P:], bk1[P:]])], 1)),
        "feat_a": np.ascontiguousarray(feat[:P, :P // HD * M_FEAT]),
        "feat_b": np.ascontiguousarray(feat_b.transpose(1, 0, 2)),
        "w1_out": cat(np.asarray(L1_attn_w_proj).T, L1_attn_b_proj),
        "w1_router": np.ascontiguousarray(np.asarray(L1_ffn_w_router).T),
        "b1_expert": np.ascontiguousarray(np.broadcast_to(np.asarray(L1_ffn_expert_bias), (P, E))),
        "e1_up_a": np.ascontiguousarray(np.stack([wg[:P], wu[:P]], 1)),
        "e1_up_b": np.ascontiguousarray(np.stack([wg[P:], wu[P:]], 1)),
        "e1_down": np.ascontiguousarray(wd.reshape(E + 1, F1 // P, P, D).transpose(2, 0, 1, 3)),
    }


def kernel(**inputs):
    import concourse.bacc as _bacc
    from concourse.bass_utils import run_bass_kernel_spmd as _run

    nc = _bacc.Bacc("TRN2", target_bir_lowering=False, num_devices=1)
    arrays = _layouts(**{k: np.asarray(v) for k, v in inputs.items()})
    a = {n: nc.dram_tensor(n, v.shape, mybir.dt.from_np(v.dtype), kind="ExternalInput").ap()
         for n, v in arrays.items()}
    out = nc.dram_tensor("out", [T, D], F32, kind="ExternalOutput").ap()
    tower(nc, a, out)
    r = _run(nc, [arrays], core_ids=[0])
    return r.results[0]["out"].reshape(B, S, D)
```

```python
from contextlib import ExitStack, contextmanager

import numpy as np
import concourse.bass as bass
from concourse import mybir

F32 = mybir.dt.float32
BF16 = mybir.dt.bfloat16
I32 = mybir.dt.int32
U32 = mybir.dt.uint32
ALU = mybir.AluOpType
ACT = mybir.ActivationFunctionType
AX = mybir.AxisListType

P = 128
D = 192
DB = D - P
B, S = 4, 1024
T = B * S
NT = T // P
CT = 4
CHUNK = CT * P
TB = S // P
H, HD = 12, 16
GH = 4
NG = H // GH
GD = GH * HD
E = 8
EPS = 1e-5
SCALE0 = float(D) ** -0.5
PARTS = 3
Q_STACK = (0, 0, 1, 1, 0, 2)
K_STACK = (0, 1, 0, 1, 2, 0)
SK = len(Q_STACK) * HD
M_FEAT = 64
KERNEL_EPS = 0.001
F0, F1 = 512, 384
LEAD = NT // 2
START = 1


@contextmanager
def semaphores(nc):
    taken = []

    def new_sem(name, start=START):
        taken.append(nc.alloc_semaphore(name))
        if start:
            nc.sync.sem_inc(taken[-1], start)
        return taken[-1]
    yield new_sem
    nc.clear_and_free_semaphores(taken)
    nc.all_engine_barrier()


class Chain:

    def __init__(self, eng, sem, per_turn=0, turn=0):
        self.eng, self.sem, self.base, self.n, self.per_turn = eng, sem, turn * per_turn, 0, per_turn

    def __call__(self, ins):
        self.n += 1
        ins.then_inc(self.sem, 1)
        self.eng.wait_ge(self.sem, START + self.base + self.n)


def sems(new_sem, names):
    return {n: new_sem(n) for n in names.split()}


def layer_norm_stats(nc, dve, link, tiles, stats, mv, var_eps, var_ready):
    dve.nop(nofuse=True)
    for j, tile in enumerate(tiles):
        last = nc.vector.bn_stats(stats[:, j, :], tile)
    link(last)
    dve.nop(nofuse=True)
    for j in range(len(tiles)):
        last = nc.vector.bn_aggr(mv[:, j, :], stats[:, j, :])
    link(last)
    nc.vector.tensor_scalar(var_eps, mv[:, :, 1], EPS, None, ALU.add).then_inc(var_ready, 1)


def layer_norm_apply(nc, link, tiles, normed, mv, var_eps, std, tmp):
    link(nc.vector.reciprocal(tmp, std))
    link(nc.vector.tensor_tensor(tmp, tmp, var_eps, ALU.mult))
    link(nc.vector.tensor_tensor(tmp, tmp, std, ALU.add))
    link(nc.vector.tensor_scalar(tmp, tmp, 0.5, None, ALU.mult))
    link(nc.vector.reciprocal(tmp, tmp))
    for j, tile in enumerate(tiles):
        last = nc.vector.tensor_scalar(normed[:, j, :], tile, mv[:, j, 0:1], tmp[:, j:j + 1],
                                       ALU.subtract, ALU.mult)
    return last


def pipeline(eng, turns, start, step, finish):
    start()
    step((0, 0), None, (1, 0))
    with eng.Fori(0, turns - 1) as i:
        step((1, i), (0, i), (0, i + 1))
        step((0, i + 1), (1, i), (1, i + 1))
    step((1, turns - 1), (0, turns - 1), None)
    finish()


def load_stacks(eng, s, b, g):
    for which, (stack, order) in enumerate(((s.q_stack, Q_STACK), (s.k_stack, K_STACK))):
        for k, part in enumerate(order):
            src = s.qk_parts[which, part, bass.ds(b * D + g * GD, GD), :]
            eng.dma_start(stack[k * HD:(k + 1) * HD, g, :, :],
                          src.rearrange("(s r) t -> r s t", r=HD)).then_inc(s.loaded[g], 16)


def embed_and_project(nc, a, s):
    with ExitStack() as ctx:
        new_sem = ctx.enter_context(semaphores(nc))

        def sb(name, shape, dt=F32):
            return ctx.enter_context(nc.sbuf_tensor("ep_" + name, shape, dt))

        h, v_nat, ps = s.h, s.v_nat, s.psum
        ids = sb("ids", [P, NT], I32)
        w_a = sb("w_a", [P, 2, P])
        w_b = sb("w_b", [DB, P])
        wv_a = sb("wv_a", [P, D])
        wv_b = sb("wv_b", [DB + 1, D])
        bias = sb("bias", [P, 3])
        stats = sb("stats", [P, 2, CT, 6])
        mv = sb("mv", [P, 2, CT, 2])
        var_eps = sb("var_eps", [P, 2, CT])
        std = sb("std", [P, 2, CT])
        tmp = sb("tmp", [P, 2, CT])
        xn = sb("xn", [P, 2, CT, D])
        xt_a = sb("xt_a", [P, 2, CHUNK])
        xt_b = sb("xt_b", [DB + 1, 2, CHUNK])
        full = sb("full", [P, 2, 3, CHUNK])
        rest = sb("rest", [P, 2, 3, CHUNK])
        parts = sb("parts", [P, 2, 3, PARTS, CHUNK], BF16)
        m = sems(new_sem, "ep_ids ep_weights ep_ones ep_ident ep_qk_ps ep_v_left ep_link ep_pool_link ep_rest")
        two = {n: [new_sem(f"ep_{n}{u}") for u in range(2)] for n in
               ("var", "std", "xn", "xt_ps", "xt", "v_ps", "high", "middle", "low", "sent")}
        gathered = [new_sem(f"ep_gathered{t}", start=0) for t in range(TB)]
        nc.all_engine_barrier()
        block = ctx.enter_context(nc.Block())
        PS_XA, PS_XB, PS_QK, PS_V = 0, 1, 2, 5

        @block.gpsimd
        def _(pool):
            nc.gpsimd.memset(s.ident[:], 0.0).then_inc(m["ep_pool_link"], 1)
            pool.wait_ge(m["ep_pool_link"], START + 1)
            nc.gpsimd.affine_select(out=s.ident[:], in_=s.ident[:], compare_op=ALU.not_equal, fill=1.0, base=0,
                                    pattern=[[-1, P]], channel_multiplier=1).then_inc(m["ep_ident"], 1)
            pool.wait_ge(m["ep_ids"], START + 16)
            GATHERED_AHEAD = 3
            for chunk in range(-GATHERED_AHEAD, NT // CT):
                for t in range((chunk + GATHERED_AHEAD) * CT, min((chunk + GATHERED_AHEAD + 1) * CT, NT)):
                    if t >= TB:
                        pool.wait_ge(gathered[t % TB], 16 * (t // TB))
                    pool.indirect_dma_start(out=h[:, t, :], out_offset=None, in_=a["table"],
                                            in_offset=bass.IndirectOffsetOnAxis(ap=ids[:, t:t + 1], axis=0)
                                            ).then_inc(gathered[t % TB], 16)
                for r in range(3 if chunk >= 0 else 0):
                    k, u = divmod(chunk, 2)
                    pool.wait_ge(two["middle"][u], START + 3 * k + r + 1)
                    nc.gpsimd.tensor_tensor(parts[:, u, r, 2, :], rest[:, u, r, :], parts[:, u, r, 1, :],
                                            ALU.subtract).then_inc(two["low"][u], 1)

        @block.sync
        def _(sp):
            sp.dma_start(ids[:], a["ids"]).then_inc(m["ep_ids"], 16)
            for dst, src in ((w_a[:], a["w0_qk_a"]), (w_b[:], a["w0_qk_b"]), (wv_a[:], a["w0_v"][0:P, :]),
                             (wv_b[:], a["w0_v"][P:D + 1, :]), (bias[:], a["b0_qk"])):
                sp.dma_start(dst, src).then_inc(m["ep_weights"], 16)
            with sp.Fori(0, B) as b:
                for u in range(2):
                    sp.wait_ge(two["low"][u], START + 3 * (b + 1))
                    cols = slice(u * CHUNK, (u + 1) * CHUNK)
                    for r, (src, which, row) in enumerate(((slice(0, P), 0, 0), (slice(0, P), 1, 0),
                                                           (slice(0, DB), 0, P), (slice(DB, P), 1, P))):
                        n = src.stop - src.start
                        dst = s.qk_parts[which, :, bass.ds(b * D + row, n), cols]
                        sp.dma_start(dst.rearrange("c r t -> r c t"),
                                     parts[src, u, min(r, 2), :, :]).then_inc(two["sent"][u], 16)
            for u in range(2):
                sp.wait_ge(two["sent"][u], START + 4 * 16 * B)

        @block.vector
        def _(dve):
            nc.vector.memset(xt_b[DB:DB + 1, :, :], 1.0).then_inc(m["ep_ones"], 1)

            def tiles_of(u, k):
                return [h[:, k * TB + (u * CT + j), :] for j in range(CT)]

            def chain(u, k):
                return Chain(dve, m["ep_link"], 7, 2 * k + u)

            def statistics(u, k, link):
                for j in range(CT):
                    dve.wait_ge(gathered[u * CT + j], 16 * (k + 1))
                layer_norm_stats(nc, dve, link, tiles_of(u, k), stats[:, u], mv[:, u], var_eps[:, u], two["var"][u])

            def normalise(u, k, link):
                dve.wait_ge(two["std"][u], START + k + 1)
                dve.wait_ge(two["xt_ps"][u], START + k)
                layer_norm_apply(nc, link, tiles_of(u, k), xn[:, u], mv[:, u], var_eps[:, u], std[:, u],
                                 tmp[:, u]).then_inc(two["xn"][u], 1)

            def split(u, k, r):
                dve.wait_ge(two["high"][u], START + 3 * k + r + 1)
                dve.wait_ge(two["low"][u], START + 3 * k)
                nc.vector.tensor_tensor(rest[:, u, r, :], full[:, u, r, :], parts[:, u, r, 0, :],
                                        ALU.subtract).then_inc(m["ep_rest"], 1)
                dve.wait_ge(m["ep_rest"], START + 3 * (2 * k + u) + r + 1)
                nc.vector.tensor_copy(parts[:, u, r, 1, :], rest[:, u, r, :]).then_inc(two["middle"][u], 1)

            def start():
                link = chain(0, 0)
                statistics(0, 0, link)
                normalise(0, 0, link)

            def step(this, prev, nxt):
                u, k = this
                if nxt:
                    link = chain(*nxt)
                    statistics(*nxt, link)
                split(u, k, 0)
                if nxt:
                    normalise(*nxt, link)
                for half in range(2):
                    dve.wait_ge(two["v_ps"][u], START + 2 * k + half + 1)
                    nc.vector.tensor_copy(v_nat[:, bass.ds(k * TB + u * CT + 2 * half, 2), :],
                                          ps[:, PS_V + half, 0:2 * D].rearrange("p (t d) -> p t d", d=D)
                                          ).then_inc(m["ep_v_left"], 1)
                split(u, k, 1)
                split(u, k, 2)
            pipeline(dve, B, start, step, lambda: None)

        @block.scalar
        def _(act):
            act.wait_ge(m["ep_weights"], START + 80)
            act.wait_ge(m["ep_ones"], START + 1)

            def root(u, k):
                act.wait_ge(two["var"][u], START + k + 1)
                nc.scalar.activation(std[:, u], var_eps[:, u], ACT.Sqrt).then_inc(two["std"][u], 1)

            def copy_xt(u, k):
                act.wait_ge(two["xt_ps"][u], START + k + 1)
                act.wait_ge(two["v_ps"][u], START + 2 * k)
                nc.scalar.copy(xt_a[:, u, :], ps[:, PS_XA, :]).then_inc(two["xt"][u], 1)
                nc.scalar.copy(xt_b[0:DB, u, :], ps[0:DB, PS_XB, :]).then_inc(two["xt"][u], 1)

            def start():
                root(0, 0)
                copy_xt(0, 0)

            def step(this, prev, nxt):
                u, k = this
                for r in range(3):
                    act.wait_ge(m["ep_qk_ps"], START + 3 * (2 * k + u) + r + 1)
                    act.wait_ge(two["middle"][u], START + 3 * k)
                    act.wait_ge(two["sent"][u], START + 64 * k)
                    nc.scalar.activation(full[:, u, r, :], ps[:, PS_QK + r, :], ACT.Identity, bias=bias[:, r:r + 1])
                    nc.scalar.activation(parts[:, u, r, 0, :], ps[:, PS_QK + r, :], ACT.Identity,
                                         bias=bias[:, r:r + 1]).then_inc(two["high"][u], 1)
                    if nxt and r == 0:
                        root(*nxt)
                if nxt:
                    copy_xt(*nxt)
            def finish():
                for u in range(2):
                    act.wait_ge(two["sent"][u], START + 64)
                load_stacks(act, s, 0, 0)
            pipeline(act, B, start, step, finish)

        @block.tensor
        def _(pe):
            pe.wait_ge(m["ep_ident"], START + 1)
            pe.wait_ge(m["ep_weights"], START + 80)
            pe.wait_ge(m["ep_ones"], START + 1)

            def transpose(u, k, prev):
                pe.wait_ge(two["xn"][u], START + k + 1)
                if prev:
                    pe.wait_ge(two["xt"][prev[0]], START + 2 * (prev[1] + 1))
                for j in range(CT):
                    nc.tensor.transpose(ps[:, PS_XA, j * P:(j + 1) * P], xn[:, u, j, 0:P], s.ident[:])
                    last = nc.tensor.transpose(ps[0:DB, PS_XB, j * P:(j + 1) * P], xn[:, u, j, P:D], s.ident[:])
                last.then_inc(two["xt_ps"][u], 1)

            def step(this, prev, nxt):
                u, k = this
                pe.wait_ge(two["xt"][u], START + 2 * (k + 1))
                for r in range(3):
                    if prev:
                        pe.wait_ge(two["high"][prev[0]], START + 3 * prev[1] + r + 1)
                    if r < 2:
                        last = nc.tensor.matmul(ps[:, PS_QK + r, :], w_a[:, r, :], xt_a[:, u, :], start=True, stop=True)
                    else:
                        last = nc.tensor.matmul(ps[:, PS_QK + r, :], w_b[:], xt_b[0:DB, u, :], start=True, stop=True)
                    last.then_inc(m["ep_qk_ps"], 1)
                for half in range(2):
                    pe.wait_ge(m["ep_v_left"], START + 2 * (2 * k + u))
                    for j in range(2):
                        toks = slice((2 * half + j) * P, (2 * half + j + 1) * P)
                        dst = ps[:, PS_V + half, j * D:(j + 1) * D]
                        nc.tensor.matmul(dst, xt_a[:, u, toks], wv_a[:], start=True, stop=False)
                        last = nc.tensor.matmul(dst, xt_b[:, u, toks], wv_b[:], start=False, stop=True)
                    last.then_inc(two["v_ps"][u], 1)
                if nxt:
                    transpose(*nxt, this)
            pipeline(pe, B, lambda: transpose(0, 0, None), step, lambda: None)


def softmax_attention(nc, s):
    with ExitStack() as ctx:
        new_sem = ctx.enter_context(semaphores(nc))

        def sb(name, shape, dt=F32):
            return ctx.enter_context(nc.sbuf_tensor("sa_" + name, shape, dt))

        ps, v_nat, attn = s.psum, s.v_nat, s.attn
        HALF = 512
        SLOTS = 3
        OUT = 4 + SLOTS
        STEPS = 2 * TB
        W = 32
        IT = HALF // P
        qst, kst, loaded = s.q_stack, s.k_stack, s.loaded
        v_ext = sb("v_ext", [P, NG, TB, GH, W])
        probs = sb("probs", [P, 2, GH, HALF])
        out_t = sb("out_t", [P, 2, HALF])
        half_max = sb("half_max", [P, NG, GH, TB, 2])
        row_max = sb("row_max", [P, NG, GH, TB])
        max_rows = sb("max_rows", [HD, NG, 2, P], BF16)
        inv = sb("inv", [P, 2, IT, GH])
        max_dram = nc.dram_tensor("max_rows_dram", [NG, GH * TB, P], BF16, kind="Internal").ap()

        def per_group(name):
            return [new_sem(f"sa_{name}{g}") for g in range(NG)]

        max_stored, max_loaded, v_ready = map(per_group, ("max_stored", "max_loaded", "v_ready"))
        scores_done, exp_done, pv_done, max_done = map(per_group, ("scores_done", "exp_done", "pv_done", "max_done"))
        ring_full = [new_sem(f"sa_ring_full{r}") for r in range(SLOTS)]
        ring_free = [new_sem(f"sa_ring_free{r}") for r in range(SLOTS)]
        out_copied = [new_sem(f"sa_out_copied{r}") for r in range(2)]
        zeros = sb("zeros", [P, D])
        zeroed, zeros_stored = (new_sem("sa_" + n) for n in ("zeroed", "zeros_stored"))
        inv_done, v_init, ones_row = (new_sem("sa_" + n)
                                      for n in ("inv_done", "v_init", "ones_row"))
        LOADS = 2 * len(Q_STACK)
        nc.all_engine_barrier()
        block = ctx.enter_context(nc.Block())

        def max_units(g, first, last):
            return [("max", g, k // (2 * TB), k // 2 % TB, k % 2) for k in range(first, last)]

        UNITS = GH * TB * 2
        AHEAD = 5
        PER = UNITS // STEPS
        before = max_units(0, 0, UNITS) + [("rows", 0, 0), ("rows", 0, 1)] + max_units(1, 0, AHEAD * PER)

        def step_units(g, st, last):
            n1, n2 = g + 1, g + 2
            split, tail = [], []
            if st < STEPS - AHEAD:
                if not (last and n1 >= NG):
                    split = max_units(n1 % NG, (AHEAD + st) * PER, (AHEAD + st + 1) * PER)
            elif not (last and n2 >= NG):
                k = st - (STEPS - AHEAD)
                split = max_units(n2 % NG, k * PER, (k + 1) * PER)
            if st == 1 and g > 0:
                tail.append(("out", g - 1, 1))
            if st == TB + 1:
                tail.append(("out", g, 0))
            if st == STEPS - AHEAD + 1 and not (last and n1 >= NG):
                tail += [("rows", n1 % NG, 0), ("rows", n1 % NG, 1)]
            if st == STEPS - 1 and g == NG - 1:
                tail.append(("out", g, 1))
            return split, tail

        def order(last):
            return [u for g in range(NG) for st in range(STEPS) for part in step_units(g, st, last) for u in part]

        RING0 = len(before)
        RING = len(order(False))
        assert RING % SLOTS == 0
        place = {last: {u: n for n, u in enumerate(order(last))} for last in (False, True)}

        def turns(eng, body):
            with eng.Fori(0, B - 1) as b:
                body(b, False)
            body(B - 1, True)

        def uses(b, n):
            return (RING0 + n) % SLOTS, RING // SLOTS * b + (RING0 + n) // SLOTS

        def load_max(sp, g, b):
            sp.dma_start(max_dram[g].rearrange("(u k) t -> k u t", u=2), max_rows[:, g, :, :]).then_inc(max_stored[g], 16)
            sp.wait_ge(max_stored[g], START + 16 * (b + 1))
            sp.dma_start(qst[SK:SK + 1, g, :, :].rearrange("o s t -> o (s t)"),
                         max_dram[g].rearrange("(o k) t -> o (k t)", o=1)).then_inc(max_loaded[g], 16)

        @block.sync
        def _(sp):
            for g in range(1, NG):
                load_stacks(sp, s, 0, g)
            for n in (UNITS, UNITS + 1):
                sp.wait_ge(ring_free[n % SLOTS], START + n // SLOTS + 1)
            load_max(sp, 0, 0)
            sp.wait_ge(zeroed, START + 1)
            for x_rows, n in zip(s.x_rows, (blocks_of(1), blocks_of(2))):
                sp.dma_start(x_rows[0:n * P, :].rearrange("(n p) d -> p n d", p=P),
                             zeros[:].unsqueeze(1).to_broadcast([P, n, D])).then_inc(zeros_stored, 16)

            def sequence(b, last):
                for g in range(NG):
                    if not (last and g == NG - 1):
                        n1, b1 = ((g + 1) % NG, b + (g + 1) // NG)
                        for half in range(2):
                            r, k = uses(b, place[last][("rows", n1, half)])
                            sp.wait_ge(ring_free[r], START + k + 1)
                            sp.nop(nofuse=True)
                        load_max(sp, n1, b1)
                    if not last:
                        sp.wait_ge(scores_done[g], START + 2 * STEPS * (b + 1))
                        load_stacks(sp, s, b + 1, g)
            turns(sp, sequence)
            sp.wait_ge(zeros_stored, START + 32)

        @block.gpsimd
        def _(pool):
            nc.gpsimd.memset(v_ext[:], 0.0).then_inc(v_init, 1)
            pool.wait_ge(v_init, START + 1)
            nc.gpsimd.memset(v_ext[:, :, :, :, HD:HD + 1], 1.0).then_inc(v_init, 1)
            pool.wait_ge(v_init, START + 2)
            nc.gpsimd.memset(kst[SK:SK + 1, :, :, :], 1.0).then_inc(ones_row, 1)
            pool.wait_ge(ones_row, START + 1)
            with pool.Fori(0, B) as b:
                for g in range(NG):
                    pool.wait_ge(pv_done[g], START + STEPS * b)
                    src = v_nat[:, bass.ds(b * TB, TB), g * GD:(g + 1) * GD]
                    nc.gpsimd.tensor_copy(v_ext[:, g, :, :, 0:HD], src.rearrange("p t (s d) -> p t s d", s=GH)
                                          ).then_inc(v_ready[g], 1)

        @block.vector
        def _(dve):
            def consume(b, n, unit, r, k):
                kind, g = unit[0], unit[1]
                slot = ps[:, 4 + r, :]
                dve.wait_ge(ring_full[r], START + k + 1)
                if kind == "max":
                    hd, qt, half = unit[2:]
                    nc.vector.tensor_reduce(half_max[:, g, hd, qt, half:half + 1], slot, AX.X,
                                            ALU.max).then_inc(ring_free[r], 1)
                elif kind == "rows":
                    nc.vector.tensor_scalar(max_rows[:, g, unit[2], :], slot[0:HD, 0:P], -1.0, None,
                                            ALU.mult).then_inc(ring_free[r], 1)
                else:
                    half = unit[2]
                    heads = slot.rearrange("p (i s w) -> p i s w", s=GH, w=W)
                    nc.vector.reciprocal(inv[:, half], heads[:, :, :, HD]).then_inc(inv_done, 1)
                    dve.wait_ge(inv_done, START + b * 2 * NG + 2 * g + half + 1)
                    dst = attn[:, bass.ds(b * TB + half * IT, IT), g * GD:(g + 1) * GD]
                    nc.vector.tensor_tensor(dst.rearrange("p i (s d) -> p i s d", s=GH), heads[:, :, :, 0:HD],
                                            inv[:, half].unsqueeze(3).to_broadcast([P, IT, GH, HD]),
                                            ALU.mult).then_inc(ring_free[r], 1)

            def combine(g, turn, n):
                for i in range(n - SLOTS + 1, n + 1):
                    r, k = turn(i)
                    dve.wait_ge(ring_free[r], START + k + 1)
                nc.vector.tensor_tensor(row_max[:, g], half_max[:, g, :, :, 0], half_max[:, g, :, :, 1],
                                        ALU.max).then_inc(max_done[g], 1)

            nc.vector.memset(zeros[:], 0.0).then_inc(zeroed, 1)
            for n, unit in enumerate(before):
                if unit[0] == "rows" and unit[2] == 0:
                    combine(unit[1], lambda i: (i % SLOTS, i // SLOTS), n - 1)
                consume(0, n, unit, n % SLOTS, n // SLOTS)

            def sequence(b, last):
                units = order(last)
                newest = {unit[1]: max(i for i, u in enumerate(units[:n]) if u[:2] == ("max", unit[1]))
                          for n, unit in enumerate(units) if unit[0] == "rows"}
                combine_at = {g: min(last_max + SLOTS, place[last][("rows", g, 0)]) for g, last_max in newest.items()}
                for n, unit in enumerate(units):
                    r, k = uses(b, n)
                    for g, last_max in newest.items():
                        if n == combine_at[g]:
                            combine(g, lambda i: uses(b, i), last_max)
                    if unit[0] == "rows":
                        dve.wait_ge(max_stored[unit[1]], START + 16 * (b + 1 if unit[1] == 0 else b))
                    consume(b, n, unit, r, k)
            turns(dve, sequence)

        @block.scalar
        def _(act):
            def exps(b, g, st):
                for pair in range(2):
                    act.wait_ge(scores_done[g], START + 2 * STEPS * b + 2 * st + pair + 1)
                    if pair == 0:
                        if st >= 2:
                            act.wait_ge(pv_done[g], START + STEPS * b + st - 1)
                        elif g > 0:
                            act.wait_ge(pv_done[g - 1], START + STEPS * b + STEPS - 1 + st)
                        else:
                            act.wait_ge(pv_done[NG - 1], START + STEPS * b)
                    nc.scalar.activation(probs[:, st % 2, 2 * pair:2 * pair + 2, :], ps[:, 2 * pair:2 * pair + 2, :],
                                         ACT.Exp, scale=SCALE0).then_inc(exp_done[g], 1)

            def copy_out(b, g, half, last):
                act.wait_ge(pv_done[g], START + STEPS * b + TB * (half + 1))
                k_half = 2 * g + half
                if k_half >= 2:
                    r, k = uses(b, place[last][("out", g - 1, half)])
                else:
                    r, k = uses(b - 1, place[False][("out", NG - 1, half)])
                act.wait_ge(ring_full[r], START + k + 1)
                nc.scalar.copy(out_t[:, half, :], ps[:, OUT, :]).then_inc(out_copied[half], 1)

            def sequence(b, last):
                for g in range(NG):
                    for st in range(STEPS):
                        exps(b, g, st)
                        if st == 0 and g > 0:
                            copy_out(b, g - 1, 1, last)
                        if st == TB:
                            copy_out(b, g, 0, last)
                copy_out(b, NG - 1, 1, last)
            turns(act, sequence)

        @block.tensor
        def _(pe):
            def scores(b, g, st, pair, follows):
                half, kt = st // TB, st % TB
                if pair == 0 and st == 0:
                    pe.wait_ge(loaded[g], START + 16 * LOADS * (b + 1))
                    pe.wait_ge(max_loaded[g], START + 16 * (b + 1))
                if follows is not None:
                    pe.wait_ge(exp_done[follows[0]], START + follows[1] + pair + 1)
                for hd in (2 * pair, 2 * pair + 1):
                    last = nc.tensor.matmul(ps[:, hd, :], kst[:, g, hd, kt * P:(kt + 1) * P],
                                            qst[:, g, hd, half * HALF:(half + 1) * HALF], start=True, stop=True)
                last.then_inc(scores_done[g], 1)

            def produce(b, unit, r, k):
                kind, g = unit[0], unit[1]
                pe.wait_ge(ring_free[r], START + k)
                if kind == "max":
                    hd, qt, half = unit[2:]
                    last = nc.tensor.matmul(ps[:, 4 + r, :], qst[0:SK, g, hd, qt * P:(qt + 1) * P],
                                            kst[0:SK, g, hd, half * 512:(half + 1) * 512], start=True, stop=True)
                elif kind == "rows":
                    heads = row_max[:, g].rearrange("p s t -> p (s t)")
                    last = nc.tensor.transpose(ps[0:HD, 4 + r, 0:P], heads[:, unit[2] * HD:(unit[2] + 1) * HD],
                                               s.ident[:])
                else:
                    half = unit[2]
                    pe.wait_ge(out_copied[half], START + NG * b + g + 1)
                    for i in range(IT):
                        last = nc.tensor.transpose(ps[:, 4 + r, i * P:(i + 1) * P],
                                                   out_t[:, half, i * P:(i + 1) * P], s.ident[:])
                last.then_inc(ring_full[r], 1)

            def times_v(b, g, st):
                half, kt = st // TB, st % TB
                if st == 0:
                    pe.wait_ge(v_ready[g], START + b + 1)
                if kt == 0:
                    pe.wait_ge(out_copied[1 - half], START + NG * b + g + half)
                pe.wait_ge(exp_done[g], START + 2 * STEPS * b + 2 * st + 2)
                for hd in range(GH):
                    last = nc.tensor.matmul(ps[hd * W:(hd + 1) * W, OUT, :], v_ext[:, g, kt, hd, :],
                                            probs[:, st % 2, hd, :], start=(kt == 0), stop=(kt == TB - 1))
                last.then_inc(pv_done[g], 1)

            for n, unit in enumerate(before):
                if unit[0] == "max" and unit[2:] == (0, 0, 0):
                    pe.wait_ge(loaded[unit[1]], START + 16 * LOADS)
                if unit[0] == "rows":
                    pe.wait_ge(max_done[unit[1]], START + 1)
                produce(0, unit, n % SLOTS, n // SLOTS)
            pe.wait_ge(ones_row, START + 1)
            for pair in range(2):
                scores(0, 0, 0, pair, None)

            ORDER = ("scores", "maxima", "scores", "maxima", "maxima", "outputs", "maxima")

            def sequence(b, last):
                n = 0
                for g in range(NG):
                    for st in range(STEPS):
                        split, tail = step_units(g, st, last)
                        final = last and g == NG - 1 and st == STEPS - 1
                        nb, ng, nst = (b, g, st + 1) if st + 1 < STEPS else (b + (g + 1) // NG, (g + 1) % NG, 0)
                        pair, left = 0, list(split)
                        for what in ORDER:
                            if what == "scores":
                                if not final:
                                    scores(nb, ng, nst, pair, (g, 2 * STEPS * b + 2 * st))
                                pair += 1
                            elif what == "outputs":
                                times_v(b, g, st)
                            elif left:
                                unit = left.pop(0)
                                ug = unit[1]
                                if unit[2:] == (0, 0, 0):
                                    pe.wait_ge(loaded[ug], START + 16 * LOADS * ((b if ug > g else b + 1) + 1))
                                produce(b, unit, *uses(b, n))
                                n += 1
                        for unit in tail:
                            if unit[0] == "rows":
                                pe.wait_ge(max_done[unit[1]], START + (b + 1 if unit[1] == 0 else b) + 1)
                            produce(b, unit, *uses(b, n))
                            n += 1
            turns(pe, sequence)


def close_attention(nc, a, s, layer):
    with ExitStack() as ctx:
        new_sem = ctx.enter_context(semaphores(nc))

        def sb(name, shape, dt=F32):
            return ctx.enter_context(nc.sbuf_tensor(f"ca{layer}_" + name, shape, dt))

        h, attn, ps = s.h, s.attn, s.psum
        router = a[f"w{layer}_router"]
        RB = router.shape[0] - P
        wo_a = sb("wo_a", [P, D])
        wo_b = sb("wo_b", [DB + 1, D])
        wr_a = sb("wr_a", [P, E])
        wr_b = sb("wr_b", [RB, E])
        rows = sb("rows", [P, 2, CT, D])
        rows_ta = sb("rows_ta", [P, 2, CHUNK])
        rows_tb = sb("rows_tb", [DB + 1, 2, CHUNK])
        x2 = sb("x2", [P, 2, CT, D])
        x2_ta = sb("x2_ta", [P, 2, CHUNK])
        x2_tb = sb("x2_tb", [DB + 1, 2, CHUNK])
        stats = sb("stats", [P, 2, CT, 6])
        mv = sb("mv", [P, 2, CT, 2])
        var_eps = sb("var_eps", [P, 2, CT])
        std = sb("std", [P, 2, CT])
        tmp = sb("tmp", [P, 2, CT])
        weights, ones, chain = (new_sem(f"ca{layer}_{n}") for n in ("weights", "ones", "chain"))
        two = {n: [new_sem(f"ca{layer}_{n}{u}") for u in range(2)] for n in
               ("rows", "rows_ps", "rows_act", "out_ps", "var", "std", "x2", "x2_ps", "x2_act", "x2_dve",
                "logits_ps", "logits", "kept", "added")}
        nc.all_engine_barrier()
        block = ctx.enter_context(nc.Block())
        PS_A, PS_B, PS_O, PS_XA, PS_XB, PS_L = 0, 1, 2, 4, 5, 6

        @block.sync
        def _(sp):
            for dst, src in ((wo_a[:], a[f"w{layer}_out"][0:P, :]), (wo_b[:], a[f"w{layer}_out"][P:D + 1, :]),
                             (wr_a[:], router[0:P, :]), (wr_b[:], router[P:, :])):
                sp.dma_start(dst, src).then_inc(weights, 16)
            for dst, src in s.expert_weights:
                sp.dma_start(dst, src).then_inc(s.experts_loaded, 16)

        def before(sem, u, k):
            return (sem[1], START + k) if u == 0 else (sem[0], START + k + 1)

        def tiles_of(chunk, first=0, n=CT):
            u, k = chunk
            return bass.ds(k * TB + (u * CT + first), n)

        @block.gpsimd
        def _(pool):
            def take(u, k):
                pool.wait_ge(two["rows_ps"][u], START + k)
                pool.nop(nofuse=True)
                nc.gpsimd.tensor_copy(rows[:, u], attn[:, tiles_of((u, k)), :]).then_inc(two["rows"][u], 1)
                pool.wait_ge(two["rows"][u], START + k + 1)

            def keep(u, k):
                pool.wait_ge(two["x2"][u], START + k + 1)
                pool.nop(nofuse=True)
                nc.gpsimd.tensor_copy(attn[:, tiles_of((u, k)), :], x2[:, u]).then_inc(two["kept"][u], 1)

            def step(this, prev, nxt):
                if nxt:
                    take(*nxt)
                if prev:
                    keep(*prev)

            pipeline(pool, B, lambda: take(0, 0), step, lambda: keep(1, B - 1))

        @block.vector
        def _(dve):
            nc.vector.memset(rows_tb[DB:DB + 1, :, :], 1.0).then_inc(ones, 1)
            nc.vector.memset(x2_tb[DB:DB + 1, :, :], 1.0).then_inc(ones, 1)

            def copy_x2(u, k):
                dve.wait_ge(two["x2_ps"][u], START + k + 1)
                dve.wait_ge(two["logits_ps"][u], START + k)
                nc.vector.tensor_copy(x2_tb[0:DB, u, :], ps[0:DB, PS_XB, :]).then_inc(two["x2_dve"][u], 1)

            def copy_logits(u, k):
                dve.wait_ge(two["logits_ps"][u], START + k + 1)
                nc.vector.tensor_copy(s.logits[:, tiles_of((u, k)), :],
                                      ps[:, PS_L, 0:CT * E].rearrange("p (t e) -> p t e", e=E)
                                      ).then_inc(two["logits"][u], 1)

            def step(this, prev, nxt):
                u, k = this
                link = Chain(dve, chain, 7, 2 * k + u)
                for half in range(2):
                    dve.wait_ge(two["out_ps"][u], START + 2 * k + half + 1)
                    tiles = h[:, tiles_of(this, 2 * half, 2), :]
                    nc.vector.tensor_tensor(tiles, tiles, ps[:, PS_O + half, 0:2 * D].rearrange(
                        "p (t d) -> p t d", d=D), ALU.add).then_inc(two["added"][u], 1)
                if prev:
                    copy_x2(*prev)
                dve.wait_ge(two["added"][u], START + 2 * k + 2)
                tiles = [h[:, k * TB + (u * CT + j), :] for j in range(CT)]
                layer_norm_stats(nc, dve, link, tiles, stats[:, u], mv[:, u], var_eps[:, u], two["var"][u])
                dve.wait_ge(two["std"][u], START + k + 1)
                dve.wait_ge(two["x2_ps"][u], START + k)
                dve.wait_ge(two["kept"][u], START + k)
                layer_norm_apply(nc, link, tiles, x2[:, u], mv[:, u], var_eps[:, u], std[:, u],
                                 tmp[:, u]).then_inc(two["x2"][u], 1)
                if prev:
                    copy_logits(*prev)

            def finish():
                copy_x2(1, B - 1)
                copy_logits(1, B - 1)
            pipeline(dve, B, lambda: None, step, finish)

        @block.scalar
        def _(act):
            def copy_rows(u, k):
                act.wait_ge(two["rows_ps"][u], START + k + 1)
                act.wait_ge(two["out_ps"][u], START + 2 * k)
                nc.scalar.copy(rows_ta[:, u, :], ps[:, PS_A, :]).then_inc(two["rows_act"][u], 1)
                nc.scalar.copy(rows_tb[0:DB, u, :], ps[0:DB, PS_B, :]).then_inc(two["rows_act"][u], 1)

            def copy_x2(u, k):
                act.wait_ge(two["x2_ps"][u], START + k + 1)
                act.wait_ge(two["logits_ps"][u], START + k)
                nc.scalar.copy(x2_ta[:, u, :], ps[:, PS_XA, :]).then_inc(two["x2_act"][u], 1)

            def step(this, prev, nxt):
                u, k = this
                if prev:
                    copy_x2(*prev)
                if nxt:
                    copy_rows(*nxt)
                act.wait_ge(two["var"][u], START + k + 1)
                nc.scalar.activation(std[:, u], var_eps[:, u], ACT.Sqrt).then_inc(two["std"][u], 1)

            def start():
                act.wait_ge(ones, START + 2)
                copy_rows(0, 0)
            pipeline(act, B, start, step, lambda: copy_x2(1, B - 1))

        @block.tensor
        def _(pe):
            pe.wait_ge(weights, START + 64)
            pe.wait_ge(ones, START + 2)

            def transposes(src, bank_a, bank_b):
                for j in range(CT):
                    nc.tensor.transpose(ps[:, bank_a, j * P:(j + 1) * P], src[:, j, 0:P], s.ident[:])
                    last = nc.tensor.transpose(ps[0:DB, bank_b, j * P:(j + 1) * P], src[:, j, P:D], s.ident[:])
                return last

            def transpose_rows(u, k):
                pe.wait_ge(two["rows"][u], START + k + 1)
                sem, done = two["rows_act"], 2 * k if u == 0 else 2 * (k + 1)
                pe.wait_ge(sem[1 - u], START + done)
                transposes(rows[:, u], PS_A, PS_B).then_inc(two["rows_ps"][u], 1)

            def transpose_x2(u, k):
                pe.wait_ge(two["x2"][u], START + k + 1)
                pe.wait_ge(*before(two["x2_act"], u, k))
                pe.wait_ge(*before(two["x2_dve"], u, k))
                transposes(x2[:, u], PS_XA, PS_XB).then_inc(two["x2_ps"][u], 1)

            def project_out(u, k):
                pe.wait_ge(two["rows_act"][u], START + 2 * (k + 1))
                pe.wait_ge(two["added"][1 - u], START + 2 * (k + u))
                for half in range(2):
                    for j in range(2):
                        toks = slice((2 * half + j) * P, (2 * half + j + 1) * P)
                        dst = ps[:, PS_O + half, j * D:(j + 1) * D]
                        nc.tensor.matmul(dst, rows_ta[:, u, toks], wo_a[:], start=True, stop=False)
                        last = nc.tensor.matmul(dst, rows_tb[:, u, toks], wo_b[:], start=False, stop=True)
                    last.then_inc(two["out_ps"][u], 1)

            def compute_logits(u, k):
                pe.wait_ge(two["x2_act"][u], START + k + 1)
                pe.wait_ge(two["x2_dve"][u], START + k + 1)
                pe.wait_ge(*before(two["logits"], u, k))
                for j in range(CT):
                    toks = slice(j * P, (j + 1) * P)
                    dst = ps[:, PS_L, j * E:(j + 1) * E]
                    nc.tensor.matmul(dst, x2_ta[:, u, toks], wr_a[:], start=True, stop=False)
                    last = nc.tensor.matmul(dst, x2_tb[0:RB, u, toks], wr_b[:], start=False, stop=True)
                last.then_inc(two["logits_ps"][u], 1)

            def step(this, prev, nxt):
                project_out(*this)
                if prev:
                    transpose_x2(*prev)
                if nxt:
                    transpose_rows(*nxt)
                if prev:
                    compute_logits(*prev)

            def finish():
                transpose_x2(1, B - 1)
                compute_logits(1, B - 1)
            pipeline(pe, B, lambda: transpose_rows(0, 0), step, finish)


def blocks_of(k):
    n = k * NT + E - 1
    return n + n % 2


def route(nc, a, s, layer, k_top, x_rows):
    with ExitStack() as ctx:
        new_sem = ctx.enter_context(semaphores(nc))

        def sb(name, shape, dt=F32):
            return ctx.enter_context(nc.sbuf_tensor(f"ro{layer}_" + name, shape, dt))

        NBLK, KT = blocks_of(k_top), k_top * NT
        BEFORE = LEAD * layer
        ps = s.psum
        before_me = sb("before_me", [P, P])
        all_ones = sb("all_ones", [P, P])
        expert_i = sb("expert_i", [P, E], I32)
        block_i = sb("block_i", [P, NBLK], I32)
        expert_f = sb("expert_f", [P, E])
        block_f = sb("block_f", [P, NBLK])
        bias = sb("bias", [P, E])
        top = sb("top", [P, NT])
        shifted = sb("shifted", [P, NT, E])
        exps = sb("exps", [P, NT, E])
        total = sb("total", [P, NT])
        scores = sb("scores", [P, NT, E])
        choice = sb("choice", [P, NT, E])
        best = sb("best", [P, NT, 8])
        best_i = sb("best_i", [P, NT, 8], U32)
        best_f = sb("best_f", [P, NT, 8])
        chosen = sb("chosen", [P, k_top, NT, E])
        tile_sum = sb("tile_sum", [P, KT, E])
        run_sum = sb("run_sum", [P, E, KT])
        count_i = sb("count_i", [P, E], I32)
        n_blocks = sb("n_blocks", [P, E])
        end_block = sb("end_block", [P, E])
        start_row = sb("start_row", [P, E])
        place = sb("place", [P, KT, E])
        place_f = sb("place_f", [P, KT])
        reached = sb("reached", [P, NBLK, E])
        owner = sb("owner", [P, NBLK + 2 * BEFORE])
        picked = sb("picked", [P, NT, E])
        weight_sum = sb("weight_sum", [P, NT])
        m = {n: new_sem(f"ro{layer}_{n}") for n in
             ("chain", "ones", "iota", "shifted", "exps", "chosen", "ranks", "bias", "sent")}
        nc.all_engine_barrier()
        block = ctx.enter_context(nc.Block())

        @block.sync
        def _(sp):
            if layer == 1:
                sp.dma_start(bias[:], a["b1_expert"]).then_inc(m["bias"], 16)
                sp.dma_start(x_rows[NBLK * P:, :].rearrange("(t p) d -> p t d", p=P), s.attn[:]
                             ).then_inc(m["sent"], 16)
                sp.wait_ge(m["sent"], START + 16)

        @block.gpsimd
        def _(pool):
            nc.gpsimd.iota(expert_i[:], [[1, E]], base=0, channel_multiplier=0).then_inc(m["iota"], 1)
            nc.gpsimd.iota(block_i[:], [[1, NBLK]], base=0, channel_multiplier=0).then_inc(m["iota"], 1)
            nc.gpsimd.memset(all_ones[:], 1.0).then_inc(m["ones"], 1)
            pool.wait_ge(m["ones"], START + 1)
            nc.gpsimd.affine_select(out=before_me[:], in_=all_ones[:], compare_op=ALU.is_gt, fill=0.0, base=0,
                                    pattern=[[1, P]], channel_multiplier=-1).then_inc(m["ones"], 1)

        @block.tensor
        def _(pe):
            pe.wait_ge(m["ones"], START + 2)
            pe.wait_ge(m["chosen"], START + k_top)
            flat = chosen[:].rearrange("p k t e -> p (k t e)")
            nc.tensor.matmul(ps[:, 0, 0:KT * E], before_me[:], flat, start=True, stop=True)
            nc.tensor.matmul(ps[:, 1, 0:KT * E], all_ones[:], flat, start=True, stop=True).then_inc(m["ranks"], 1)

        @block.scalar
        def _(act):
            act.wait_ge(m["shifted"], START + 1)
            nc.scalar.activation(exps[:], shifted[:], ACT.Exp).then_inc(m["exps"], 1)

        @block.vector
        def _(dve):
            link = Chain(dve, m["chain"])

            def over(x, shape):
                return x.to_broadcast(shape)

            te = [P, NT, E]
            link(nc.vector.tensor_reduce(top[:], s.logits[:], AX.X, ALU.max))
            nc.vector.tensor_tensor(shifted[:], s.logits[:], over(top[:].unsqueeze(2), te),
                                    ALU.subtract).then_inc(m["shifted"], 1)
            dve.wait_ge(m["exps"], START + 1)
            link(nc.vector.tensor_reduce(total[:], exps[:], AX.X, ALU.add))
            link(nc.vector.reciprocal(total[:], total[:]))
            link(nc.vector.tensor_tensor(scores[:], exps[:], over(total[:].unsqueeze(2), te), ALU.mult))
            ranked = scores
            if layer == 1:
                dve.wait_ge(m["bias"], START + 16)
                link(nc.vector.tensor_tensor(choice[:], scores[:], over(bias[:].unsqueeze(1), te), ALU.add))
                ranked = choice
            for t in range(NT):
                last = nc.vector.max(best[:, t, :], ranked[:, t, :])
            link(last)
            for t in range(NT):
                last = nc.vector.max_index(best_i[:, t, :], best[:, t, :], ranked[:, t, :])
            link(last)
            link(nc.vector.tensor_copy(best_f[:], best_i[:]))
            dve.wait_ge(m["iota"], START + 2)
            link(nc.vector.tensor_copy(expert_f[:], expert_i[:]))
            link(nc.vector.tensor_copy(block_f[:], block_i[:]))
            for k in range(k_top):
                nc.vector.tensor_tensor(chosen[:, k], over(expert_f[:].unsqueeze(1), te),
                                        over(best_f[:, :, k:k + 1], te), ALU.is_equal).then_inc(m["chosen"], 1)
            if layer == 0:
                link(nc.vector.tensor_copy(s.gate[:, 0, :], total[:]))
            else:
                for k in range(k_top):
                    dve.wait_ge(m["chosen"], START + k + 1)
                    link(nc.vector.tensor_tensor(picked[:], scores[:], chosen[:, k], ALU.mult))
                    link(nc.vector.tensor_reduce(s.gate[:, k, :], picked[:], AX.X, ALU.add))
                link(nc.vector.tensor_tensor(weight_sum[:], s.gate[:, 0, :], s.gate[:, 1, :], ALU.add))
                link(nc.vector.tensor_scalar(weight_sum[:], weight_sum[:], 1e-9, None, ALU.add))
                link(nc.vector.reciprocal(weight_sum[:], weight_sum[:]))
                for k in range(k_top):
                    link(nc.vector.tensor_tensor(s.gate[:, k, :], s.gate[:, k, :], weight_sum[:], ALU.mult))
            dve.wait_ge(m["ranks"], START + 1)
            link(nc.vector.tensor_copy(tile_sum[:].rearrange("p t e -> p (t e)"), ps[:, 1, 0:KT * E]))
            dve.wait_ge(m["ones"], START + 2)
            for e in range(E):
                last = nc.vector.tensor_tensor_scan(run_sum[:, e, :], all_ones[:, 0:KT], tile_sum[:, :, e], 0.0,
                                                    ALU.mult, ALU.add)
            link(last)
            link(nc.vector.tensor_scalar(n_blocks[:], run_sum[:, :, KT - 1], float(P - 1), None, ALU.add))
            link(nc.vector.tensor_copy(count_i[:], n_blocks[:]))
            link(nc.vector.tensor_scalar(count_i[:], count_i[:], P.bit_length() - 1, None, ALU.arith_shift_right))
            link(nc.vector.tensor_copy(n_blocks[:], count_i[:]))
            link(nc.vector.tensor_tensor_scan(end_block[:], all_ones[:, 0:E], n_blocks[:], 0.0, ALU.mult, ALU.add))
            link(nc.vector.tensor_tensor(start_row[:], end_block[:], n_blocks[:], ALU.subtract))
            link(nc.vector.tensor_scalar(start_row[:], start_row[:], float(P), None, ALU.mult))
            kte = [P, KT, E]
            link(nc.vector.tensor_tensor(place[:], run_sum[:].rearrange("p e t -> p t e"), tile_sum[:], ALU.subtract))
            link(nc.vector.tensor_tensor(place[:], place[:], ps[:, 0, 0:KT * E].rearrange("p (t e) -> p t e", e=E),
                                         ALU.add))
            link(nc.vector.tensor_tensor(place[:], place[:], over(start_row[:].unsqueeze(1), kte), ALU.add))
            link(nc.vector.tensor_tensor(place[:], place[:], chosen[:].rearrange("p k t e -> p (k t) e"), ALU.mult))
            link(nc.vector.tensor_reduce(place_f[:], place[:], AX.X, ALU.add))
            link(nc.vector.tensor_copy(s.place[:, 0:KT], place_f[:]))
            nbe = [P, NBLK, E]
            routed = owner[:, BEFORE:BEFORE + NBLK]
            if BEFORE:
                link(nc.vector.memset(owner[:], float(E)))
            link(nc.vector.tensor_tensor(reached[:], over(block_f[:].unsqueeze(2), nbe),
                                         over(end_block[:].unsqueeze(1), nbe), ALU.is_ge))
            link(nc.vector.tensor_reduce(routed, reached[:], AX.X, ALU.add))
            link(nc.vector.tensor_scalar(routed, routed, float(E - 1), None, ALU.min))
            link(nc.vector.tensor_copy(s.owner[:, 0:NBLK + 2 * BEFORE], owner[:]))


def experts(nc, a, s, layer, k_top, x_rows, y_rows, out):
    with ExitStack() as ctx:
        new_sem = ctx.enter_context(semaphores(nc))

        def sb(name, shape, dt=F32):
            return ctx.enter_context(nc.sbuf_tensor(f"ex{layer}_" + name, shape, dt))

        F = (F0, F1)[layer]
        FC = F // P
        NE = E + layer
        BEFORE = LEAD * layer
        KT = k_top * NT
        N = blocks_of(k_top) + 2 * BEFORE
        TURNS = N // 2
        FIRST = BEFORE // 2
        LAST = TURNS - FIRST
        ps = s.psum
        up_a, up_b, down = (dst for dst, _ in s.expert_weights)
        x = sb("x", [P, 2, D])
        xt_a = sb("xt_a", [P, 2, P])
        xt_b = sb("xt_b", [DB, 2, P])
        silu = sb("silu", [P, 2, F])
        g = sb("g", [P, 2, F])
        g_t = sb("g_t", [P, 2, F])
        y = sb("y", [P, 2, D])
        two = {n: [new_sem(f"ex{layer}_{n}{u}") for u in range(2)] for n in
               ("loaded", "stored", "x_ps", "xt_a", "xt_b", "gate_ps", "up_ps", "silu", "g", "g_ps", "g_t", "y_ps", "y")}
        scattered = [new_sem(f"ex{layer}_scattered{i}", start=0) for i in range(8)]
        rows_placed = new_sem(f"ex{layer}_rows_placed")
        if layer == 1:
            PAIR, BUFS = 2, 4
            ROUNDS = NT // (BUFS * PAIR)
            MIXED_EARLY = (TURNS - 1 - (LAST + 1)) // 2
            assert MIXED_EARLY * 2 == TURNS - 1 - (LAST + 1)
            rows = sb("rows", [P, BUFS, k_top, PAIR, D])
            landed = [[new_sem(f"ex_landed{p}_{i}", start=0) for i in range(k_top * PAIR)] for p in range(BUFS)]
            weighted, out_stored = (new_sem("ex_" + n) for n in ("weighted", "out_stored"))
            summed = [new_sem(f"ex_summed{p}") for p in range(BUFS)]
        nc.all_engine_barrier()
        block = ctx.enter_context(nc.Block())
        PS_X, PS_GATE, PS_UP, PS_G, PS_Y = 0, 1, 3, 5, 6

        def turns(eng, lo, hi, step):
            if hi > lo:
                with eng.Fori(lo, hi) as i:
                    step(1, i, 0, i, 0, i + 1)
                    step(0, i + 1, 1, i, 1, i + 1)

        def blocks(eng, first, step, final):
            first()
            turns(eng, 0, TURNS - 1, step)
            final(1, TURNS - 1, 0, TURNS - 1)

        @block.gpsimd
        def _(pool):
            for i in range(KT):
                pool.indirect_dma_start(out=x_rows, out_offset=bass.IndirectOffsetOnAxis(ap=s.place[:, i:i + 1], axis=0),
                                        in_=s.attn[:, i % NT, :], in_offset=None).then_inc(scattered[i % 8], 16)
            for i in range(8):
                pool.wait_ge(scattered[i], 16 * (KT // 8))
            pool.nop(nofuse=True).then_inc(rows_placed, 1)
            if layer == 1:
                for u in range(2):
                    pool.wait_ge(two["stored"][u], START + 16 * (LAST - FIRST))
                for c in range(ROUNDS):
                    for p in range(BUFS):
                        if c:
                            pool.wait_ge(summed[p], START + k_top * c)
                        for k in range(k_top):
                            for j in range(PAIR):
                                i = k * NT + (BUFS * c + p) * PAIR + j
                                pool.indirect_dma_start(out=rows[:, p, k, j, :], out_offset=None, in_=y_rows,
                                                        in_offset=bass.IndirectOffsetOnAxis(ap=s.place[:, i:i + 1],
                                                                                            axis=0)
                                                        ).then_inc(landed[p][k * PAIR + j], 16)

        @block.sync
        def _(sp):
            def store(u, k):
                sp.wait_ge(two["y"][u], START + k + 1)
                sp.dma_start(y_rows[bass.ds((2 * k + u) * P - BEFORE * P, P), :], y[:, u, :]).then_inc(two["stored"][u], 16)

            with sp.Fori(FIRST, LAST) as i:
                store(0, i)
                store(1, i)
            for u in range(2):
                sp.wait_ge(two["stored"][u], START + 16 * (LAST - FIRST))
            if layer == 1:
                for i in range(0, NT // PAIR, 2):
                    for p in (i % BUFS, (i + 1) % BUFS):
                        sp.wait_ge(summed[p], START + k_top * (i // BUFS + 1))
                    first, n = i * PAIR, 2 * PAIR
                    sp.dma_start(out[first * P:(first + n) * P, :].rearrange("(t p) d -> p t d", p=P),
                                 s.h[:, first:first + n, :]).then_inc(out_stored, 16)
                sp.wait_ge(out_stored, START + 16 * NT // (2 * PAIR))

        @block.scalar
        def _(act):
            LEAD_AT, ROUTED_AT, TAIL_AT = blocks_of(k_top), -BEFORE, 0

            def load(u, k, at):
                act.dma_start(x[:, u, :], x_rows[bass.ds(2 * k * P + (u + at) * P, P), :]
                              ).then_inc(two["loaded"][u], 16)

            def copy_x(u, k):
                act.wait_ge(two["x_ps"][u], START + k + 1)
                act.wait_ge(two["up_ps"][u], START + k)
                nc.scalar.copy(xt_a[:, u, :], ps[:, PS_X, 0:P]).then_inc(two["xt_a"][u], 1)
                nc.scalar.copy(xt_b[:, u, :], ps[0:DB, PS_X, P:2 * P]).then_inc(two["xt_b"][u], 1)

            def activate(u, k):
                act.wait_ge(two["gate_ps"][u], START + k + 1)
                act.wait_ge(two["g"][u], START + k)
                nc.scalar.activation(silu[:, u, :], ps[:, PS_GATE + u, 0:F], ACT.Silu).then_inc(two["silu"][u], 1)

            def first():
                if layer == 0:
                    act.wait_ge(rows_placed, START + 1)
                load(0, 0, LEAD_AT if BEFORE else ROUTED_AT)
                load(1, 0, LEAD_AT if BEFORE else ROUTED_AT)
                copy_x(0, 0)
                activate(0, 0)
                copy_x(1, 0)

            def step_at(at):
                def step(u, k, pu, pk, nu, nk):
                    load(nu, nk, at)
                    activate(u, k)
                    copy_x(nu, nk)
                return step

            first()
            if layer == 1:
                turns(act, 0, FIRST - 1, step_at(LEAD_AT))
                act.wait_ge(rows_placed, START + 1)
            turns(act, max(FIRST - 1, 0), LAST - 1, step_at(ROUTED_AT))
            turns(act, LAST - 1, TURNS - 1, step_at(TAIL_AT))
            activate(1, TURNS - 1)

        @block.vector
        def _(dve):
            def product(u, k):
                dve.wait_ge(two["silu"][u], START + k + 1)
                dve.wait_ge(two["up_ps"][u], START + k + 1)
                dve.wait_ge(two["g_ps"][u], START + k)
                nc.vector.tensor_tensor(g[:, u, :], silu[:, u, :], ps[:, PS_UP + u, 0:F], ALU.mult
                                        ).then_inc(two["g"][u], 1)

            def copy_g(u, k):
                dve.wait_ge(two["g_ps"][u], START + k + 1)
                dve.wait_ge(two["y_ps"][u], START + k)
                nc.vector.tensor_copy(g_t[:, u, :], ps[:, PS_G, 0:F]).then_inc(two["g_t"][u], 1)

            def copy_y(u, k):
                dve.wait_ge(two["y_ps"][u], START + k + 1)
                dve.wait_ge(two["stored"][u], START + 16 * (k - FIRST))
                nc.vector.tensor_copy(y[:, u, :], ps[:, PS_Y, 0:D]).then_inc(two["y"][u], 1)

            def add_shared(first_tile):
                def finish(u, k):
                    dve.wait_ge(two["y_ps"][u], START + k + 1)
                    tile = s.h[:, bass.ds(2 * k + (u + first_tile), 1), :].rearrange("p o d -> p (o d)")
                    nc.vector.tensor_tensor(tile, tile, ps[:, PS_Y, 0:D], ALU.add).then_inc(two["y"][u], 1)
                return finish

            def step_with(finish):
                def step(u, k, pu, pk, nu, nk):
                    copy_g(pu, pk)
                    product(u, k)
                    finish(pu, pk)
                return step

            def mix(c, p):
                for sem in landed[p]:
                    dve.wait_ge(sem, 16 * (c + 1))
                pair = bass.ds((BUFS * c + p) * PAIR, PAIR)
                for k in range(k_top):
                    weight = s.gate[:, k, pair].unsqueeze(2).to_broadcast([P, PAIR, D])
                    nc.vector.tensor_tensor(rows[:, p, k], rows[:, p, k], weight, ALU.mult).then_inc(weighted, 1)
                for k in range(k_top):
                    dve.wait_ge(weighted, START + k_top * (BUFS * c + p) + k + 1)
                    dve.wait_ge(summed[p], START + k_top * c + k)
                    nc.vector.tensor_tensor(s.h[:, pair, :], s.h[:, pair, :], rows[:, p, k], ALU.add
                                            ).then_inc(summed[p], 1)

            product(0, 0)
            if layer == 0:
                turns(dve, 0, TURNS - 1, step_with(copy_y))
                finish = copy_y
            else:
                turns(dve, 0, FIRST, step_with(add_shared(0)))
                turns(dve, FIRST, LAST, step_with(copy_y))
                finish = add_shared(LEAD - (BEFORE + blocks_of(k_top)))
                step = step_with(finish)
                step(1, LAST, 0, LAST, 0, LAST + 1)
                step(0, LAST + 1, 1, LAST, 1, LAST + 1)
                with dve.Fori(0, MIXED_EARLY) as c:
                    for half in range(2):
                        i = 2 * c + (LAST + 1 + half)
                        step(1, i, 0, i, 0, i + 1)
                        mix(c, 2 * half)
                        step(0, i + 1, 1, i, 1, i + 1)
                        mix(c, 2 * half + 1)
            step_with(finish)(1, TURNS - 1, 0, TURNS - 1, None, None)
            copy_g(1, TURNS - 1)
            finish(1, TURNS - 1)
            if layer == 1:
                for c in range(MIXED_EARLY, ROUNDS):
                    for p in range(BUFS):
                        mix(c, p)

        @block.tensor
        def _(pe):
            pe.wait_ge(s.experts_loaded, START + 16 * len(s.expert_weights))

            def owner(u, k):
                return pe.value_load(s.owner[0:1, bass.ds(2 * k + u, 1)], min_val=0, max_val=NE - 1)

            def transpose_x(u, k, pu, pk):
                pe.wait_ge(two["loaded"][u], START + 16 * (k + 1))
                if pk is not None:
                    pe.wait_ge(two["xt_b"][pu], START + pk + 1)
                nc.tensor.transpose(ps[:, PS_X, 0:P], x[:, u, 0:P], s.ident[:])
                nc.tensor.transpose(ps[0:DB, PS_X, P:2 * P], x[:, u, P:D], s.ident[:]).then_inc(two["x_ps"][u], 1)

            def project(u, k, e, which, bank, done):
                dst = ps[:, bank + u, 0:F]
                nc.tensor.matmul(dst, xt_a[:, u, :], up_a[:, which, bass.ds(e, 1), :].rearrange("p o f -> p (o f)"),
                                 start=True, stop=False)
                nc.tensor.matmul(dst, xt_b[:, u, :], up_b[:, which, bass.ds(e, 1), :].rearrange("p o f -> p (o f)"),
                                 start=False, stop=True).then_inc(done[u], 1)

            def gate(u, k, e):
                pe.wait_ge(two["xt_b"][u], START + k + 1)
                pe.wait_ge(two["silu"][u], START + k)
                project(u, k, e, 0, PS_GATE, two["gate_ps"])

            def up(u, k, e):
                pe.wait_ge(two["g"][u], START + k)
                project(u, k, e, 1, PS_UP, two["up_ps"])

            def transpose_g(u, k, pu, pk):
                pe.wait_ge(two["g"][u], START + k + 1)
                if pk is not None:
                    pe.wait_ge(two["g_t"][pu], START + pk)
                for c in range(FC):
                    last = nc.tensor.transpose(ps[:, PS_G, c * P:(c + 1) * P], g[:, u, c * P:(c + 1) * P], s.ident[:])
                last.then_inc(two["g_ps"][u], 1)

            def down_project(u, k, e, pu, pk):
                pe.wait_ge(two["g_t"][u], START + k + 1)
                if pk is not None:
                    pe.wait_ge(two["y"][pu], START + pk)
                for c in range(FC):
                    last = nc.tensor.matmul(ps[:, PS_Y, 0:D], g_t[:, u, c * P:(c + 1) * P],
                                            down[:, bass.ds(e, 1), c, :].rearrange("p o d -> p (o d)"),
                                            start=(c == 0), stop=(c == FC - 1))
                last.then_inc(two["y_ps"][u], 1)

            def first():
                transpose_x(0, 0, None, None)
                e = owner(0, 0)
                gate(0, 0, e)
                up(0, 0, e)
                transpose_x(1, 0, 0, 0)

            def step(u, k, pu, pk, nu, nk):
                e = owner(u, k)
                gate(u, k, e)
                transpose_g(pu, pk, u, k)
                if nu is not None:
                    transpose_x(nu, nk, u, k)
                up(u, k, e)
                down_project(pu, pk, owner(pu, pk), u, k)

            def final(u, k, pu, pk):
                step(u, k, pu, pk, None, None)
                transpose_g(u, k, pu, pk + 1)
                down_project(u, k, owner(u, k), pu, pk + 1)
            blocks(pe, first, step, final)




def relu_attention(nc, a, s, y_rows):
    with ExitStack() as ctx:
        new_sem = ctx.enter_context(semaphores(nc))

        def sb(name, shape, dt=F32):
            return ctx.enter_context(nc.sbuf_tensor("ra_" + name, shape, dt))

        h, attn, ps = s.h, s.attn, s.psum
        V1 = HD + 1
        HH = H // 2
        PAIRS = H // 2
        PA = P // (2 * HD)
        FA = 2 * PA * M_FEAT
        FB = H * M_FEAT - FA
        NORM = float(HD) ** -0.25
        CTX, SLOTS = 4, 3
        PS_XA, PS_XB = 6, 3
        OUT = (7, 6)
        w_a = sb("w_a", [P, 3, P])
        w_b = sb("w_b", [DB, 3, P])
        wv_a = sb("wv_a", [P, D])
        wv_b = sb("wv_b", [DB + 1, D])
        bias = sb("bias", [P, 3])
        half_bias = sb("half_bias", [P, 3])
        feat_a = sb("feat_a", [P, FA])
        feat_b = sb("feat_b", [P, 2, FB])
        stats = sb("stats", [P, 2, CT, 6])
        mv = sb("mv", [P, 2, CT, 2])
        var_eps = sb("var_eps", [P, 2, CT])
        std = sb("std", [P, 2, CT])
        tmp = sb("tmp", [P, 2, CT])
        xn = sb("xn", [P, 2, CT, D])
        xt_a = sb("xt_a", [P, 2, CHUNK])
        xt_b = sb("xt_b", [DB + 1, 2, CHUNK])
        qk = sb("qk", [P, 2, 3, CHUNK])
        q_feat = sb("q_feat", [P, PAIRS, S])
        k_feat = sb("k_feat", [P, 2, H * M_FEAT])
        v_ext = sb("v_ext", [P, 2, CT, H, V1])
        context = sb("context", [P, PAIRS, HH * V1])
        inv = sb("inv", [P, 2, H])
        rows = sb("rows", [P, 2, CT, D])
        rounded = sb("rounded", [P, CT, D], BF16)
        landed = [[new_sem(f"ra_landed{u}_{j}", start=0) for j in range(CT)] for u in range(2)]
        mixed = [new_sem(f"ra_mixed{u}") for u in range(2)]
        weights, ones, halved, chain, inv_done = (new_sem("ra_" + n) for n in
                                                  ("weights", "ones", "halved", "chain", "inv_done"))
        ring_full, ring_act, ring_dve = ([new_sem(f"ra_{n}{i}") for i in range(SLOTS)]
                                         for n in ("ring_full", "ring_act", "ring_dve"))
        var, ln_std, normed, xt_full, xt = ([new_sem(f"ra_{n}{u}") for u in range(2)] for n in
                                            ("var", "std", "normed", "xt_full", "xt"))
        context_full, context_ready, accumulated = (new_sem("ra_" + n) for n in
                                                    ("context_full", "context_ready", "accumulated"))
        out_full = [new_sem(f"ra_out_full{i}") for i in range(2)]
        out_free = [new_sem(f"ra_out_free{i}") for i in range(2)]
        nc.all_engine_barrier()
        block = ctx.enter_context(nc.Block())

        UNITS = ([("qk", r, "act") for r in range(3)] + [("v", i, "act") for i in range(CT)] + [("qf", p, "dve") for p in range(PAIRS)]
                 + [("kf", i, "dve") for i in range(2 * CT)])
        assert 2 * len(UNITS) % SLOTS == 0
        PER_BODY = 2 * len(UNITS) // SLOTS

        def readers(eng, n_last):
            return [sum(1 for n in range(n_last) if n % SLOTS == i and UNITS[n % len(UNITS)][2] == eng)
                    for i in range(SLOTS)]

        TOTAL = {eng: readers(eng, 2 * len(UNITS)) for eng in ("act", "dve")}
        ring_free = {"act": ring_act, "dve": ring_dve}

        def at(kind, i, u):
            return u * len(UNITS) + [x[:2] for x in UNITS].index((kind, i))

        def full(b, n):
            return ring_full[n % SLOTS], START + PER_BODY * b + n // SLOTS + 1

        def left(b, n):
            eng = UNITS[n % len(UNITS)][2]
            return ring_free[eng][n % SLOTS], START + TOTAL[eng][n % SLOTS] * b + readers(eng, n + 1)[n % SLOTS]

        def wait_left(eng, b, numbers):
            newest = {(UNITS[n % len(UNITS)][2], n % SLOTS): n for n in sorted(numbers)}
            for n in newest.values():
                eng.wait_ge(*left(b, n))

        @block.sync
        def _(sp):
            for dst, src in ((w_a[:], a["w1_qk"][0:P]), (w_b[:], a["w1_qk"][P:D]), (wv_a[:], a["w1_v"][0:P]),
                             (wv_b[:], a["w1_v"][P:D + 1]), (bias[:], a["b1_qk"]), (feat_a[:], a["feat_a"]),
                             (feat_b[:], a["feat_b"])):
                sp.dma_start(dst, src).then_inc(weights, 16)

        @block.gpsimd
        def _(pool):
            nc.gpsimd.memset(context[:], 0.0).then_inc(ones, 1)
            pool.wait_ge(ones, START + 1)
            nc.gpsimd.memset(v_ext[:, :, :, :, HD:V1], 1.0).then_inc(ones, 1)
            for t in range(NT):
                u, k = t // CT % 2, t // TB
                if k and t % CT == 0:
                    pool.wait_ge(mixed[u], START + k)
                pool.indirect_dma_start(out=rows[:, u, t % CT, :], out_offset=None, in_=y_rows,
                                        in_offset=bass.IndirectOffsetOnAxis(ap=s.place[:, t:t + 1], axis=0)
                                        ).then_inc(landed[u][t % CT], 16)

        @block.vector
        def _(dve):
            nc.vector.memset(xt_b[DB:DB + 1, :, :], 1.0).then_inc(halved, 1)
            dve.wait_ge(weights, START + 112)
            nc.vector.tensor_scalar(half_bias[:], bias[:], NORM, None, ALU.mult).then_inc(halved, 1)
            dve.wait_ge(ones, START + 2)

            def features(b, n, dst):
                dve.wait_ge(*full(b, n))
                nc.vector.tensor_scalar(dst, ps[:, n % SLOTS, 0:dst.shape[-1]], 0.0, KERNEL_EPS, ALU.max, ALU.add
                                        ).then_inc(ring_dve[n % SLOTS], 1)

            def tiles_of(u, k):
                return [h[:, k * TB + (u * CT + j), :] for j in range(CT)]

            def close_experts(u, k, link):
                for j in range(CT):
                    dve.wait_ge(landed[u][j], 16 * (k + 1))
                chunk = bass.ds(k * TB + u * CT, CT)
                link(nc.vector.tensor_copy(rounded[:], rows[:, u]))
                link(nc.vector.tensor_tensor(rows[:, u], rounded[:], s.gate[:, 0, chunk].unsqueeze(2).to_broadcast(
                    [P, CT, D]), ALU.mult))
                nc.vector.tensor_tensor(h[:, chunk, :], h[:, chunk, :], rows[:, u], ALU.add).then_inc(mixed[u], 1)
                dve.wait_ge(mixed[u], START + k + 1)

            def statistics(u, k, link):
                layer_norm_stats(nc, dve, link, tiles_of(u, k), stats[:, u], mv[:, u], var_eps[:, u], var[u])

            def normalise(u, k, link):
                dve.wait_ge(ln_std[u], START + k + 1)
                layer_norm_apply(nc, link, tiles_of(u, k), xn[:, u], mv[:, u], var_eps[:, u], std[:, u],
                                 tmp[:, u]).then_inc(normed[u], 1)

            def prepare(u, k):
                link = Chain(dve, chain, 9, 2 * k + u)
                close_experts(u, k, link)
                statistics(u, k, link)
                normalise(u, k, link)

            def step(this, prev, nxt):
                u, k = this
                if nxt:
                    prepare(*nxt)
                for i in range(2):
                    dve.wait_ge(out_full[i], START + TB // 2 * k)
                for p in range(PAIRS):
                    features(k, at("qf", p, u), q_feat[:, p, u * CHUNK:(u + 1) * CHUNK])
                for j in range(CT):
                    dve.wait_ge(accumulated, START + TB * k + max(u * CT + j - 1, 0))
                    features(k, at("kf", 2 * j, u), k_feat[:, j % 2, 0:FA])
                    features(k, at("kf", 2 * j + 1, u), k_feat[:, j % 2, FA:])
                if u == 1:
                    copy_contexts(k)
                    divide(k)

            def copy_contexts(k):
                dve.wait_ge(accumulated, START + TB * (k + 1))
                for bank in range(2):
                    for lo in range(2):
                        part = slice(lo * M_FEAT, (lo + 1) * M_FEAT)
                        for p in range(PAIRS // 2):
                            col = (2 * p + lo) * V1
                            last = nc.vector.tensor_copy(
                                context[part, bank * PAIRS // 2 + p, col:col + V1],
                                ps[part, CTX + bank, p * HH * V1 + col:p * HH * V1 + col + V1])
                last.then_inc(context_ready, 1)

            def divide(k):
                for t in range(TB):
                    i = t % 2
                    dve.wait_ge(out_full[i], START + TB // 2 * k + t // 2 + 1)
                    heads = ps[:, OUT[i], 0:H * V1].rearrange("p (h v) -> p h v", v=V1)
                    nc.vector.reciprocal(inv[:, i, :], heads[:, :, HD]).then_inc(inv_done, 1)
                    dve.wait_ge(inv_done, START + TB * k + t + 1)
                    nc.vector.tensor_tensor(attn[:, k * TB + t, :].rearrange("p (h d) -> p h d", d=HD),
                                            heads[:, :, 0:HD], inv[:, i, :].unsqueeze(2).to_broadcast([P, H, HD]),
                                            ALU.mult).then_inc(out_free[i], 1)
            pipeline(dve, B, lambda: prepare(0, 0), step, lambda: None)

        @block.scalar
        def _(act):
            act.wait_ge(halved, START + 2)
            act.wait_ge(ones, START + 2)

            def root(u, k):
                act.wait_ge(var[u], START + k + 1)
                nc.scalar.activation(std[:, u], var_eps[:, u], ACT.Sqrt).then_inc(ln_std[u], 1)

            def copy_xt(u, k):
                act.wait_ge(xt_full[u], START + k + 1)
                nc.scalar.copy(xt_a[:, u, :], ps[:, PS_XA, :]).then_inc(xt[u], 1)
                nc.scalar.copy(xt_b[0:DB, u, :], ps[0:DB, PS_XB, :]).then_inc(xt[u], 1)

            def step(this, prev, nxt):
                u, k = this
                for n, (kind, i, eng) in enumerate(UNITS):
                    if eng != "act":
                        continue
                    n += u * len(UNITS)
                    slot = n % SLOTS
                    act.wait_ge(*full(k, n))
                    if kind == "qk":
                        ins = nc.scalar.activation(qk[:, u, i, :], ps[:, slot, :], ACT.Identity,
                                                   bias=half_bias[:, i:i + 1], scale=NORM)
                    else:
                        ins = nc.scalar.copy(v_ext[:, u, i, :, 0:HD],
                                             ps[:, slot, 0:D].rearrange("p (h d) -> p h d", d=HD))
                    ins.then_inc(ring_act[slot], 1)
                    if nxt and (kind, i) == ("qk", 0):
                        root(*nxt)
                if nxt:
                    copy_xt(*nxt)

            def start():
                root(0, 0)
                copy_xt(0, 0)
            pipeline(act, B, start, step, lambda: None)

        @block.tensor
        def _(pe):
            pe.wait_ge(weights, START + 112)
            pe.wait_ge(halved, START + 2)

            def slot_left(b, n):
                slot = n % SLOTS
                for eng in ("act", "dve"):
                    count = readers(eng, n)[slot]
                    if n >= SLOTS:
                        if UNITS[(n - SLOTS) % len(UNITS)][2] == eng:
                            pe.wait_ge(ring_free[eng][slot], START + TOTAL[eng][slot] * b + count)
                    else:
                        pe.wait_ge(ring_free[eng][slot], START + TOTAL[eng][slot] * b)

            def unit(b, u, kind, i):
                n = at(kind, i, u)
                slot = n % SLOTS
                slot_left(b, n)
                if kind == "qk":
                    nc.tensor.matmul(ps[:, slot, :], w_a[:, i, :], xt_a[:, u, :], start=True, stop=False)
                    last = nc.tensor.matmul(ps[:, slot, :], w_b[:, i, :], xt_b[0:DB, u, :], start=False, stop=True)
                elif kind == "v":
                    toks = slice(i * P, (i + 1) * P)
                    nc.tensor.matmul(ps[:, slot, 0:D], xt_a[:, u, toks], wv_a[:], start=True, stop=False)
                    last = nc.tensor.matmul(ps[:, slot, 0:D], xt_b[:, u, toks], wv_b[:], start=False, stop=True)
                elif kind == "qf":
                    if i < PA:
                        last = nc.tensor.matmul(ps[:, slot, :], feat_a[:, i * P:(i + 1) * P], qk[:, u, 0, :],
                                                start=True, stop=True)
                    else:
                        last = nc.tensor.matmul(ps[:, slot, :], feat_b[:, 0, (i - PA) * P:(i - PA + 1) * P],
                                                qk[:, u, 2, :], start=True, stop=True)
                else:
                    toks = slice(i // 2 * P, (i // 2 + 1) * P)
                    if i % 2 == 0:
                        last = nc.tensor.matmul(ps[:, slot, 0:FA], qk[:, u, 1, toks], feat_a[:], start=True, stop=True)
                    else:
                        last = nc.tensor.matmul(ps[:, slot, 0:FB], qk[:, u, 2, toks], feat_b[:, 1, :],
                                                start=True, stop=True)
                last.then_inc(ring_full[slot], 1)

            def accumulate(b, u, j):
                t = u * CT + j
                needed = [at("kf", 2 * j, u), at("kf", 2 * j + 1, u)]
                if j == 0:
                    needed += [at("v", i, u) for i in range(CT)]
                wait_left(pe, b, needed)
                if t == 0:
                    pe.wait_ge(context_ready, START + b)
                for p in range(PAIRS):
                    bank, col = p // (PAIRS // 2), p % (PAIRS // 2) * HH * V1
                    heads = slice(bank * HH, (bank + 1) * HH)
                    last = nc.tensor.matmul(ps[:, CTX + bank, col:col + HH * V1], k_feat[:, j % 2, p * P:(p + 1) * P],
                                            v_ext[:, u, j, heads, :].rearrange("p h v -> p (h v)"),
                                            start=(t == 0 and col == 0), stop=(t == TB - 1), skip_group_check=True)
                last.then_inc(accumulated, 1)

            def transpose(u, k, this):
                pe.wait_ge(normed[u], START + k + 1)
                if this:
                    pe.wait_ge(xt[this[0]], START + 2 * (this[1] + 1))
                    pe.wait_ge(out_free[1], START + TB // 2 * this[1])
                for j in range(CT):
                    nc.tensor.transpose(ps[:, PS_XA, j * P:(j + 1) * P], xn[:, u, j, 0:P], s.ident[:])
                    last = nc.tensor.transpose(ps[0:DB, PS_XB, j * P:(j + 1) * P], xn[:, u, j, P:D], s.ident[:])
                last.then_inc(xt_full[u], 1)

            def outputs(k, nxt):
                pe.wait_ge(context_ready, START + k + 1)
                wait_left(pe, k, [at("qf", p, u) for p in range(PAIRS) for u in range(2)])
                for t in range(TB):
                    i = t % 2
                    pe.wait_ge(out_free[i], START + TB // 2 * k + t // 2)
                    if t == 1 and nxt:
                        pe.wait_ge(xt[nxt[0]], START + 2 * (nxt[1] + 1))
                    for p in range(PAIRS):
                        bank = p // (PAIRS // 2)
                        last = nc.tensor.matmul(ps[:, OUT[i], bank * HH * V1:(bank + 1) * HH * V1],
                                                q_feat[:, p, t * P:(t + 1) * P], context[:, p, :],
                                                start=(p % (PAIRS // 2) == 0), stop=(p % (PAIRS // 2) == PAIRS // 2 - 1))
                    last.then_inc(out_full[i], 1)

            def step(this, prev, nxt):
                u, k = this
                pe.wait_ge(xt[u], START + 2 * (k + 1))
                for i in range(3):
                    unit(k, u, "qk", i)
                for i in range(CT):
                    unit(k, u, "v", i)
                wait_left(pe, k, [at("qk", i, u) for i in range(3)])
                for i in range(PAIRS):
                    unit(k, u, "qf", i)
                unit(k, u, "kf", 0)
                unit(k, u, "kf", 1)
                for j in range(CT):
                    if j + 1 < CT:
                        unit(k, u, "kf", 2 * j + 2)
                        unit(k, u, "kf", 2 * j + 3)
                    elif u == 0:
                        transpose(*nxt, this)
                    accumulate(k, u, j)
                if u == 1:
                    if nxt:
                        transpose(*nxt, this)
                    outputs(k, nxt)
            pipeline(pe, B, lambda: transpose(0, 0, None), step, lambda: None)


class Stores:
    pass


@contextmanager
def expert_weights(nc, a, layer):
    names = [f"e{layer}_{n}" for n in ("up_a", "up_b", "down")]
    with ExitStack() as ctx:
        new_sem = ctx.enter_context(semaphores(nc))
        pairs = [(ctx.enter_context(nc.sbuf_tensor("w_" + n, a[n].shape, F32))[:], a[n]) for n in names]
        yield pairs, new_sem(f"experts{layer}_loaded")


def tower(nc, a, out):
    with ExitStack() as ctx:
        def sb(name, shape, dt=F32):
            return ctx.enter_context(nc.sbuf_tensor(name, shape, dt))

        def scratch(name, shape, dt=F32):
            return nc.dram_tensor(name, shape, dt, kind="Internal").ap()

        s = Stores()
        s.psum = ctx.enter_context(nc.psum_tensor("psum", [P, 8, 512], F32))
        s.h = sb("h", [P, NT, D])
        s.attn = sb("attn", [P, NT, D])
        s.ident = sb("ident", [P, P])
        s.logits = sb("logits", [P, NT, E])
        s.gate = sb("gate", [P, 2, NT])
        s.place = sb("place", [P, 2 * NT], U32)
        s.owner = sb("owner", [P, blocks_of(2) + NT], I32)
        s.qk_parts = scratch("qk_parts", [2, PARTS, B * D, S], BF16)
        s.x_rows = [scratch(f"x_rows{i}", [(blocks_of(i + 1) + i * NT) * P, D]) for i in range(2)]
        y_rows = [scratch(f"y_rows{i}", [blocks_of(i + 1) * P, D]) for i in range(2)]
        with (semaphores(nc) as new_sem, nc.sbuf_tensor("v_nat", [P, NT, D], F32) as s.v_nat,
              nc.sbuf_tensor("q_stack", [SK + 1, NG, GH, S], BF16) as s.q_stack,
              nc.sbuf_tensor("k_stack", [SK + 1, NG, GH, S], BF16) as s.k_stack):
            s.loaded = [new_sem(f"stacks_loaded{g}") for g in range(NG)]
            embed_and_project(nc, a, s)
            softmax_attention(nc, s)
        for layer, k_top in enumerate((1, 2)):
            if layer == 1:
                relu_attention(nc, a, s, y_rows[0])
            with expert_weights(nc, a, layer) as (s.expert_weights, s.experts_loaded):
                close_attention(nc, a, s, layer)
                route(nc, a, s, layer, k_top, s.x_rows[layer])
                experts(nc, a, s, layer, k_top, s.x_rows[layer], y_rows[layer], out)


def _layouts(x, L0_tok_weight, L0_attn_W_qkv, L0_attn_b_qkv, L0_attn_W_out, L0_attn_b_out, L0_ffn_router_w,
             L0_ffn_router_b, L0_ffn_w1, L0_ffn_w2, L0_ffn_w3, L1_attn_w_qkv, L1_attn_b_qkv, L1_attn_w_proj,
             L1_attn_b_proj, L1_attn_projection, L1_ffn_w_router, L1_ffn_expert_bias, L1_ffn_Wg, L1_ffn_Wu,
             L1_ffn_Wd, L1_ffn_sg, L1_ffn_su, L1_ffn_sd):
    f = np.float32

    def rows_of(w, n):
        full = np.zeros((n * P, w.shape[-1]), f)
        full[:w.shape[0]] = w
        return np.ascontiguousarray(full.reshape(n, P, -1).transpose(1, 0, 2))

    blocks = np.zeros((3, D, D), f)
    for hd in range(H):
        at = slice(hd * HD, (hd + 1) * HD)
        for k in range(3):
            blocks[k, at, at] = L0_attn_W_qkv[hd, :, k * HD:(k + 1) * HD]
    bq, bk, bv = (np.asarray(L0_attn_b_qkv)[:, k * HD:(k + 1) * HD].reshape(D) for k in range(3))
    q1, k1, v1 = (np.asarray(L1_attn_w_qkv)[k * D:(k + 1) * D].T for k in range(3))
    bq1, bk1, bv1 = (np.asarray(L1_attn_b_qkv)[k * D:(k + 1) * D] for k in range(3))
    feat = np.zeros((H, HD, H, M_FEAT), f)
    for hd in range(H):
        feat[hd, :, hd, :] = np.asarray(L1_attn_projection).T
    feat = feat.reshape(D, H * M_FEAT)
    feat_b = np.zeros((2, P, (H - P // HD) * M_FEAT), f)
    feat_b[0, :DB] = feat[P:, P // HD * M_FEAT:]
    feat_b[1, DB:] = feat[P:, P // HD * M_FEAT:]
    wg = np.concatenate([L1_ffn_Wg, np.asarray(L1_ffn_sg)[None]]).transpose(2, 0, 1)
    wu = np.concatenate([L1_ffn_Wu, np.asarray(L1_ffn_su)[None]]).transpose(2, 0, 1)
    wd = np.concatenate([L1_ffn_Wd, np.asarray(L1_ffn_sd)[None]]).transpose(0, 2, 1)

    def cat(*rows):
        return np.ascontiguousarray(np.concatenate([np.asarray(r).reshape(-1, np.shape(rows[0])[-1]) for r in rows]))

    return {
        "ids": np.ascontiguousarray(np.asarray(x).reshape(NT, P).T),
        "table": np.ascontiguousarray(np.asarray(L0_tok_weight).T),
        "w0_qk_a": np.ascontiguousarray(blocks[:2, :P, :P].transpose(1, 0, 2)),
        "w0_qk_b": np.ascontiguousarray(np.concatenate([blocks[0, P:, P:], blocks[1, P:, P:]], 1)),
        "w0_v": cat(blocks[2], bv),
        "b0_qk": np.ascontiguousarray(np.stack([bq[:P], bk[:P], np.concatenate([bq[P:], bk[P:]])], 1)),
        "w0_out": cat(L0_attn_W_out, L0_attn_b_out),
        "w0_router": cat(L0_ffn_router_w, L0_ffn_router_b),
        "e0_up_a": np.ascontiguousarray(np.stack([np.asarray(L0_ffn_w1)[:, :P], np.asarray(L0_ffn_w2)[:, :P]]).transpose(2, 0, 1, 3)),
        "e0_up_b": np.ascontiguousarray(np.stack([np.asarray(L0_ffn_w1)[:, P:], np.asarray(L0_ffn_w2)[:, P:]]).transpose(2, 0, 1, 3)),
        "e0_down": np.ascontiguousarray(np.asarray(L0_ffn_w3).reshape(E, F0 // P, P, D).transpose(2, 0, 1, 3)),
        "w1_qk": np.ascontiguousarray(np.stack([q1[:, :P], k1[:, :P], np.concatenate([q1[:, P:], k1[:, P:]], 1)], 1)),
        "w1_v": cat(v1, bv1),
        "b1_qk": np.ascontiguousarray(np.stack([bq1[:P], bk1[:P], np.concatenate([bq1[P:], bk1[P:]])], 1)),
        "feat_a": np.ascontiguousarray(feat[:P, :P // HD * M_FEAT]),
        "feat_b": np.ascontiguousarray(feat_b.transpose(1, 0, 2)),
        "w1_out": cat(np.asarray(L1_attn_w_proj).T, L1_attn_b_proj),
        "w1_router": np.ascontiguousarray(np.asarray(L1_ffn_w_router).T),
        "b1_expert": np.ascontiguousarray(np.broadcast_to(np.asarray(L1_ffn_expert_bias), (P, E))),
        "e1_up_a": np.ascontiguousarray(np.stack([wg[:P], wu[:P]], 1)),
        "e1_up_b": np.ascontiguousarray(np.stack([wg[P:], wu[P:]], 1)),
        "e1_down": np.ascontiguousarray(wd.reshape(E + 1, F1 // P, P, D).transpose(2, 0, 1, 3)),
    }


def kernel(**inputs):
    import concourse.bacc as _bacc
    from concourse.bass_utils import run_bass_kernel_spmd as _run

    nc = _bacc.Bacc("TRN2", target_bir_lowering=False, num_devices=1)
    arrays = _layouts(**{k: np.asarray(v) for k, v in inputs.items()})
    a = {n: nc.dram_tensor(n, v.shape, mybir.dt.from_np(v.dtype), kind="ExternalInput").ap()
         for n, v in arrays.items()}
    out = nc.dram_tensor("out", [T, D], F32, kind="ExternalOutput").ap()
    tower(nc, a, out)
    r = _run(nc, [arrays], core_ids=[0])
    return r.results[0]["out"].reshape(B, S, D)
```
